# Optimizing a Trainium2 kernel written in Bass

```python
import numpy as np
import jax
import jax.numpy as jnp

def _softmax(x, axis=-1):
    return jax.nn.softmax(x, axis=axis)

def _gelu(x):
    return jax.nn.gelu(x, approximate=True)

def _silu(x):
    return jax.nn.silu(x)

def _sigmoid(x):
    return jax.nn.sigmoid(x)

def _layernorm(x, axis=-1, eps=1e-05):
    m = jnp.mean(x, axis=axis, keepdims=True)
    v = jnp.var(x, axis=axis, keepdims=True)
    return (x - m) / jnp.sqrt(v + eps)

def _scatter_add(tgt, idx, src, axis=0):
    return tgt.at[idx].add(src)

def _segment_sum(src, seg, n):
    return jax.ops.segment_sum(src, seg, n)
kernel_name = 'mk_xattn_ffn_d2_seqx_r4_5ced5c'

def setup_inputs(seed: int=0):
    np.random.seed(seed)
    _w = jnp.asarray

    def _rec_inputs():
        import jax
        import jax.numpy as jnp
        _rk = jax.random.key(seed)
        x = -0.000125 + 0.9999 * jax.random.normal(jax.random.fold_in(_rk, 1), (8, 256, 256), jnp.float32)
        _lenS = 256 - jax.random.randint(jax.random.fold_in(_rk, 7), (8,), 0, max(1, 256 // 4) + 1, jnp.int32)
        _lenS2 = 256 - jax.random.randint(jax.random.fold_in(_rk, 8), (8,), 0, max(1, 256 // 4) + 1, jnp.int32)
        _ctx_768P = jax.random.normal(jax.random.fold_in(_rk, 11), (8, 16, 192), jnp.float32)
        _ctx_768c = jax.random.dirichlet(jax.random.fold_in(_rk, 511), 0.3 * jnp.ones((16,), jnp.float32), (8, 256))
        _ctx_768t = jnp.einsum('bsk,bkd->bsd', _ctx_768c, _ctx_768P)
        _ctx_768t = _ctx_768t * jax.lax.rsqrt(jnp.mean(jnp.square(_ctx_768t)) + 1e-12) * 0.953939
        ctx_768 = 0.00272024 + 0.999456 * (_ctx_768t + 0.3 * jax.random.normal(jax.random.fold_in(_rk, 611), (8, 256, 192), jnp.float32))
        return (x, ctx_768)
    x, ctx_768 = _rec_inputs()

    def _L0_xattn_setup():
        import jax, jax.numpy as jnp
        import numpy as np
        QUERY_DIM = 256
        CONTEXT_DIM = 192
        HEADS = 8
        DIM_HEAD = 64
        INNER = HEADS * DIM_HEAD
        key = jax.random.key(seed)
        ks = jax.random.split(key, 7)
        B, S, L = (8, 1024, 77)
        x = jax.random.normal(ks[0], (B, S, QUERY_DIM), dtype=jnp.float32)
        context = jax.random.normal(ks[1], (B, L, CONTEXT_DIM), dtype=jnp.float32)
        Wq = jax.random.normal(ks[2], (QUERY_DIM, INNER), dtype=jnp.float32) * QUERY_DIM ** (-0.5)
        Wk = jax.random.normal(ks[3], (CONTEXT_DIM, INNER), dtype=jnp.float32) * CONTEXT_DIM ** (-0.5)
        Wv = jax.random.normal(ks[4], (CONTEXT_DIM, INNER), dtype=jnp.float32) * CONTEXT_DIM ** (-0.5)
        Wo = jax.random.normal(ks[5], (INNER, QUERY_DIM), dtype=jnp.float32) * INNER ** (-0.5)
        bo = jax.random.normal(ks[6], (QUERY_DIM,), dtype=jnp.float32) * 0.01
        return {'x': x, 'context': context, 'Wq': Wq, 'Wk': Wk, 'Wv': Wv, 'Wo': Wo, 'bo': bo}
    _L0_xattn_all = _L0_xattn_setup()
    _L0_xattn_in = {k: v for k, v in _L0_xattn_all.items() if k in ('Wq', 'Wk', 'Wv', 'Wo', 'bo')}
    del _L0_xattn_all

    def _L0_ffn_setup():
        import jax, jax.numpy as jnp
        import numpy as np
        B, S, D = (2, 512, 256)
        F = 1024
        E, K = (8, 2)
        EPS = 1e-09
        key = jax.random.key(seed)
        k1, k2, k3, k4 = jax.random.split(key, 4)
        x = jax.random.normal(k1, (B, S, D), dtype=jnp.float32)
        w_gate = jax.random.normal(k2, (D, E), dtype=jnp.float32) * 0.02
        w_gate_up = jax.random.normal(k3, (E, D, 2 * F), dtype=jnp.float32) * 0.02
        w_down = jax.random.normal(k4, (E, F, D), dtype=jnp.float32) * 0.02
        return {'x': x, 'w_gate': w_gate, 'w_gate_up': w_gate_up, 'w_down': w_down}
    _L0_ffn_all = _L0_ffn_setup()
    _L0_ffn_in = {k: v for k, v in _L0_ffn_all.items() if k in ('w_gate', 'w_gate_up', 'w_down')}
    del _L0_ffn_all

    def _L1_xattn_setup():
        import jax, jax.numpy as jnp
        import numpy as np
        NUM_HEADS = 16
        key = jax.random.key(seed)
        ks = jax.random.split(key, 8)
        dim, cond_dim = (256, 192)
        B, N, condN = (4, 512, 256)
        s = lambda k, shp, fan: jax.random.normal(k, shp, dtype=jnp.float32) * fan ** (-0.5)
        return {'x': jax.random.normal(ks[0], (B, N, dim), dtype=jnp.float32), 'cond': jax.random.normal(ks[1], (B, condN, cond_dim), dtype=jnp.float32), 'q_w': s(ks[2], (dim, dim), dim), 'q_b': jnp.zeros((dim,), jnp.float32), 'kv_w': s(ks[3], (cond_dim, 2 * dim), cond_dim), 'kv_b': jnp.zeros((2 * dim,), jnp.float32), 'proj_w': s(ks[4], (dim, dim), dim), 'proj_b': jnp.zeros((dim,), jnp.float32)}
    _L1_xattn_all = _L1_xattn_setup()
    _L1_xattn_in = {k: v for k, v in _L1_xattn_all.items() if k in ('q_w', 'q_b', 'kv_w', 'kv_b', 'proj_w', 'proj_b')}
    del _L1_xattn_all

    def _L1_ffn_setup():
        import jax, jax.numpy as jnp
        import numpy as np
        B, N, D = (4, 1024, 256)
        E, S, F = (16, 64, 512)
        DO = 256
        EPS = 1e-05

        def _layernorm(x, g, b):
            mu = jnp.mean(x, axis=-1, keepdims=True)
            var = jnp.mean(jnp.square(x - mu), axis=-1, keepdims=True)
            return (x - mu) * jax.lax.rsqrt(var + EPS) * g + b
        key = jax.random.key(seed)
        ks = jax.random.split(key, 8)
        d = {'x': jax.random.normal(ks[0], (B, N, D), dtype=jnp.float32), 'norm_g': jnp.ones((D,), jnp.float32), 'norm_b': jnp.zeros((D,), jnp.float32), 'slot_g': jnp.ones((D,), jnp.float32), 'slot_b': jnp.zeros((D,), jnp.float32), 'scale': jnp.ones((1,), jnp.float32), 'slot_embeds': jax.random.normal(ks[1], (E, S, D), jnp.float32) / np.sqrt(D), 'Wg': jax.random.normal(ks[2], (E, D, F), jnp.float32) * np.sqrt(2.0 / (D + F)), 'bg': jnp.zeros((E, F), jnp.float32), 'Wu': jax.random.normal(ks[3], (E, D, F), jnp.float32) * np.sqrt(2.0 / (D + F)), 'bu': jnp.zeros((E, F), jnp.float32), 'Wd': jax.random.normal(ks[4], (E, F, DO), jnp.float32) * np.sqrt(2.0 / (F + DO)), 'bd': jnp.zeros((E, DO), jnp.float32)}
        return d
    _L1_ffn_all = _L1_ffn_setup()
    _L1_ffn_in = {k: v for k, v in _L1_ffn_all.items() if k in ('norm_g', 'norm_b', 'slot_g', 'slot_b', 'scale', 'slot_embeds', 'Wg', 'bg', 'Wu', 'bu', 'Wd', 'bd')}
    del _L1_ffn_all
    return {'x': x, 'ctx_768': ctx_768, 'L0_xattn_Wq': _L0_xattn_in['Wq'], 'L0_xattn_Wk': _L0_xattn_in['Wk'], 'L0_xattn_Wv': _L0_xattn_in['Wv'], 'L0_xattn_Wo': _L0_xattn_in['Wo'], 'L0_xattn_bo': _L0_xattn_in['bo'], 'L0_ffn_w_gate': _L0_ffn_in['w_gate'], 'L0_ffn_w_gate_up': _L0_ffn_in['w_gate_up'], 'L0_ffn_w_down': _L0_ffn_in['w_down'], 'L1_xattn_q_w': _L1_xattn_in['q_w'], 'L1_xattn_q_b': _L1_xattn_in['q_b'], 'L1_xattn_kv_w': _L1_xattn_in['kv_w'], 'L1_xattn_kv_b': _L1_xattn_in['kv_b'], 'L1_xattn_proj_w': _L1_xattn_in['proj_w'], 'L1_xattn_proj_b': _L1_xattn_in['proj_b'], 'L1_ffn_norm_g': _L1_ffn_in['norm_g'], 'L1_ffn_norm_b': _L1_ffn_in['norm_b'], 'L1_ffn_slot_g': _L1_ffn_in['slot_g'], 'L1_ffn_slot_b': _L1_ffn_in['slot_b'], 'L1_ffn_scale': _L1_ffn_in['scale'], 'L1_ffn_slot_embeds': _L1_ffn_in['slot_embeds'], 'L1_ffn_Wg': _L1_ffn_in['Wg'], 'L1_ffn_bg': _L1_ffn_in['bg'], 'L1_ffn_Wu': _L1_ffn_in['Wu'], 'L1_ffn_bu': _L1_ffn_in['bu'], 'L1_ffn_Wd': _L1_ffn_in['Wd'], 'L1_ffn_bd': _L1_ffn_in['bd']}

def reference(x, ctx_768, L0_xattn_Wq, L0_xattn_Wk, L0_xattn_Wv, L0_xattn_Wo, L0_xattn_bo, L0_ffn_w_gate, L0_ffn_w_gate_up, L0_ffn_w_down, L1_xattn_q_w, L1_xattn_q_b, L1_xattn_kv_w, L1_xattn_kv_b, L1_xattn_proj_w, L1_xattn_proj_b, L1_ffn_norm_g, L1_ffn_norm_b, L1_ffn_slot_g, L1_ffn_slot_b, L1_ffn_scale, L1_ffn_slot_embeds, L1_ffn_Wg, L1_ffn_bg, L1_ffn_Wu, L1_ffn_bu, L1_ffn_Wd, L1_ffn_bd):
    import jax
    import jax.numpy as jnp

    def _L0_xattn_ref(x, context, Wq, Wk, Wv, Wo, bo):
        import jax, jax.numpy as jnp
        import numpy as np
        QUERY_DIM = 256
        CONTEXT_DIM = 192
        HEADS = 8
        DIM_HEAD = 64
        INNER = HEADS * DIM_HEAD
        B, S, _ = x.shape
        L = context.shape[1]
        scale = DIM_HEAD ** (-0.5)
        q = (x @ Wq).reshape(B, S, HEADS, DIM_HEAD).transpose(0, 2, 1, 3)
        k = (context @ Wk).reshape(B, L, HEADS, DIM_HEAD).transpose(0, 2, 1, 3)
        v = (context @ Wv).reshape(B, L, HEADS, DIM_HEAD).transpose(0, 2, 1, 3)
        attn = jnp.einsum('bhsd,bhld->bhsl', q, k) * scale
        attn = jax.nn.softmax(attn, axis=-1)
        out = jnp.einsum('bhsl,bhld->bhsd', attn, v)
        out = out.transpose(0, 2, 1, 3).reshape(B, S, INNER)
        return out @ Wo + bo

    def _L0_ffn_ref(x, w_gate, w_gate_up, w_down):
        import jax, jax.numpy as jnp
        import numpy as np
        B, S, D = (2, 512, 256)
        F = 1024
        E, K = (8, 2)
        EPS = 1e-09
        gate_logits = x @ w_gate
        gate_probs = jax.nn.softmax(gate_logits, axis=-1)
        topk_vals, topk_idx = jax.lax.top_k(gate_probs, K)
        masked = jnp.sum(jax.nn.one_hot(topk_idx, E, dtype=gate_probs.dtype) * topk_vals[..., None], axis=-2)
        denom = jnp.maximum(jnp.sum(masked, axis=-1, keepdims=True), EPS)
        gate_probs = masked / denom
        gu = jnp.einsum('bsd,edh->ebsh', x, w_gate_up)
        g, u = jnp.split(gu, 2, axis=-1)
        act = jax.nn.silu(g) * u
        expert_out = jnp.einsum('ebsf,efd->ebsd', act, w_down)
        return jnp.einsum('bse,ebsd->bsd', gate_probs, expert_out)

    def _L1_xattn_ref(x, cond, q_w, q_b, kv_w, kv_b, proj_w, proj_b):
        import jax, jax.numpy as jnp
        import numpy as np
        NUM_HEADS = 16
        B, N, C = x.shape
        condN = cond.shape[1]
        H = NUM_HEADS
        hd = C // H
        scale = hd ** (-0.5)
        q = (x @ q_w + q_b).reshape(B, N, H, hd).transpose(0, 2, 1, 3)
        kv = (cond @ kv_w + kv_b).reshape(B, condN, 2, H, hd)
        k = kv[:, :, 0].transpose(0, 2, 1, 3)
        v = kv[:, :, 1].transpose(0, 2, 1, 3)
        attn = jnp.einsum('bhnd,bhmd->bhnm', q * scale, k)
        attn = jax.nn.softmax(attn, axis=-1)
        out = jnp.einsum('bhnm,bhmd->bhnd', attn, v)
        out = out.transpose(0, 2, 1, 3).reshape(B, N, C)
        return out @ proj_w + proj_b

    def _L1_ffn_ref(x, norm_g, norm_b, slot_g, slot_b, scale, slot_embeds, Wg, bg, Wu, bu, Wd, bd):
        import jax, jax.numpy as jnp
        import numpy as np
        B, N, D = (4, 1024, 256)
        E, S, F = (16, 64, 512)
        DO = 256
        EPS = 1e-05

        def _layernorm(x, g, b):
            mu = jnp.mean(x, axis=-1, keepdims=True)
            var = jnp.mean(jnp.square(x - mu), axis=-1, keepdims=True)
            return (x - mu) * jax.lax.rsqrt(var + EPS) * g + b
        x = _layernorm(x, norm_g, norm_b)
        se = _layernorm(slot_embeds, slot_g, slot_b) * scale
        logits = jnp.einsum('bnd,esd->bnes', x, se)
        dispatch = jax.nn.softmax(logits, axis=1)
        combine = jax.nn.softmax(logits.reshape(x.shape[0], x.shape[1], -1), axis=-1)
        slots = jnp.einsum('bnd,bnes->besd', x, dispatch)
        gate = jax.nn.gelu(jnp.einsum('besd,edf->besf', slots, Wg) + bg[None, :, None, :], approximate=False)
        up = jnp.einsum('besd,edf->besf', slots, Wu) + bu[None, :, None, :]
        eout = jnp.einsum('besf,efo->beso', gate * up, Wd) + bd[None, :, None, :]
        eout = eout.reshape(eout.shape[0], -1, eout.shape[-1])
        return jnp.einsum('bns,bso->bno', combine, eout)
    x = x + _L0_xattn_ref(_layernorm(x, axis=-1), ctx_768, L0_xattn_Wq, L0_xattn_Wk, L0_xattn_Wv, L0_xattn_Wo, L0_xattn_bo)
    x = x + _L0_ffn_ref(_layernorm(x, axis=-1), L0_ffn_w_gate, L0_ffn_w_gate_up, L0_ffn_w_down)
    x = x + _L1_xattn_ref(_layernorm(x, axis=-1), ctx_768, L1_xattn_q_w, L1_xattn_q_b, L1_xattn_kv_w, L1_xattn_kv_b, L1_xattn_proj_w, L1_xattn_proj_b)
    x = x + _L1_ffn_ref(_layernorm(x, axis=-1), L1_ffn_norm_g, L1_ffn_norm_b, L1_ffn_slot_g, L1_ffn_slot_b, L1_ffn_scale, L1_ffn_slot_embeds, L1_ffn_Wg, L1_ffn_bg, L1_ffn_Wu, L1_ffn_bu, L1_ffn_Wd, L1_ffn_bd)
    return x

_drawn_inputs = setup_inputs


def setup_inputs(seed=0):
    import zlib

    import numpy as np

    out = dict(_drawn_inputs(seed))
    spreads = {'L1_xattn_q_b': (0.0, 0.1),
     'L1_xattn_kv_b': (0.0, 0.1),
     'L1_xattn_proj_b': (0.0, 0.1),
     'L1_ffn_norm_g': (1.0, 0.2),
     'L1_ffn_norm_b': (0.0, 0.1),
     'L1_ffn_slot_g': (1.0, 0.2),
     'L1_ffn_slot_b': (0.0, 0.1),
     'L1_ffn_bg': (0.0, 0.1),
     'L1_ffn_bu': (0.0, 0.1),
     'L1_ffn_bd': (0.0, 0.1)}
    factors = {'L0_xattn_bo': 4.627}
    for name, (base, spread) in spreads.items():
        noise = np.random.default_rng([zlib.crc32(name.encode()), seed]).standard_normal(out[name].shape)
        drawn = base * np.exp(spread * noise) if base else spread * noise
        out[name] = jnp.asarray(drawn.astype(out[name].dtype))
    for name, factor in factors.items():
        out[name] = (out[name] * factor).astype(out[name].dtype)
    return out
```

```python
from contextlib import ExitStack

import concourse.bass as bass
from concourse import mybir

F32 = mybir.dt.float32
F32R = mybir.dt.float32r
I32 = mybir.dt.int32
U32 = mybir.dt.uint32
ALU = mybir.AluOpType
ACT = mybir.ActivationFunctionType
AX = mybir.AxisListType

P = 128
BATCH, SEQ, D = 8, 256, 256
CTX_D = 192
NT = SEQ // P
KD = D // P
CTX_K = (P, CTX_D - P)
LN_EPS = 1e-5
RSQRT_MAGIC = float(0x5F3759DF)
NEWTON = 3
CREDIT = 2


def nth(n):
    return n + 1 + CREDIT


def two_before(n):
    return n + 1



def pair_loop(eng, step):
    with eng.Fori(0, BATCH // 2 - 1) as pair:
        step(pair, 0, False)
        step(pair, 1, False)
    step(BATCH // 2 - 1, 0, False)
    step(BATCH // 2 - 1, 1, True)


NEWTON_STEPS = 4 * NEWTON


def newton_rsqrt(pool, step_done, base, y, half_v, tmp, three_halves):
    for n in range(NEWTON):
        pool.tensor_tensor(tmp, y, y, ALU.mult).then_inc(step_done, 1)
        pool.wait_ge(step_done, base + 4 * n + 1)
        pool.tensor_tensor(tmp, tmp, half_v, ALU.mult).then_inc(step_done, 1)
        pool.wait_ge(step_done, base + 4 * n + 2)
        pool.tensor_tensor(tmp, tmp, three_halves, ALU.add).then_inc(step_done, 1)
        pool.wait_ge(step_done, base + 4 * n + 3)
        pool.tensor_tensor(y, y, tmp, ALU.mult).then_inc(step_done, 1)
        pool.wait_ge(step_done, base + 4 * n + 4)


STATS_STEPS = 4


def row_stats(dve, step_done, base, x, stats, mean_var, half_v, seed_bits, seed):
    for t in range(x.shape[1]):
        ins = dve.bn_stats(stats[:, t, :], x[:, t, :])
    ins.then_inc(step_done, 1)
    dve.wait_ge(step_done, base + 1)
    dve.memset(half_v, 0.0)
    for t in range(x.shape[1]):
        ins = dve.bn_aggr(mean_var[:, t, :], stats[:, t, :])
    ins.then_inc(step_done, 1)
    dve.wait_ge(step_done, base + 2)
    dve.tensor_scalar(half_v, mean_var[:, :, 1], LN_EPS, None, ALU.add).then_inc(step_done, 1)
    dve.wait_ge(step_done, base + 3)
    dve.tensor_scalar(seed_bits, half_v.bitcast(I32), 1, None, ALU.logical_shift_right).then_inc(step_done, 1)
    dve.wait_ge(step_done, base + 4)
    dve.tensor_scalar(half_v, half_v, -0.5, None, ALU.mult)
    return dve.tensor_scalar(seed.bitcast(I32), seed_bits, -1.0, RSQRT_MAGIC, ALU.mult, ALU.add)


def cross_attention(nc, tag, x_in, ctx_t, wq, wk, wv, wo, out_bias, x_out, ident_in, heads, head_dim,
                    q_bias=None, k_bias=None, v_bias=None):
    H = heads
    HPT = H // 4
    R = P // HPT
    INNER = heads * head_dim
    HG = H // 2
    GI = HG * head_dim
    GK = GI // P
    SCALE = float(head_dim) ** -0.5
    biased = q_bias is not None
    PRO = 7
    SIDE = PRO + 3

    with ExitStack() as ctx:
        def sb(name, shape, dt=F32):
            return ctx.enter_context(nc.sbuf_tensor(f"{tag}_{name}", shape, dt))

        def pb(name, shape):
            return ctx.enter_context(nc.psum_tensor(f"{tag}_{name}", shape, F32))

        def sem(name):
            return ctx.enter_context(nc.semaphore(f"{tag}_{name}"))

        ident = sb("ident", [P, P])
        wq_sb = sb("wq", [P, KD, 4 * P])
        wk_sb = sb("wk", [P, 2, 4 * P])
        wv_sb = sb("wv", [P, 2, INNER])
        wo_sb = sb("wo", [P, INNER // P, D])
        obias = sb("obias", [P, D])
        if biased:
            qb_sb = sb("qb", [P, 4])
            kb_sb = sb("kb", [P, 4])
            vb_sb = sb("vb", [P, INNER])
        x_sb = [sb(f"x{i}", [P, NT, D]) for i in range(2)]
        c_sb = [sb(f"c{i}", [P, 2, SEQ]) for i in range(2)]
        xb_sb = [sb(f"xb{i}", [P, NT, D]) for i in range(2)]
        xo_sb = [sb(f"xo{i}", [P, NT, D]) for i in range(2)]
        xn_sb = [sb(f"xn{i}", [P, NT, D]) for i in range(2)]
        xnt_sb = sb("xnt", [P, KD, SEQ])
        q_sb = [sb(f"q{i}", [P, 4, SEQ]) for i in range(2)]
        k_sb = [sb(f"k{i}", [P, 4, SEQ]) for i in range(2)]
        v_sb = [sb(f"v{i}", [P, 2, INNER]) for i in range(2)]
        prob = [sb(f"prob{i}", [P, NT, SEQ]) for i in range(2)]
        prob_t = [sb(f"probt{i}", [P, 2, SEQ]) for i in range(2)]
        neg_max = [sb(f"nmax{i}", [P, NT]) for i in range(2)]
        row_sum = [sb(f"rsum{i}", [P, NT, H]) for i in range(2)]
        inv_sum = [sb(f"inv{i}", [P, NT, HG]) for i in range(2)]
        o_sb = sb("o", [P, NT, INNER])
        ot_sb = sb("ot", [P, INNER // P, SEQ])
        stats = sb("stats", [P, NT, 6])
        mean_var = sb("mv", [P, NT, 2])
        half_v = sb("halfv", [P, NT])
        seed_bits = sb("seedb", [P, NT], I32)
        rstd = sb("rstd", [P, NT])
        nwt = sb("nwt", [P, NT])
        three_halves = sb("three_halves", [P, NT])

        score_ps = [pb(f"score{i}", [P, NT, SEQ]) for i in range(2)]
        trans_ps = [pb(f"trans{i}", [P, 2, SEQ]) for i in range(2)]
        out_ps = [pb(f"outp{i}", [P, NT, GI]) for i in range(2)]
        side_ps = [pb(f"side{i}", [P, 512]) for i in range(2)]

        weights_in = sem("weights_in")
        x_loaded = [sem(f"x_loaded{i}") for i in range(2)]
        c_loaded = [sem(f"c_loaded{i}") for i in range(2)]
        constant_set = sem("constant_set")
        stats_step = sem("stats_step")
        seed_ready = sem("seed_ready")
        newton_step = sem("newton_step")
        xn_ready = sem("xn_ready")
        xn_turned = sem("xn_turned")
        c_used = sem("c_used")
        xb_ready = sem("xb_ready")
        side_full = [sem(f"side_full{i}") for i in range(2)]
        side_free = [sem(f"side_free{i}") for i in range(2)]
        qb_scaled = sem("qb_scaled")
        scores_done = sem("scores_done")
        max_done = sem("max_done")
        exp_done = sem("exp_done")
        turned = sem("turned")
        prob_t_ready = sem("prob_t_ready")
        pv_done = sem("pv_done")
        inv_ready = sem("inv_ready")
        o_ready = sem("o_ready")
        xo_ready = sem("xo_ready")
        stored = [sem(f"stored{i}") for i in range(2)]

        x_dram = x_in.rearrange("b (t p) d -> b p t d", p=P)
        xo_dram = x_out.rearrange("b (t p) d -> b p t d", p=P)
        WEIGHTS = 16 * (8 + 3 * biased)

        TURNS = H + 3
        SIDE_AT = 2
        assert SIDE_AT + PRO <= TURNS and SIDE % 2 == 0

        FREE_STEPS = [[j for j in range(SIDE - 1) if j % 2 == bank] for bank in range(2)]
        FULL_STEPS = [[j for j in range(SIDE) if j % 2 == bank and j not in (0, PRO - 1)] for bank in range(2)]

        def count(steps, b, j):
            skipped = sum(x < PRO for x in steps) if isinstance(b, int) and b == BATCH - 1 else 0
            return len(steps) * (b + 1) + steps.index(j) + 1 - skipped

        def full(b, j):
            if j == 0:
                return xn_turned, nth(b + 1)
            if j == PRO - 1:
                return c_used, nth(b + 1)
            return side_full[j % 2], count(FULL_STEPS[j % 2], b, j)

        def emptied(b, j):
            if j == SIDE - 1:
                return xo_ready, nth(b)
            return side_free[j % 2], count(FREE_STEPS[j % 2], b, j)

        def before(b, j):
            if isinstance(b, int) and b == BATCH - 1 and j in (PRO, PRO + 1):
                return emptied(b - 1, SIDE - 1 if j == PRO else SIDE - 2)
            if j >= 2:
                return emptied(b, j - 2)
            return None if isinstance(b, int) and b < 0 else emptied(b - 1, SIDE - 2 + j)

        def ready(b, j):
            return side_free[j % 2], len(FREE_STEPS[j % 2]) * b + FREE_STEPS[j % 2].index(j) + 1

        def group_end(i):
            return (i - 3) // HG if i >= 3 and (i - 3) % HG == HG - 1 else None

        block = ctx.enter_context(nc.Block())

        @block.sync
        def _(sp):
            sp.sem_inc(stored[0], 16)
            sp.sem_inc(stored[1], 16)

            def load(pair, s):
                b = 2 * pair + s
                sp.wait_ge(xb_ready, two_before(b))
                sp.dma_start(x_sb[s][:], x_dram[b]).then_inc(x_loaded[s], 16)
                sp.wait_ge(c_used, two_before(b))
                for k, rows in enumerate(CTX_K):
                    sp.dma_start(c_sb[s][0:rows, k, :], ctx_t[b, k * P:k * P + rows, :]).then_inc(c_loaded[s], 16)

            def store(pair, s):
                sp.wait_ge(xo_ready, nth(2 * pair + s))
                sp.dma_start(xo_dram[2 * pair + s], xo_sb[s][:]).then_inc(stored[s], 16)

            load(0, 0)
            sp.dma_start(ident[:], ident_in).then_inc(weights_in, 16)
            sp.dma_start(wq_sb[:], wq.rearrange("(k p) n -> p k n", p=P)).then_inc(weights_in, 16)
            for k, rows in enumerate(CTX_K):
                sp.dma_start(wk_sb[0:rows, k, :], wk[k * P:k * P + rows, :]).then_inc(weights_in, 16)
                sp.dma_start(wv_sb[0:rows, k, :], wv[k * P:k * P + rows, :]).then_inc(weights_in, 16)
            sp.dma_start(wo_sb[:], wo.rearrange("(k p) n -> p k n", p=P)).then_inc(weights_in, 16)
            sp.dma_start(obias[:], out_bias.partition_broadcast(P)).then_inc(weights_in, 16)
            if biased:
                sp.dma_start(qb_sb[:], q_bias).then_inc(weights_in, 16)
                sp.dma_start(kb_sb[:], k_bias).then_inc(weights_in, 16)
                sp.dma_start(vb_sb[:], v_bias.partition_broadcast(P)).then_inc(weights_in, 16)
            load(0, 1)
            with sp.Fori(0, BATCH // 2 - 1) as pair:
                for s in range(2):
                    store(pair, s)
                    load(pair + 1, s)
            for s in range(2):
                store(BATCH // 2 - 1, s)
            for s in range(2):
                sp.wait_ge(stored[s], 16 * (BATCH // 2 + 1))

        @block.gpsimd
        def _(pool):
            pool.sem_inc(xb_ready, CREDIT)
            pool.memset(three_halves[:], 1.5).then_inc(constant_set, 1)
            pool.wait_ge(constant_set, 1)
            pool.wait_ge(weights_in, WEIGHTS)

            def normalise(pair, s):
                b = 2 * pair + s
                pool.wait_ge(seed_ready, b + 1)
                newton_rsqrt(pool, newton_step, NEWTON_STEPS * b, rstd[:], half_v[:], nwt[:],
                             three_halves[:])
                pool.wait_ge(xn_turned, two_before(b))
                pool.wait_ge(xo_ready, two_before(b))
                pool.tensor_tensor(xb_sb[s][:, 0, :], x_sb[s][:, 0, :], obias[:], ALU.add)
                for t in range(NT):
                    ins = pool.tensor_scalar(xn_sb[s][:, t, :], x_sb[s][:, t, :], mean_var[:, t, 0:1],
                                             rstd[:, t:t + 1], ALU.subtract, ALU.mult)
                ins.then_inc(xn_ready, 1)
                pool.tensor_tensor(xb_sb[s][:, 1, :], x_sb[s][:, 1, :], obias[:], ALU.add)\
                    .then_inc(xb_ready, 1)

            with pool.Fori(0, BATCH // 2) as pair:
                normalise(pair, 0)
                normalise(pair, 1)

        @block.scalar
        def _(act):
            act.sem_inc(exp_done, CREDIT)
            act.wait_ge(weights_in, WEIGHTS)

            def side(pair, s, j):
                b = 2 * pair + s
                bank = j % 2
                if j == 0:
                    act.wait_ge(*full(b, j))
                    act.activation(xnt_sb[:].rearrange("p k n -> p (k n)"), side_ps[bank][:], ACT.Copy)\
                       .then_inc(side_free[bank], 1)
                elif j in (1, 2):
                    act.wait_ge(*full(b, j))
                    q = q_sb[1 - s][:, 2 * (j - 1):2 * j, :]
                    if biased:
                        for n in range(2):
                            m = 2 * (j - 1) + n
                            ins = act.activation(q[:, n, :], side_ps[bank][:, n * SEQ:(n + 1) * SEQ],
                                                 ACT.Identity, bias=qb_sb[:, m:m + 1], scale=SCALE)
                    else:
                        ins = act.activation(q.rearrange("p k n -> p (k n)"), side_ps[bank][:], ACT.Copy,
                                             scale=SCALE)
                    ins.then_inc(side_free[bank], 1)
                elif j in (PRO, PRO + 1):
                    act.wait_ge(*full(b, j))
                    g = j - PRO
                    act.activation(ot_sb[:, g * GK:(g + 1) * GK, :].rearrange("p k n -> p (k n)"),
                                   side_ps[bank][:, 0:GK * SEQ], ACT.Copy).then_inc(side_free[bank], 1)

            def step(pair, s, last):
                b = 2 * pair + s
                for i in range(TURNS):
                    if i < H:
                        u = H * b + i
                        act.wait_ge(max_done, u + 1)
                        act.wait_ge(turned, two_before(u))
                        for t in range(NT):
                            ins = act.activation(prob[i % 2][:, t, :], score_ps[i % 2][:, t, :], ACT.Exp,
                                                 bias=neg_max[i % 2][:, t:t + 1],
                                                 accum_out=row_sum[s][:, t, i:i + 1])
                        ins.then_inc(exp_done, 1)
                    if 0 <= i - SIDE_AT < PRO and not last:
                        side(pair, s, i - SIDE_AT)
                side(pair, s, PRO)
                side(pair, s, PRO + 1)

            if biased:
                act.wait_ge(qb_scaled, 1)
            for j in range(PRO):
                side(-1, 1, j)
            pair_loop(act, step)

        @block.tensor
        def _(pe):
            pe.sem_inc(c_used, CREDIT)
            pe.sem_inc(xn_turned, CREDIT)
            pe.sem_inc(turned, CREDIT)
            pe.sem_inc(pv_done, CREDIT)
            pe.wait_ge(weights_in, WEIGHTS)

            def side(pair, s, j):
                b = 2 * pair + s
                n, o = b + 1, 1 - s
                nth_of_slot = pair + s
                ps = side_ps[j % 2]
                if before(b, j) is not None:
                    pe.wait_ge(*before(b, j))
                if j == 0:
                    pe.wait_ge(xn_ready, n + 1)
                    for k in range(KD):
                        for t in range(NT):
                            ins = pe.transpose(ps[:, k * SEQ + t * P:k * SEQ + (t + 1) * P],
                                               xn_sb[o][:, t, k * P:(k + 1) * P], ident[:])
                elif j in (1, 2):
                    pe.wait_ge(*emptied(b, 0))
                    for m in range(2):
                        col = (2 * (j - 1) + m) * P
                        for k in range(KD):
                            ins = pe.matmul(ps[:, m * SEQ:(m + 1) * SEQ], wq_sb[:, k, col:col + P],
                                            xnt_sb[:, k, :], start=(k == 0), stop=(k == KD - 1))
                elif j in (3, 4):
                    pe.wait_ge(c_loaded[o], 32 * (nth_of_slot + 1))
                    for m in range(2):
                        col = (2 * (j - 3) + m) * P
                        for k, rows in enumerate(CTX_K):
                            ins = pe.matmul(ps[:, m * SEQ:(m + 1) * SEQ], wk_sb[0:rows, k, col:col + P],
                                            c_sb[o][0:rows, k, :], start=(k == 0), stop=(k == 1))
                elif j in (5, 6):
                    m = j - 5
                    for k, rows in enumerate(CTX_K):
                        ins = pe.matmul(ps[:, 0:INNER], c_sb[o][0:rows, k, m * P:(m + 1) * P],
                                        wv_sb[0:rows, k, :], start=(k == 0), stop=(k == 1))
                elif j in (PRO, PRO + 1):
                    g = j - PRO
                    pe.wait_ge(o_ready, nth(2 * b + g))
                    for k in range(GK):
                        for t in range(NT):
                            ins = pe.transpose(ps[:, k * SEQ + t * P:k * SEQ + (t + 1) * P],
                                               o_sb[:, t, (g * GK + k) * P:(g * GK + k + 1) * P], ident[:])
                else:
                    for g in range(2):
                        pe.wait_ge(*emptied(b, PRO + g))
                    for t in range(NT):
                        for k in range(INNER // P):
                            ins = pe.matmul(ps[:, t * D:(t + 1) * D], ot_sb[:, k, t * P:(t + 1) * P],
                                            wo_sb[:, k, :], start=(k == 0), stop=(k == INNER // P - 1))
                ins.then_inc(full(b, j)[0], 1)

            def step(pair, s, last):
                b = 2 * pair + s
                for i in range(TURNS):
                    if i < H:
                        u = H * b + i
                        if i == 0:
                            for j in (3, 4):
                                pe.wait_ge(*ready(b, j))
                        pe.wait_ge(exp_done, two_before(u))
                        m, r = i // HPT, (i % HPT) * R
                        for t in range(NT):
                            ins = pe.matmul(score_ps[i % 2][:, t, :], q_sb[s][r:r + R, m, t * P:(t + 1) * P],
                                            k_sb[s][r:r + R, m, :], start=True, stop=True)
                        ins.then_inc(scores_done, 1)
                    if 0 <= i - SIDE_AT < PRO and not last:
                        side(pair, s, i - SIDE_AT)
                    if 0 <= i - 2 < H:
                        h = i - 2
                        u = H * b + h
                        pe.wait_ge(exp_done, nth(u))
                        pe.wait_ge(prob_t_ready, two_before(u))
                        for k in range(2):
                            for t in range(NT):
                                ins = pe.transpose(trans_ps[h % 2][:, k, t * P:(t + 1) * P],
                                                   prob[h % 2][:, t, k * P:(k + 1) * P], ident[:])
                        ins.then_inc(turned, 1)
                    if 0 <= i - 3 < H:
                        h = i - 3
                        u = H * b + h
                        g, hg = h // HG, h % HG
                        if h == 0:
                            for j in (5, 6):
                                pe.wait_ge(*ready(b, j))
                        if hg == 0:
                            pe.wait_ge(o_ready, two_before(2 * b + g))
                        pe.wait_ge(prob_t_ready, nth(u))
                        for t in range(NT):
                            for k in range(2):
                                ins = pe.matmul(out_ps[g][:, t, hg * head_dim:(hg + 1) * head_dim],
                                                prob_t[h % 2][:, k, t * P:(t + 1) * P],
                                                v_sb[s][:, k, h * head_dim:(h + 1) * head_dim],
                                                start=(k == 0), stop=(k == 1))
                        ins.then_inc(pv_done, 1)
                for j in range(PRO, SIDE):
                    side(pair, s, j)

            for j in range(PRO):
                side(-1, 1, j)
            for bank in range(2):
                pe.wait_ge(side_free[bank], sum(j < PRO for j in FREE_STEPS[bank]))
                pe.sem_inc(side_free[bank], sum(j >= PRO for j in FREE_STEPS[bank]))
                pe.sem_inc(side_full[bank], sum(j >= PRO for j in FULL_STEPS[bank]))
            pair_loop(pe, step)

        @block.vector
        def _(dve):
            dve.sem_inc(prob_t_ready, CREDIT)
            dve.sem_inc(o_ready, CREDIT)
            dve.sem_inc(xo_ready, CREDIT)
            dve.wait_ge(weights_in, WEIGHTS)
            if biased:
                dve.tensor_scalar(qb_sb[:], qb_sb[:], SCALE, None, ALU.mult).then_inc(qb_scaled, 1)

            def statistics(pair, s):
                n, o = 2 * pair + s + 1, 1 - s
                dve.wait_ge(x_loaded[o], 16 * (pair + s + 1))
                if not (isinstance(n, int) and n == 0):
                    dve.wait_ge(xn_ready, n)
                row_stats(dve, stats_step, STATS_STEPS * n, x_sb[o][:], stats[:], mean_var[:], half_v[:],
                          seed_bits[:], rstd[:]).then_inc(seed_ready, 1)

            def side(pair, s, j):
                b = 2 * pair + s
                o = 1 - s
                bank = j % 2
                ps = side_ps[bank]
                if j in (3, 4):
                    dve.wait_ge(*full(b, j))
                    k = k_sb[o][:, 2 * (j - 3):2 * (j - 3) + 2, :]
                    if biased:
                        for n in range(2):
                            m = 2 * (j - 3) + n
                            ins = dve.tensor_scalar(k[:, n, :], ps[:, n * SEQ:(n + 1) * SEQ],
                                                    kb_sb[:, m:m + 1], None, ALU.add)
                    else:
                        ins = dve.tensor_copy(k.rearrange("p k n -> p (k n)"), ps[:])
                    ins.then_inc(side_free[bank], 1)
                elif j in (5, 6):
                    dve.wait_ge(*full(b, j))
                    if biased:
                        ins = dve.tensor_tensor(v_sb[o][:, j - 5, :], ps[:, 0:INNER], vb_sb[:], ALU.add)
                    else:
                        ins = dve.tensor_copy(v_sb[o][:, j - 5, :], ps[:, 0:INNER])
                    ins.then_inc(side_free[bank], 1)
                elif j == SIDE - 1:
                    dve.wait_ge(*full(b, j))
                    dve.wait_ge(xb_ready, nth(b))
                    dve.wait_ge(stored[s], 16 * pair + 16)
                    dve.tensor_tensor(xo_sb[s][:].rearrange("p t d -> p (t d)"), ps[:],
                                      xb_sb[s][:].rearrange("p t d -> p (t d)"), ALU.add)\
                       .then_inc(xo_ready, 1)

            def step(pair, s, last):
                b = 2 * pair + s
                for i in range(TURNS):
                    if i < H:
                        u = H * b + i
                        dve.wait_ge(scores_done, u + 1)
                        dve.tensor_reduce(neg_max[i % 2][:], score_ps[i % 2][:], AX.X, ALU.max, negate=True)\
                           .then_inc(max_done, 1)
                    if i == 0 and not last:
                        statistics(pair, s)
                    if 0 <= i - SIDE_AT < PRO and not last:
                        side(pair, s, i - SIDE_AT)
                    if 0 <= i - 2 < H:
                        h = i - 2
                        u = H * b + h
                        dve.wait_ge(turned, nth(u))
                        dve.wait_ge(pv_done, two_before(u))
                        dve.tensor_copy(prob_t[h % 2][:], trans_ps[h % 2][:]).then_inc(prob_t_ready, 1)
                    g = group_end(i)
                    if g is not None:
                        dve.wait_ge(exp_done, nth(H * b + (g + 1) * HG - 1))
                        dve.reciprocal(inv_sum[g][:], row_sum[s][:, :, g * HG:(g + 1) * HG])\
                           .then_inc(inv_ready, 1)
                        dve.wait_ge(inv_ready, 2 * b + g + 1)
                        dve.wait_ge(pv_done, nth(H * b + (g + 1) * HG - 1))
                        for t in range(NT):
                            ins = dve.tensor_tensor(
                                o_sb[:, t, g * GI:(g + 1) * GI].rearrange("p (h d) -> p h d", d=head_dim),
                                out_ps[g][:, t, :].rearrange("p (h d) -> p h d", d=head_dim),
                                inv_sum[g][:, t, :].unsqueeze(2).to_broadcast([P, HG, head_dim]), ALU.mult)
                        ins.then_inc(o_ready, 1)
                side(pair, s, SIDE - 1)

            statistics(-1, 1)
            for j in range(PRO):
                side(-1, 1, j)
            pair_loop(dve, step)

EXPERTS, HID = 8, 1024
TILES = BATCH * NT
DENOM_MIN = 1e-9


def gated_experts(nc, tag, x_in, w_gate, w_gate_up, w_down, x_out, ident_in, iota_in):
    FT = HID // P
    CH = 512
    CHUNKS = BATCH * SEQ // CH
    CT = CH // P
    PIECE = 2 * HID
    PIECES = KD + 1
    HIDDENS = CHUNKS * FT
    assert FT * D == PIECE

    with ExitStack() as ctx:
        def sb(name, shape, dt=F32):
            return ctx.enter_context(nc.sbuf_tensor(f"{tag}_{name}", shape, dt))

        def pb(name, shape):
            return ctx.enter_context(nc.psum_tensor(f"{tag}_{name}", shape, F32))

        def sem(name):
            return ctx.enter_context(nc.semaphore(f"{tag}_{name}"))

        xt_hi = sb("xt_hi", [P, KD, BATCH * SEQ], F32R)
        xt_lo = sb("xt_lo", [P, KD, BATCH * SEQ], F32R)
        acc = sb("acc", [P, TILES, D])
        gate = sb("gate", [P, TILES, EXPERTS])
        weights_in = sem("weights_in")

        route_tokens(nc, ctx, tag, x_in, w_gate, ident_in, iota_in, xt_hi, xt_lo, gate)

        w_hi = [sb(f"w_hi{i}", [P, PIECES, PIECE], F32R) for i in range(2)]
        w_lo = [sb(f"w_lo{i}", [P, PIECES, PIECE], F32R) for i in range(2)]
        stage = [sb(f"stage{i}", [P, PIECE]) for i in range(2)]
        silu = [sb(f"silu{i}", [P, CH]) for i in range(2)]
        prod = [sb(f"prod{i}", [P, CH]) for i in range(2)]
        h_hi = [sb(f"h_hi{i}", [P, CH], F32R) for i in range(2)]
        h_lo = [sb(f"h_lo{i}", [P, CH], F32R) for i in range(2)]
        g_ps = [pb(f"g{i}", [P, CH]) for i in range(2)]
        u_ps = [pb(f"u{i}", [P, CH]) for i in range(2)]
        y_ps = pb("y", [P, CT, D])

        tick = sb("tick", [P, 1])
        constant_set = sem("constant_set")
        acc_loaded = sem("acc_loaded")
        staged = [sem(f"staged{i}") for i in range(2)]
        stage_used = sem("stage_used")
        split_hi = sem("split_hi")
        gu_done = sem("gu_done")
        silu_done = sem("silu_done")
        prod_done = sem("prod_done")
        hi_done = sem("hi_done")
        lo_done = sem("lo_done")
        down_done = sem("down_done")
        y_taken = sem("y_taken")
        stored = sem("stored")

        block = ctx.enter_context(nc.Block())

        def hidden_index(pair, s, c, f):
            return (2 * pair + s) * CHUNKS * FT + c * FT + f

        def expert_pairs(eng, expert):
            with eng.Fori(0, EXPERTS // 2) as pair:
                expert(pair, 0)
                expert(pair, 1)

        @block.sync
        def _(sp):
            sp.dma_start(acc[:], x_in.rearrange("b (t p) d -> p (b t) d", p=P)).then_inc(acc_loaded, 16)

            with sp.Fori(0, EXPERTS // 2) as pair:
                for s in range(2):
                    for i in range(PIECES):
                        n = (2 * pair + s) * PIECES + i
                        slot = (s * PIECES + i) % 2
                        sp.wait_ge(stage_used, two_before(n))
                        if i < KD:
                            src = w_gate_up[2 * pair + s, i * P:(i + 1) * P, :]
                            sp.dma_start(stage[slot][:], src).then_inc(staged[slot], 16)
                        else:
                            src = w_down[2 * pair + s].rearrange("(f p) d -> p f d", p=P)
                            sp.dma_start(stage[slot][:].rearrange("p (f d) -> p f d", d=D), src)\
                              .then_inc(staged[slot], 16)
            sp.wait_ge(y_taken, EXPERTS * CHUNKS + 1)
            sp.dma_start(x_out.rearrange("b (t p) d -> p (b t) d", p=P), acc[:]).then_inc(stored, 16)
            sp.wait_ge(stored, 16)

        @block.gpsimd
        def _(pool):
            pool.sem_inc(stage_used, CREDIT)
            pool.memset(tick[:], 0.0).then_inc(constant_set, 1)
            pool.wait_ge(constant_set, 1)

            def split(pair, s):
                pool.wait_ge(down_done, (2 * pair + s + 1) * HIDDENS)
                for i in range(PIECES):
                    n = (2 * pair + s) * PIECES + i
                    slot = (s * PIECES + i) % 2
                    pool.wait_ge(staged[slot], 16 * (PIECES * pair + (s * PIECES + i) // 2 + 1))
                    pool.tensor_tensor(tick[:], tick[:], tick[:], ALU.mult)
                    pool.tensor_copy(w_hi[s][:, i, :], stage[slot][:]).then_inc(split_hi, 1)
                    pool.wait_ge(split_hi, n + 1)
                    pool.tensor_tensor(w_lo[s][:, i, :], stage[slot][:], w_hi[s][:, i, :].bitcast(F32),
                                       ALU.subtract).then_inc(stage_used, 1)

            expert_pairs(pool, split)

        @block.scalar
        def _(act):
            def expert(pair, s):
                with act.Fori(0, CHUNKS) as c:
                    for f in range(FT):
                        n = hidden_index(pair, s, c, f)
                        i = f % 2
                        act.wait_ge(prod_done, two_before(n))
                        act.wait_ge(gu_done, n + 1)
                        act.activation(silu[i][:], g_ps[i][:], ACT.Silu).then_inc(silu_done, 1)
                        act.wait_ge(down_done, 2 * HIDDENS + n - 1)
                        act.wait_ge(prod_done, nth(n))
                        act.activation(h_hi[i][:], prod[i][:], ACT.Copy).then_inc(hi_done, 1)

            expert_pairs(act, expert)

        @block.tensor
        def _(pe):
            pe.sem_inc(down_done, 2 * HIDDENS)

            def three_passes(out, a_hi, a_lo, b_hi, b_lo, start, stop):
                pe.matmul(out, a_hi, b_hi, start=start, stop=False, skip_group_check=True)
                pe.matmul(out, a_lo, b_hi, start=False, stop=False, skip_group_check=True)
                return pe.matmul(out, a_hi, b_lo, start=False, stop=stop, skip_group_check=True)

            def expert(pair, s):
                with pe.Fori(0, CHUNKS) as c:
                    pe.wait_ge(stage_used, nth((2 * pair + s) * PIECES + PIECES - 1))
                    def down(f):
                        n = hidden_index(pair, s, c, f)
                        i = f % 2
                        if f == 0:
                            pe.wait_ge(y_taken, (2 * pair + s) * CHUNKS + c + 1)
                        pe.wait_ge(lo_done, n + 1)
                        for t in range(CT):
                            a, cols = slice(t * P, (t + 1) * P), slice(f * D, (f + 1) * D)
                            ins = three_passes(y_ps[:, t, :], h_hi[i][:, a], h_lo[i][:, a],
                                               w_hi[s][:, KD, cols], w_lo[s][:, KD, cols],
                                               f == 0 and t % 2 == 0, f == FT - 1)
                        ins.then_inc(down_done, 1)

                    for f in range(FT):
                        n = hidden_index(pair, s, c, f)
                        i = f % 2
                        pe.wait_ge(prod_done, two_before(n))
                        for ps, first in ((g_ps[i], f * P), (u_ps[i], HID + f * P)):
                            for k in range(KD):
                                ins = three_passes(ps[:], w_hi[s][:, k, first:first + P],
                                                   w_lo[s][:, k, first:first + P],
                                                   xt_hi[:, k, bass.ts(c, CH)], xt_lo[:, k, bass.ts(c, CH)],
                                                   k == 0, k == KD - 1)
                        ins.then_inc(gu_done, 1)
                        if f >= 1:
                            down(f - 1)
                    down(FT - 1)

            expert_pairs(pe, expert)

        @block.vector
        def _(dve):
            dve.sem_inc(prod_done, CREDIT)
            dve.sem_inc(y_taken, 1)
            dve.wait_ge(acc_loaded, 16)

            def expert(pair, s):
                with dve.Fori(0, CHUNKS) as c:
                    for f in range(FT):
                        n = hidden_index(pair, s, c, f)
                        i = f % 2
                        dve.wait_ge(silu_done, n + 1)
                        dve.tensor_tensor(prod[i][:], silu[i][:], u_ps[i][:], ALU.mult).then_inc(prod_done, 1)
                        dve.wait_ge(hi_done, n + 1)
                        dve.tensor_tensor(h_lo[i][:], prod[i][:], h_hi[i][:].bitcast(F32), ALU.subtract)\
                           .then_inc(lo_done, 1)
                    dve.wait_ge(down_done, 2 * HIDDENS + hidden_index(pair, s, c, FT))
                    for t in range(CT):
                        tile = c * CT + t
                        ins = dve.scalar_tensor_tensor(
                            acc[:, bass.ds(tile, 1), :].rearrange("p a d -> p (a d)"), y_ps[:, t, :],
                            gate[:, bass.ds(tile, 1), bass.ds(2 * pair + s, 1)].rearrange("p a e -> p (a e)"),
                            acc[:, bass.ds(tile, 1), :].rearrange("p a d -> p (a d)"), ALU.mult, ALU.add)
                    ins.then_inc(y_taken, 1)

            expert_pairs(dve, expert)


def route_tokens(nc, ctx_outer, tag, x_in, w_gate, ident_in, iota_in, xt_hi, xt_lo, gate):
    with ExitStack() as ctx:
        def sb(name, shape, dt=F32):
            return ctx.enter_context(nc.sbuf_tensor(f"{tag}r_{name}", shape, dt))

        def pb(name, shape):
            return ctx.enter_context(nc.psum_tensor(f"{tag}r_{name}", shape, F32))

        def sem(name):
            return ctx.enter_context(nc.semaphore(f"{tag}r_{name}"))

        ident = sb("ident", [P, P])
        iota = sb("iota", [P, EXPERTS])
        wg_sb = sb("wg", [P, KD, EXPERTS])
        x_sb = [sb(f"x{i}", [P, NT, D]) for i in range(2)]
        xn_sb = [sb(f"xn{i}", [P, NT, D]) for i in range(2)]
        xt_sb = [sb(f"xt{i}", [P, KD, SEQ]) for i in range(2)]
        logits = sb("logits", [P, TILES, EXPERTS])
        ex = sb("ex", [P, TILES, EXPERTS])
        left = sb("left", [P, TILES, EXPERTS])
        mask = sb("mask", [P, TILES, EXPERTS])
        mask2 = sb("mask2", [P, TILES, EXPERTS])
        cand = sb("cand", [P, TILES, EXPERTS])
        red = sb("red", [P, TILES])
        stats = sb("stats", [P, NT, 6])
        mean_var = sb("mv", [P, NT, 2])
        half_v = sb("halfv", [P, NT])
        seed_bits = sb("seedb", [P, NT], I32)
        rstd = sb("rstd", [P, NT])
        nwt = sb("nwt", [P, NT])
        three_halves = sb("three_halves", [P, NT])
        trans_ps = [pb(f"trans{i}", [P, KD, SEQ]) for i in range(2)]
        logit_ps = [pb(f"logit{i}", [P, NT, EXPERTS]) for i in range(2)]

        weights_in = sem("weights_in")
        x_loaded = [sem(f"x_loaded{i}") for i in range(2)]
        constant_set = sem("constant_set")
        stats_step = sem("stats_step")
        seed_ready = sem("seed_ready")
        newton_step = sem("newton_step")
        xn_ready = sem("xn_ready")
        turned = sem("turned")
        hi_done = sem("hi_done")
        xt_done = sem("xt_done")
        lo_done = sem("lo_done")
        logits_done = sem("logits_done")
        logits_taken = sem("logits_taken")
        gate_step = sem("gate_step")
        exp_done = sem("exp_done")

        x_dram = x_in.rearrange("b (t p) d -> b p t d", p=P)
        block = ctx.enter_context(nc.Block())

        def pairs(eng, step):
            with eng.Fori(0, BATCH // 2) as pair:
                step(pair, 0)
                step(pair, 1)

        @block.sync
        def _(sp):
            sp.dma_start(ident[:], ident_in).then_inc(weights_in, 16)
            sp.dma_start(iota[:], iota_in.partition_broadcast(P)).then_inc(weights_in, 16)
            sp.dma_start(wg_sb[:], w_gate.rearrange("(k p) e -> p k e", p=P)).then_inc(weights_in, 16)

            def load(pair, s):
                b = 2 * pair + s
                sp.wait_ge(xn_ready, two_before(b))
                sp.dma_start(x_sb[s][:], x_dram[b]).then_inc(x_loaded[s], 16)

            pairs(sp, load)

        @block.gpsimd
        def _(pool):
            pool.sem_inc(xn_ready, CREDIT)
            pool.memset(three_halves[:], 1.5).then_inc(constant_set, 1)
            pool.wait_ge(constant_set, 1)

            def normalise(pair, s):
                b = 2 * pair + s
                pool.wait_ge(turned, two_before(b))
                pool.wait_ge(seed_ready, b + 1)
                newton_rsqrt(pool, newton_step, NEWTON_STEPS * b, rstd[:], half_v[:], nwt[:],
                             three_halves[:])
                pool.tensor_tensor(nwt[:], nwt[:], nwt[:], ALU.mult)
                for t in range(NT):
                    ins = pool.tensor_scalar(xn_sb[s][:, t, :], x_sb[s][:, t, :], mean_var[:, t, 0:1],
                                             rstd[:, t:t + 1], ALU.subtract, ALU.mult)
                ins.then_inc(xn_ready, 1)

            pairs(pool, normalise)

        @block.scalar
        def _(act):
            act.sem_inc(xt_done, CREDIT)

            def split(pair, s):
                b = 2 * pair + s
                act.wait_ge(turned, nth(b))
                act.wait_ge(logits_done, two_before(b))
                act.wait_ge(lo_done, two_before(b))
                act.activation(xt_sb[s][:], trans_ps[s][:], ACT.Copy).then_inc(xt_done, 1)
                act.wait_ge(xt_done, nth(b))
                for k in range(KD):
                    ins = act.activation(xt_hi[:, k, bass.ts(b, SEQ)], xt_sb[s][:, k, :], ACT.Copy)
                ins.then_inc(hi_done, 1)

            pairs(act, split)
            act.wait_ge(gate_step, 2)
            act.activation(ex[:], ex[:], ACT.Exp).then_inc(exp_done, 1)

        @block.tensor
        def _(pe):
            pe.sem_inc(turned, CREDIT)
            pe.sem_inc(logits_done, CREDIT)
            pe.wait_ge(weights_in, 48)

            def turn(pair, s):
                b = 2 * pair + s
                pe.wait_ge(xt_done, two_before(b))
                pe.wait_ge(xn_ready, nth(b))
                for k in range(KD):
                    for t in range(NT):
                        ins = pe.transpose(trans_ps[s][:, k, t * P:(t + 1) * P],
                                           xn_sb[s][:, t, k * P:(k + 1) * P], ident[:])
                ins.then_inc(turned, 1)
                pe.wait_ge(logits_taken, two_before(b))
                pe.wait_ge(xt_done, nth(b))
                for t in range(NT):
                    for k in range(KD):
                        ins = pe.matmul(logit_ps[s][:, t, :], xt_sb[s][:, k, t * P:(t + 1) * P], wg_sb[:, k, :],
                                        start=(k == 0), stop=(k == KD - 1))
                ins.then_inc(logits_done, 1)

            pairs(pe, turn)

        @block.vector
        def _(dve):
            dve.sem_inc(lo_done, CREDIT)
            dve.sem_inc(logits_taken, CREDIT)
            dve.wait_ge(weights_in, 48)

            def step(pair, s):
                b = 2 * pair + s
                dve.wait_ge(xn_ready, b + CREDIT)
                dve.wait_ge(x_loaded[s], 16 * (pair + 1))
                row_stats(dve, stats_step, STATS_STEPS * b, x_sb[s][:], stats[:], mean_var[:], half_v[:],
                          seed_bits[:], rstd[:]).then_inc(seed_ready, 1)
                dve.wait_ge(hi_done, b + 1)
                for k in range(KD):
                    ins = dve.tensor_tensor(xt_lo[:, k, bass.ts(b, SEQ)], xt_sb[s][:, k, :],
                                            xt_hi[:, k, bass.ts(b, SEQ)].bitcast(F32), ALU.subtract)
                ins.then_inc(lo_done, 1)
                dve.wait_ge(logits_done, nth(b))
                dve.tensor_copy(logits[:, bass.ts(b, NT), :], logit_ps[s][:]).then_inc(logits_taken, 1)

            pairs(dve, step)

            def wide(ap):
                return ap.unsqueeze(2).to_broadcast([P, TILES, EXPERTS])

            iota_w = iota[:].unsqueeze(1).to_broadcast([P, TILES, EXPERTS])
            dve.wait_ge(logits_taken, nth(BATCH - 1))
            dve.tensor_reduce(red[:], logits[:], AX.X, ALU.max).then_inc(gate_step, 1)
            dve.wait_ge(gate_step, 1)
            dve.tensor_tensor(ex[:], logits[:], wide(red[:]), ALU.subtract).then_inc(gate_step, 1)
            dve.wait_ge(exp_done, 1)
            dve.tensor_reduce(red[:], ex[:], AX.X, ALU.add).then_inc(gate_step, 1)
            dve.wait_ge(gate_step, 3)
            dve.reciprocal(red[:], red[:]).then_inc(gate_step, 1)
            dve.wait_ge(gate_step, 4)
            dve.tensor_tensor(ex[:], ex[:], wide(red[:]), ALU.mult).then_inc(gate_step, 1)
            dve.wait_ge(gate_step, 5)
            dve.tensor_copy(left[:], ex[:]).then_inc(gate_step, 1)
            dve.wait_ge(gate_step, 6)
            at = 6
            for m in (mask, mask2):
                dve.tensor_reduce(red[:], left[:], AX.X, ALU.max).then_inc(gate_step, 1)
                dve.wait_ge(gate_step, at + 1)
                dve.tensor_tensor(cand[:], left[:], wide(red[:]), ALU.is_lt).then_inc(gate_step, 1)
                dve.wait_ge(gate_step, at + 2)
                dve.scalar_tensor_tensor(cand[:], cand[:], float(EXPERTS), iota_w, ALU.mult, ALU.add)\
                   .then_inc(gate_step, 1)
                dve.wait_ge(gate_step, at + 3)
                dve.tensor_reduce(red[:], cand[:], AX.X, ALU.min).then_inc(gate_step, 1)
                dve.wait_ge(gate_step, at + 4)
                dve.tensor_tensor(m[:], iota_w, wide(red[:]), ALU.is_equal).then_inc(gate_step, 1)
                dve.wait_ge(gate_step, at + 5)
                dve.scalar_tensor_tensor(left[:], m[:], -2.0, left[:], ALU.mult, ALU.add)\
                   .then_inc(gate_step, 1)
                dve.wait_ge(gate_step, at + 6)
                at += 6
            dve.tensor_tensor(mask[:], mask[:], mask2[:], ALU.add).then_inc(gate_step, 1)
            dve.wait_ge(gate_step, at + 1)
            dve.tensor_tensor(ex[:], ex[:], mask[:], ALU.mult).then_inc(gate_step, 1)
            dve.wait_ge(gate_step, at + 2)
            dve.tensor_reduce(red[:], ex[:], AX.X, ALU.add).then_inc(gate_step, 1)
            dve.wait_ge(gate_step, at + 3)
            dve.tensor_scalar(red[:], red[:], DENOM_MIN, None, ALU.max).then_inc(gate_step, 1)
            dve.wait_ge(gate_step, at + 4)
            dve.reciprocal(red[:], red[:]).then_inc(gate_step, 1)
            dve.wait_ge(gate_step, at + 5)
            dve.tensor_tensor(gate[:], ex[:], wide(red[:]), ALU.mult)


SLOT_EXPERTS, SLOTS, SLOT_HID = 16, 64, 512
ALL_SLOTS = SLOT_EXPERTS * SLOTS
ST = ALL_SLOTS // P
SF = SLOT_HID // P
NS = BATCH * SLOTS
RANGE = KD * NS
PAIR_COLS = 2 * RANGE


def normalise_slots(nc, tag, slot_embeds, slot_g, slot_b, scale, ident_in, se_t, se_sw):
    with ExitStack() as ctx:
        def sb(name, shape, dt=F32):
            return ctx.enter_context(nc.sbuf_tensor(f"{tag}_{name}", shape, dt))

        def sem(name):
            return ctx.enter_context(nc.semaphore(f"{tag}_{name}"))

        ident = sb("ident", [P, P])
        rows = sb("rows", [P, ST, D])
        g_sb = sb("g", [P, D])
        b_sb = sb("b", [P, D])
        scale_sb = sb("scale", [P, 1])
        stats = sb("stats", [P, ST, 6])
        mean_var = sb("mv", [P, ST, 2])
        half_v = sb("halfv", [P, ST])
        seed_bits = sb("seedb", [P, ST], I32)
        rstd = sb("rstd", [P, ST])
        nwt = sb("nwt", [P, ST])
        three_halves = sb("three_halves", [P, ST])
        turn_ps = [ctx.enter_context(nc.psum_tensor(f"{tag}_turn{i}", [P, 4, P], F32)) for i in range(4)]

        loaded = sem("loaded")
        constant_set = sem("constant_set")
        stats_step = sem("stats_step")
        seed_ready = sem("seed_ready")
        newton_step = sem("newton_step")
        normed = sem("normed")
        turned = sem("turned")
        taken = sem("taken")

        block = ctx.enter_context(nc.Block())

        @block.sync
        def _(sp):
            sp.dma_start(rows[:], slot_embeds.rearrange("e s d -> (e s) d").rearrange("(t p) d -> p t d", p=P))\
              .then_inc(loaded, 16)
            sp.dma_start(ident[:], ident_in).then_inc(loaded, 16)
            sp.dma_start(g_sb[:], slot_g.partition_broadcast(P)).then_inc(loaded, 16)
            sp.dma_start(b_sb[:], slot_b.partition_broadcast(P)).then_inc(loaded, 16)
            sp.dma_start(scale_sb[:], scale.partition_broadcast(P)).then_inc(loaded, 16)

        @block.gpsimd
        def _(pool):
            pool.memset(three_halves[:], 1.5).then_inc(constant_set, 1)
            pool.wait_ge(constant_set, 1)
            pool.wait_ge(seed_ready, 1)
            newton_rsqrt(pool, newton_step, 0, rstd[:], half_v[:], nwt[:], three_halves[:])

        @block.vector
        def _(dve):
            dve.wait_ge(loaded, 80)
            row_stats(dve, stats_step, 0, rows[:], stats[:], mean_var[:], half_v[:], seed_bits[:],
                      rstd[:]).then_inc(seed_ready, 1)
            dve.wait_ge(newton_step, NEWTON_STEPS)
            for t in range(ST):
                ins = dve.tensor_scalar(rows[:, t, :], rows[:, t, :], mean_var[:, t, 0:1], rstd[:, t:t + 1],
                                        ALU.subtract, ALU.mult)
            ins.then_inc(normed, 1)
            dve.wait_ge(normed, 1)
            dve.tensor_tensor(rows[:], rows[:], g_sb[:].unsqueeze(1).to_broadcast([P, ST, D]), ALU.mult)\
               .then_inc(normed, 1)
            dve.wait_ge(normed, 2)
            dve.tensor_tensor(rows[:], rows[:], b_sb[:].unsqueeze(1).to_broadcast([P, ST, D]), ALU.add)\
               .then_inc(normed, 1)
            dve.wait_ge(normed, 3)
            dve.tensor_scalar(rows[:], rows[:], scale_sb[:], None, ALU.mult).then_inc(normed, 1)

        @block.tensor
        def _(pe):
            pe.wait_ge(normed, 4)
            for k in range(KD):
                for half in range(2):
                    for t in range(4):
                        ins = pe.transpose(turn_ps[2 * k + half][:, t, :],
                                           rows[:, 4 * half + t, k * P:(k + 1) * P], ident[:])
                    ins.then_inc(turned, 1)

        @block.scalar
        def _(act):
            for k in range(KD):
                for half in range(2):
                    n = 2 * k + half
                    act.wait_ge(turned, n + 1)
                    cols = slice(half * 4 * P, (half + 1) * 4 * P)
                    act.activation(se_t[:, k, cols], turn_ps[n][:].rearrange("p t s -> p (t s)"), ACT.Copy)
                    src = turn_ps[n][:].rearrange("p t (r s) -> p t r s", r=2)
                    dst = se_sw[:, k, cols].rearrange("p (t r s) -> p t r s", t=4, r=2)
                    for r in range(2):
                        act.activation(dst[:, :, r, :], src[:, :, 1 - r, :], ACT.Copy)


def dispatch_tokens(nc, tag, x_in, norm_g, norm_b, ident_in, se_t, se_sw, arena, inv_rows, comb_dram):
    HALF = ALL_SLOTS // 2
    QUARTERS = 4
    EH = SLOT_EXPERTS // 4
    SLOTS_CREDIT = 8
    COMB_CREDIT = 4
    DISP_CREDIT = 2

    with ExitStack() as ctx:
        def sb(name, shape, dt=F32):
            return ctx.enter_context(nc.sbuf_tensor(f"{tag}_{name}", shape, dt))

        def pb(name, shape):
            return ctx.enter_context(nc.psum_tensor(f"{tag}_{name}", shape, F32))

        def sem(name):
            return ctx.enter_context(nc.semaphore(f"{tag}_{name}"))

        ident = sb("ident", [P, P])
        g_sb = sb("g", [P, D])
        b_sb = sb("b", [P, D])
        x_sb = [sb(f"x{i}", [P, NT, D]) for i in range(2)]
        xh_sb = [sb(f"xh{i}", [P, NT, D]) for i in range(2)]
        xt_sb = [sb(f"xt{i}", [P, KD, SEQ]) for i in range(2)]
        comb = [sb(f"comb{i}", [P, ALL_SLOTS]) for i in range(2)]
        comb_t = [sb(f"combt{i}", [P, ST, P]) for i in range(2)]
        disp_t = [sb(f"dispt{i}", [P, 2, SEQ]) for i in range(2)]
        disp = sb("disp", [P, NT, ALL_SLOTS])
        stats = sb("stats", [P, NT, 6])
        mean_var = sb("mv", [P, NT, 2])
        half_v = sb("halfv", [P, NT])
        seed_bits = sb("seedb", [P, NT], I32)
        rstd = sb("rstd", [P, NT])
        nwt = sb("nwt", [P, NT])
        three_halves = sb("three_halves", [P, NT])
        neg_max_c = [sb(f"nmaxc{i}", [P, 1]) for i in range(2)]
        sum_c = [sb(f"sumc{i}", [P, 1]) for i in range(2)]
        neg_max_d = [sb(f"nmaxd{i}", [P, 2]) for i in range(2)]
        sum_d = [sb(f"sumd{i}", [P, 2]) for i in range(2)]
        inv_d = [sb(f"invd{i}", [P, 2]) for i in range(2)]

        comb_ps = pb("combp", [P, 2, HALF])
        disp_ps = [pb(f"dispp{i}", [P, 2, SEQ]) for i in range(2)]
        turn_ps = [pb(f"turn{i}", [P, 4, P]) for i in range(2)]
        slot_ps = [pb(f"slot{i}", [P, HALF]) for i in range(2)]

        weights_in = sem("weights_in")
        x_loaded = [sem(f"x_loaded{i}") for i in range(2)]
        constant_set = sem("constant_set")
        stats_step = sem("stats_step")
        seed_ready = sem("seed_ready")
        newton_step = sem("newton_step")
        xn_ready = sem("xn_ready")
        norm_step = sem("norm_step")
        xh_ready = sem("xh_ready")
        xt_turned = sem("xt_turned")
        xt_ready = sem("xt_ready")
        comb_logits = sem("comb_logits")
        comb_max = sem("comb_max")
        comb_exp = sem("comb_exp")
        inv_step = sem("inv_step")
        comb_turned = sem("comb_turned")
        comb_taken = sem("comb_taken")
        comb_stored = [sem(f"comb_stored{i}") for i in range(2)]
        disp_logits = sem("disp_logits")
        disp_max = sem("disp_max")
        disp_exp = sem("disp_exp")
        inv_d_ready = sem("inv_d_ready")
        disp_ready = sem("disp_ready")
        disp_turned = sem("disp_turned")
        disp_taken = sem("disp_taken")
        slots_done = sem("slots_done")
        slots_taken = sem("slots_taken")

        x_dram = x_in.rearrange("b (t p) d -> b p t d", p=P)
        block = ctx.enter_context(nc.Block())

        def pairs(eng, step):
            with eng.Fori(0, BATCH // 2) as pair:
                step(pair, 0)
                step(pair, 1)

        @block.sync
        def _(sp):
            sp.sem_inc(comb_stored[0], 16)
            sp.sem_inc(comb_stored[1], 16)
            sp.dma_start(ident[:], ident_in).then_inc(weights_in, 16)
            sp.dma_start(g_sb[:], norm_g.partition_broadcast(P)).then_inc(weights_in, 16)
            sp.dma_start(b_sb[:], norm_b.partition_broadcast(P)).then_inc(weights_in, 16)

            def load(pair, s):
                sp.wait_ge(xn_ready, two_before(2 * pair + s))
                sp.dma_start(x_sb[s][:], x_dram[2 * pair + s]).then_inc(x_loaded[s], 16)

            def store(pair, s):
                for t in range(NT):
                    n = (2 * pair + s) * NT + t
                    sp.wait_ge(comb_taken, nth(2 * n + 1))
                    sp.dma_start(comb_dram[2 * pair + s, :, :, t * P:(t + 1) * P].rearrange("i s n -> s i n"),
                                 comb_t[t][:]).then_inc(comb_stored[t], 16)

            load(0, 0)
            load(0, 1)
            with sp.Fori(0, BATCH // 2 - 1) as pair:
                for s in range(2):
                    store(pair, s)
                    load(pair + 1, s)
            for s in range(2):
                store(BATCH // 2 - 1, s)
            for t in range(NT):
                sp.wait_ge(comb_stored[t], 16 * (BATCH + 1))

        @block.gpsimd
        def _(pool):
            pool.sem_inc(xn_ready, CREDIT)
            pool.sem_inc(norm_step, CREDIT)
            pool.memset(three_halves[:], 1.5).then_inc(constant_set, 1)
            pool.wait_ge(constant_set, 1)
            pool.wait_ge(weights_in, 48)

            def normalise(pair, s):
                b = 2 * pair + s
                pool.wait_ge(slots_done, SLOTS_CREDIT + 4 * (b - 1))
                for twice in range(2):
                    src = x_sb[s] if twice == 0 else xh_sb[s]
                    pool.wait_ge(seed_ready, 2 * b + twice + 1)
                    newton_rsqrt(pool, newton_step, NEWTON_STEPS * (2 * b + twice), rstd[:], half_v[:], nwt[:],
                                 three_halves[:])
                    pool.tensor_tensor(nwt[:], nwt[:], nwt[:], ALU.mult)
                    for t in range(NT):
                        ins = pool.tensor_scalar(xh_sb[s][:, t, :], src[:, t, :], mean_var[:, t, 0:1],
                                                 rstd[:, t:t + 1], ALU.subtract, ALU.mult)
                    ins.then_inc(xn_ready if twice == 0 else norm_step, 1)
                pool.wait_ge(norm_step, CREDIT + 2 * b + 1)
                for t in range(NT):
                    ins = pool.tensor_tensor(xh_sb[s][:, t, :], xh_sb[s][:, t, :], g_sb[:], ALU.mult)
                ins.then_inc(norm_step, 1)
                pool.wait_ge(norm_step, CREDIT + 2 * b + 2)
                for t in range(NT):
                    ins = pool.tensor_tensor(xh_sb[s][:, t, :], xh_sb[s][:, t, :], b_sb[:], ALU.add)
                ins.then_inc(xh_ready, 1)

            pairs(pool, normalise)

        @block.scalar
        def _(act):
            act.sem_inc(comb_exp, CREDIT)
            act.sem_inc(slots_taken, CREDIT)

            def step(pair, s):
                b = 2 * pair + s
                act.wait_ge(xt_turned, b + 1)
                act.activation(xt_sb[s][:], turn_ps[0][:].rearrange("p (k t) n -> p k (t n)", k=KD), ACT.Copy)\
                   .then_inc(xt_ready, 1)
                for t in range(NT):
                    n = NT * b + t
                    act.wait_ge(comb_max, n + 1)
                    act.wait_ge(comb_turned, 2 * n - 2 + COMB_CREDIT)
                    act.activation(comb[t][:], comb_ps[:].rearrange("p a s -> p (a s)"), ACT.Exp,
                                   bias=neg_max_c[t][:], accum_out=sum_c[t][:]).then_inc(comb_exp, 1)
                for q in range(QUARTERS + 1):
                    if q < QUARTERS:
                        n = QUARTERS * b + q
                        i = q % 2
                        act.wait_ge(disp_max, n + 1)
                        act.wait_ge(disp_turned, two_before(n))
                        for j in range(2):
                            ins = act.activation(disp_t[i][:, j, :], disp_ps[i][:, j, :], ACT.Exp,
                                                 bias=neg_max_d[i][:, j:j + 1], accum_out=sum_d[i][:, j:j + 1])
                        ins.then_inc(disp_exp, 1)
                    if q >= 1:
                        n = QUARTERS * b + q - 1
                        act.wait_ge(disp_turned, nth(n))
                        act.wait_ge(slots_done, SLOTS_CREDIT + 4 * b)
                        act.activation(disp[:, :, (q - 1) * 2 * P:q * 2 * P].rearrange("p t s -> p t s"),
                                       turn_ps[1][:].rearrange("p (t j) s -> p t (j s)", t=NT), ACT.Copy)\
                           .then_inc(disp_taken, 1)
                for k in range(KD):
                    for half in range(2):
                        n = 4 * b + 2 * k + half
                        act.wait_ge(slots_done, SLOTS_CREDIT + n + 1)
                        src = slot_ps[half][:].rearrange("p (i r s) -> p i r s", r=2, s=SLOTS)
                        for r in range(2):
                            at = r * RANGE + k * NS
                            first = (2 * pair + (s if r == 0 else 1 - s)) * SLOTS
                            dst = arena[:, half * EH:(half + 1) * EH, at:at + NS]
                            ins = act.activation(dst[:, :, bass.ds(first, SLOTS)], src[:, :, r, :], ACT.Copy)
                        ins.then_inc(slots_taken, 1)

            pairs(act, step)

        @block.tensor
        def _(pe):
            pe.sem_inc(slots_done, SLOTS_CREDIT)
            pe.sem_inc(comb_turned, COMB_CREDIT)
            pe.sem_inc(disp_turned, CREDIT)
            pe.wait_ge(weights_in, 48)

            def step(pair, s):
                b = 2 * pair + s
                se = se_sw if s else se_t
                pe.wait_ge(comb_taken, nth(4 * b - 1))
                pe.wait_ge(xh_ready, b + 1)
                for k in range(KD):
                    for t in range(NT):
                        ins = pe.transpose(turn_ps[0][:, 2 * k + t, :], xh_sb[s][:, t, k * P:(k + 1) * P],
                                           ident[:])
                ins.then_inc(xt_turned, 1)
                pe.wait_ge(xt_ready, b + 1)

                def comb_scores(t):
                    n = NT * b + t
                    pe.wait_ge(comb_exp, n + CREDIT)
                    for half in range(2):
                        for k in range(KD):
                            ins = pe.matmul(comb_ps[:, half, :], xt_sb[s][:, k, t * P:(t + 1) * P],
                                            se[:, k, half * HALF:(half + 1) * HALF],
                                            start=(k == 0), stop=(k == KD - 1))
                    ins.then_inc(comb_logits, 1)

                def comb_turn(t):
                    n = NT * b + t
                    pe.wait_ge(comb_exp, nth(n))
                    for half in range(2):
                        pe.wait_ge(comb_taken, nth(2 * n + half - 1))
                        for i in range(4):
                            c = (4 * half + i) * P
                            ins = pe.transpose(turn_ps[0][:, i, :], comb[t][:, c:c + P], ident[:])
                        ins.then_inc(comb_turned, 1)

                def disp_scores(q):
                    n = QUARTERS * b + q
                    pe.wait_ge(disp_exp, DISP_CREDIT + n - 1)
                    for j in range(2):
                        for k in range(KD):
                            ins = pe.matmul(disp_ps[q % 2][:, j, :], se_t[:, k, (2 * q + j) * P:(2 * q + j + 1) * P],
                                            xt_sb[s][:, k, :], start=(k == 0), stop=(k == KD - 1))
                    ins.then_inc(disp_logits, 1)

                def disp_turn(q):
                    n = QUARTERS * b + q
                    pe.wait_ge(disp_ready, n + 1)
                    pe.wait_ge(disp_taken, DISP_CREDIT + n - 1 + 1)
                    for t in range(NT):
                        for j in range(2):
                            ins = pe.transpose(turn_ps[1][:, 2 * t + j, :], disp_t[q % 2][:, j, t * P:(t + 1) * P],
                                               ident[:])
                    ins.then_inc(disp_turned, 1)

                comb_scores(0)
                disp_scores(0)
                comb_scores(1)
                disp_scores(1)
                comb_turn(0)
                disp_turn(0)
                disp_scores(2)
                comb_turn(1)
                disp_turn(1)
                disp_scores(3)
                disp_turn(2)
                disp_turn(3)
                for k in range(KD):
                    for half in range(2):
                        n = 4 * b + 2 * k + half
                        pe.wait_ge(slots_taken, two_before(n))
                        pe.wait_ge(disp_taken, DISP_CREDIT + QUARTERS * (b + 1))
                        for t in range(NT):
                            ins = pe.matmul(slot_ps[half][:], xh_sb[s][:, t, k * P:(k + 1) * P],
                                            disp[:, t, half * HALF:(half + 1) * HALF],
                                            start=(t == 0), stop=(t == NT - 1))
                        ins.then_inc(slots_done, 1)

            pairs(pe, step)

        @block.vector
        def _(dve):
            dve.sem_inc(disp_exp, DISP_CREDIT)
            dve.sem_inc(disp_taken, DISP_CREDIT)
            dve.sem_inc(comb_taken, CREDIT)

            def statistics(pair, s, twice):
                n, o = 2 * pair + s + 1, 1 - s
                if twice:
                    dve.wait_ge(xn_ready, nth(n))
                else:
                    dve.wait_ge(norm_step, 2 * n + 1)
                    dve.wait_ge(x_loaded[o], 16 * (pair + s + 1))
                row_stats(dve, stats_step, STATS_STEPS * (2 * n + twice), xh_sb[o][:] if twice else x_sb[o][:],
                          stats[:], mean_var[:], half_v[:], seed_bits[:], rstd[:]).then_inc(seed_ready, 1)

            def step(pair, s, last):
                b = 2 * pair + s

                def comb_max_of(t):
                    n = NT * b + t
                    dve.wait_ge(comb_logits, n + 1)
                    dve.tensor_reduce(neg_max_c[t][:], comb_ps[:].rearrange("p a s -> p (a s)"), AX.X, ALU.max,
                                      negate=True).then_inc(comb_max, 1)

                def comb_take(t):
                    n = NT * b + t
                    dve.wait_ge(comb_exp, nth(n))
                    dve.reciprocal(inv_rows[:, bass.ds(n, 1)], sum_c[t][:])
                    dve.wait_ge(comb_stored[t], 16 * (b + 1))
                    for half in range(2):
                        dve.wait_ge(comb_turned, COMB_CREDIT + 2 * n + half + 1)
                        dve.tensor_copy(comb_t[t][:, 4 * half:4 * half + 4, :], turn_ps[0][:])\
                           .then_inc(comb_taken, 1)

                def disp_max_of(q):
                    n = QUARTERS * b + q
                    dve.wait_ge(disp_logits, n + 1)
                    dve.tensor_reduce(neg_max_d[q % 2][:], disp_ps[q % 2][:], AX.X, ALU.max, negate=True)\
                       .then_inc(disp_max, 1)

                def disp_divide(q):
                    n = QUARTERS * b + q
                    i = q % 2
                    dve.wait_ge(disp_exp, DISP_CREDIT + n + 1)
                    dve.reciprocal(inv_d[i][:], sum_d[i][:]).then_inc(inv_d_ready, 1)
                    dve.wait_ge(inv_d_ready, n + 1)
                    for j in range(2):
                        ins = dve.tensor_scalar(disp_t[i][:, j, :], disp_t[i][:, j, :], inv_d[i][:, j:j + 1],
                                                None, ALU.mult)
                    ins.then_inc(disp_ready, 1)

                comb_max_of(0)
                disp_max_of(0)
                comb_max_of(1)
                disp_max_of(1)
                if not last:
                    statistics(pair, s, 0)
                comb_take(0)
                disp_divide(0)
                disp_max_of(2)
                comb_take(1)
                if not last:
                    statistics(pair, s, 1)
                disp_divide(1)
                disp_max_of(3)
                disp_divide(2)
                disp_divide(3)

            statistics(-1, 1, 0)
            statistics(-1, 1, 1)
            pair_loop(dve, step)


def slot_experts(nc, tag, wg, wu, wd, bg, bu, bd, arena):
    W = KD * SLOT_HID
    PART = 3 * W // SF
    E = SLOT_EXPERTS
    assert W == SF * D and NS == 4 * P

    with ExitStack() as ctx:
        def sb(name, shape, dt=F32):
            return ctx.enter_context(nc.sbuf_tensor(f"{tag}_{name}", shape, dt))

        def pb(name, shape):
            return ctx.enter_context(nc.psum_tensor(f"{tag}_{name}", shape, F32))

        def sem(name):
            return ctx.enter_context(nc.semaphore(f"{tag}_{name}"))

        w_hi = [sb(f"w_hi{i}", [P, 3 * W], F32R) for i in range(2)]
        w_lo = [sb(f"w_lo{i}", [P, 3 * W], F32R) for i in range(2)]
        stage = [sb(f"stage{i}", [P, 3 * W]) for i in range(2)]
        bd_sb = [sb(f"bd{i}", [P, D]) for i in range(2)]
        bg_sb = sb("bg", [P, E, SF])
        bu_sb = sb("bu", [P, E, SF])
        xs_hi = [sb(f"xs_hi{i}", [P, RANGE], F32R) for i in range(2)]
        xs_lo = [sb(f"xs_lo{i}", [P, RANGE], F32R) for i in range(2)]
        gelu = [sb(f"gelu{i}", [P, NS]) for i in range(2)]
        prod = [sb(f"prod{i}", [P, NS]) for i in range(2)]
        h_hi = [sb(f"h_hi{i}", [P, NS], F32R) for i in range(2)]
        h_lo = [sb(f"h_lo{i}", [P, NS], F32R) for i in range(2)]
        tick = sb("tick", [P, 1])
        g_ps = [pb(f"g{i}", [P, NS]) for i in range(2)]
        u_ps = [pb(f"u{i}", [P, NS]) for i in range(2)]
        y_ps = [pb(f"y{i}", [P, 4, D]) for i in range(2)]

        biases_in = sem("biases_in")
        staged = [sem(f"staged{i}") for i in range(2)]
        w_hi_done = sem("w_hi_done")
        w_lo_done = sem("w_lo_done")
        x_hi_done = sem("x_hi_done")
        x_lo_done = sem("x_lo_done")
        gu_done = sem("gu_done")
        gelu_done = sem("gelu_done")
        prod_done = sem("prod_done")
        hi_done = sem("hi_done")
        lo_done = sem("lo_done")
        down_done = sem("down_done")
        y_taken = sem("y_taken")

        def slots_of(pair, s):
            return arena[:, bass.ds(pair, 1), s * RANGE:(s + 1) * RANGE].rearrange("p i c -> p (i c)")

        def expert_loop(eng, step):
            with eng.Fori(0, E // 2 - 1) as pair:
                step(pair, 0, False)
                step(pair, 1, False)
            step(E // 2 - 1, 0, False)
            step(E // 2 - 1, 1, True)

        block = ctx.enter_context(nc.Block())

        @block.sync
        def _(sp):
            sp.sem_inc(w_lo_done, 2 * SF)
            with sp.Fori(0, E // 2) as pair:
                for s in range(2):
                    e = 2 * pair + s
                    sp.wait_ge(w_lo_done, SF * e + SF)
                    for n, (w, parts) in enumerate(((wg, KD), (wu, KD), (wd, SF))):
                        dst = stage[s][:, n * W:(n + 1) * W].rearrange("p (k n) -> p k n", k=parts)
                        sp.dma_start(dst, w[e].rearrange("(k p) n -> p k n", p=P)).then_inc(staged[s], 16)
                    sp.wait_ge(y_taken, two_before(e))
                    sp.dma_start(bd_sb[s][:], bd[e].partition_broadcast(P)).then_inc(staged[s], 16)

        @block.gpsimd
        def _(pool):
            def split(pair, s):
                for f in range(SF):
                    part = slice(f * PART, (f + 1) * PART)
                    pool.wait_ge(w_hi_done, SF * (2 * pair + s) + f + 1)
                    pool.tensor_tensor(w_lo[s][:, part], stage[s][:, part], w_hi[s][:, part].bitcast(F32),
                                       ALU.subtract).then_inc(w_lo_done, 1)

            with pool.Fori(0, E // 2) as pair:
                split(pair, 0)
                split(pair, 1)

        @block.scalar
        def _(act):
            act.dma_start(bg_sb[:], bg).then_inc(biases_in, 16)
            act.dma_start(bu_sb[:], bu).then_inc(biases_in, 16)

            def split_weights(pair, s, f):
                o = 1 - s
                part = slice(f * PART, (f + 1) * PART)
                if f == 0:
                    act.wait_ge(staged[o], 64 * (pair + s + 1))
                    if not (isinstance(pair, int) and pair < 0):
                        act.wait_ge(down_done, CREDIT + SF * (2 * pair + s))
                act.activation(w_hi[o][:, part], stage[o][:, part], ACT.Copy).then_inc(w_hi_done, 1)

            def split_slots(pair, s):
                act.activation(xs_hi[1 - s][:], slots_of(pair + s, 1 - s), ACT.Copy).then_inc(x_hi_done, 1)

            def expert(pair, s, last):
                for f in range(SF):
                    n = (2 * pair + s) * SF + f
                    i = f % 2
                    act.wait_ge(prod_done, two_before(n))
                    act.wait_ge(gu_done, n + 1)
                    act.activation(gelu[i][:], g_ps[i][:], ACT.Gelu,
                                   bias=bg_sb[:, bass.ds(2 * pair + s, 1), f]).then_inc(gelu_done, 1)
                    act.wait_ge(down_done, two_before(n))
                    act.wait_ge(prod_done, nth(n))
                    act.activation(h_hi[i][:], prod[i][:], ACT.Copy).then_inc(hi_done, 1)
                    if not last:
                        split_weights(pair, s, f)
                        if f == 1:
                            split_slots(pair, s)

            for f in range(SF):
                split_weights(-1, 1, f)
            split_slots(-1, 1)
            act.wait_ge(biases_in, 32)
            expert_loop(act, expert)

        @block.tensor
        def _(pe):
            pe.sem_inc(down_done, CREDIT)

            def three_passes(out, a_hi, a_lo, b_hi, b_lo, start, stop):
                pe.matmul(out, a_hi, b_hi, start=start, stop=False, skip_group_check=True)
                pe.matmul(out, a_lo, b_hi, start=False, stop=False, skip_group_check=True)
                return pe.matmul(out, a_hi, b_lo, start=False, stop=stop, skip_group_check=True)

            def gate_up(pair, s, f):
                e = 2 * pair + s
                n = e * SF + f
                if f == 0:
                    pe.wait_ge(w_lo_done, 2 * SF + SF * e + SF)
                    pe.wait_ge(x_lo_done, e + 1)
                pe.wait_ge(prod_done, two_before(n))
                for ps, first in ((g_ps[f % 2], 0), (u_ps[f % 2], W)):
                    for k in range(KD):
                        a = slice(first + k * SLOT_HID + f * P, first + k * SLOT_HID + (f + 1) * P)
                        x = slice(k * NS, (k + 1) * NS)
                        ins = three_passes(ps[:], w_hi[s][:, a], w_lo[s][:, a], xs_hi[s][:, x], xs_lo[s][:, x],
                                           k == 0, k == KD - 1)
                ins.then_inc(gu_done, 1)

            def down(pair, s, f):
                e = 2 * pair + s
                n = e * SF + f
                i = f % 2
                if f == 0:
                    pe.wait_ge(y_taken, two_before(e))
                pe.wait_ge(lo_done, n + 1)
                for t in range(4):
                    a, c = slice(t * P, (t + 1) * P), slice(2 * W + f * D, 2 * W + (f + 1) * D)
                    ins = three_passes(y_ps[s][:, t, :], h_hi[i][:, a], h_lo[i][:, a], w_hi[s][:, c],
                                       w_lo[s][:, c], f == 0 and t % 2 == 0, f == SF - 1)
                ins.then_inc(down_done, 1)

            def expert(pair, s, last):
                for f in range(1, SF):
                    gate_up(pair, s, f)
                    down(pair, s, f - 1)
                if not last:
                    gate_up(pair + s, 1 - s, 0)
                down(pair, s, SF - 1)

            gate_up(0, 0, 0)
            expert_loop(pe, expert)

        @block.vector
        def _(dve):
            dve.sem_inc(prod_done, CREDIT)
            dve.sem_inc(y_taken, CREDIT)

            def split_slots(pair, s):
                o = 1 - s
                dve.wait_ge(x_hi_done, 2 * pair + s + 2)
                dve.tensor_tensor(xs_lo[o][:], slots_of(pair + s, o), xs_hi[o][:].bitcast(F32), ALU.subtract)\
                   .then_inc(x_lo_done, 1)

            def expert(pair, s, last):
                e = 2 * pair + s
                for f in range(SF):
                    n = e * SF + f
                    i = f % 2
                    dve.wait_ge(gelu_done, n + 1)
                    dve.scalar_tensor_tensor(prod[i][:], u_ps[i][:], bu_sb[:, bass.ds(e, 1), f], gelu[i][:],
                                             ALU.add, ALU.mult).then_inc(prod_done, 1)
                    dve.wait_ge(hi_done, n + 1)
                    dve.tensor_tensor(h_lo[i][:], prod[i][:], h_hi[i][:].bitcast(F32), ALU.subtract)\
                       .then_inc(lo_done, 1)
                    if f == 2 and not last:
                        split_slots(pair, s)
                dve.wait_ge(staged[s], 64 * (pair + 1))
                dve.wait_ge(down_done, nth(SF * e + SF - 1))
                for half in range(2):
                    rows = slice(half * SLOTS, (half + 1) * SLOTS)
                    dst = arena[rows, bass.ds(pair, 1), :].rearrange("p i (j r d) -> p (i j) r d", r=2, d=D)
                    ins = dve.tensor_tensor(dst[:, :, half ^ s, :], y_ps[s][rows, :, :],
                                            bd_sb[s][rows, :].unsqueeze(1).to_broadcast([SLOTS, 4, D]), ALU.add)
                ins.then_inc(y_taken, 1)

            dve.wait_ge(biases_in, 32)
            split_slots(-1, 1)
            expert_loop(dve, expert)


def combine_slots(nc, tag, x_in, comb_dram, inv_rows, arena, x_out):
    with ExitStack() as ctx:
        def sb(name, shape, dt=F32):
            return ctx.enter_context(nc.sbuf_tensor(f"{tag}_{name}", shape, dt))

        def sem(name):
            return ctx.enter_context(nc.semaphore(f"{tag}_{name}"))

        x_sb = [sb(f"x{i}", [P, NT, D]) for i in range(2)]
        xo_sb = [sb(f"xo{i}", [P, NT, D]) for i in range(2)]
        ct_sb = [sb(f"ct{i}", [P, ST, SEQ]) for i in range(2)]
        out_ps = [ctx.enter_context(nc.psum_tensor(f"{tag}_out{i}", [P, NT, D], F32)) for i in range(2)]

        loaded = [sem(f"loaded{i}") for i in range(2)]
        out_done = sem("out_done")
        xo_ready = sem("xo_ready")
        stored = [sem(f"stored{i}") for i in range(2)]

        x_dram = x_in.rearrange("b (t p) d -> b p t d", p=P)
        xo_dram = x_out.rearrange("b (t p) d -> b p t d", p=P)
        block = ctx.enter_context(nc.Block())

        def pairs(eng, step):
            with eng.Fori(0, BATCH // 2) as pair:
                step(pair, 0)
                step(pair, 1)

        @block.sync
        def _(sp):
            sp.sem_inc(stored[0], 16)
            sp.sem_inc(stored[1], 16)

            def load(pair, s):
                b = 2 * pair + s
                sp.wait_ge(out_done, two_before(b))
                sp.dma_start(ct_sb[s][:], comb_dram[b].rearrange("i s n -> s i n")).then_inc(loaded[s], 16)
                sp.wait_ge(xo_ready, two_before(b))
                sp.dma_start(x_sb[s][:], x_dram[b]).then_inc(loaded[s], 16)

            def store(pair, s):
                sp.wait_ge(xo_ready, nth(2 * pair + s))
                sp.dma_start(xo_dram[2 * pair + s], xo_sb[s][:]).then_inc(stored[s], 16)

            load(0, 0)
            load(0, 1)
            with sp.Fori(0, BATCH // 2 - 1) as pair:
                for s in range(2):
                    store(pair, s)
                    load(pair + 1, s)
            for s in range(2):
                store(BATCH // 2 - 1, s)
            for s in range(2):
                sp.wait_ge(stored[s], 16 * (BATCH // 2 + 1))

        @block.tensor
        def _(pe):
            pe.sem_inc(out_done, CREDIT)

            def step(pair, s):
                b = 2 * pair + s
                pe.wait_ge(loaded[s], 32 * (pair + 1))
                pe.wait_ge(xo_ready, two_before(b))
                for t in range(NT):
                    for i in range(ST):
                        ins = pe.matmul(out_ps[s][:, t, :], ct_sb[s][:, i, t * P:(t + 1) * P],
                                        arena[:, i, bass.ts(b, D)], start=(i == 0), stop=(i == ST - 1))
                ins.then_inc(out_done, 1)

            pairs(pe, step)

        @block.vector
        def _(dve):
            dve.sem_inc(xo_ready, CREDIT)

            def step(pair, s):
                b = 2 * pair + s
                dve.wait_ge(out_done, nth(b))
                dve.wait_ge(stored[s], 16 * (pair + 1))
                for t in range(NT):
                    ins = dve.scalar_tensor_tensor(xo_sb[s][:, t, :], out_ps[s][:, t, :],
                                                   inv_rows[:, bass.ds(NT * b + t, 1)], x_sb[s][:, t, :],
                                                   ALU.mult, ALU.add)
                ins.then_inc(xo_ready, 1)

            pairs(dve, step)


def slot_mixture(nc, tag, x_in, norm_g, norm_b, slot_g, slot_b, scale, slot_embeds, wg, bg, wu, bu, wd, bd,
                 x_out, ident_in):
    comb_dram = nc.dram_tensor(f"{tag}_comb", (BATCH, ST, P, SEQ), F32, kind="Internal").ap()
    with ExitStack() as ctx:
        arena = ctx.enter_context(nc.sbuf_tensor(f"{tag}_arena", [P, SLOT_EXPERTS // 2, PAIR_COLS], F32))
        inv_rows = ctx.enter_context(nc.sbuf_tensor(f"{tag}_inv_rows", [P, TILES], F32))
        with ExitStack() as inner:
            se_t = inner.enter_context(nc.sbuf_tensor(f"{tag}_se_t", [P, KD, ALL_SLOTS], F32))
            se_sw = inner.enter_context(nc.sbuf_tensor(f"{tag}_se_sw", [P, KD, ALL_SLOTS], F32))
            normalise_slots(nc, f"{tag}n", slot_embeds, slot_g, slot_b, scale, ident_in, se_t, se_sw)
            dispatch_tokens(nc, f"{tag}d", x_in, norm_g, norm_b, ident_in, se_t, se_sw, arena, inv_rows, comb_dram)
        slot_experts(nc, f"{tag}e", wg, wu, wd, bg, bu, bd, arena)
        combine_slots(nc, f"{tag}c", x_in, comb_dram, inv_rows, arena, x_out)


def two_layer_program(nc, a, out):
    hidden = [nc.dram_tensor(f"hidden{i}", (BATCH, SEQ, D), F32, kind="Internal").ap() for i in range(3)]
    cross_attention(nc, "l0", a["x"], a["ctx_t"], a["L0_xattn_Wq"], a["L0_xattn_Wk"], a["L0_xattn_Wv"],
                    a["L0_xattn_Wo"], a["L0_xattn_bo"], hidden[0], a["identity"], heads=8, head_dim=64)
    gated_experts(nc, "l0f", hidden[0], a["L0_ffn_w_gate"], a["L0_ffn_w_gate_up"], a["L0_ffn_w_down"],
                  hidden[1], a["identity"], a["expert_numbers"])
    cross_attention(nc, "l1", hidden[1], a["ctx_t"], a["l1_wq"], a["l1_wk"], a["l1_wv"],
                    a["L1_xattn_proj_w"], a["L1_xattn_proj_b"], hidden[2], a["identity"], heads=16, head_dim=16,
                    q_bias=a["l1_bq"], k_bias=a["l1_bk"], v_bias=a["l1_bv"])
    slot_mixture(nc, "l1f", hidden[2], a["L1_ffn_norm_g"], a["L1_ffn_norm_b"], a["L1_ffn_slot_g"],
                 a["L1_ffn_slot_b"], a["L1_ffn_scale"], a["L1_ffn_slot_embeds"], a["L1_ffn_Wg"], a["l1_bg"],
                 a["L1_ffn_Wu"], a["l1_bu"], a["L1_ffn_Wd"], a["L1_ffn_bd"], out, a["identity"])


def kernel(**inputs):
    import numpy as _np
    import concourse.bacc as _bacc
    from concourse import mybir as _mybir
    from concourse.bass_utils import run_bass_kernel_spmd as _run

    heads, head_dim, row_group = 16, 16, 32

    def spread_heads(w):
        out = _np.zeros((*w.shape[:-1], heads, row_group), w.dtype)
        out[..., :head_dim] = w.reshape(*w.shape[:-1], heads, head_dim)
        return out.reshape(*w.shape[:-1], heads * row_group)

    def column_tiles(b):
        return b.reshape(-1, P).T

    i = {k: _np.asarray(v) for k, v in inputs.items()}
    inner = heads * head_dim
    kv_w, kv_b = i["L1_xattn_kv_w"], i["L1_xattn_kv_b"]
    laid = {k: v for k, v in i.items() if k.startswith("L0_")}
    for name in ("L1_xattn_proj_w", "L1_xattn_proj_b", "L1_ffn_norm_g", "L1_ffn_norm_b", "L1_ffn_slot_g",
                 "L1_ffn_slot_b", "L1_ffn_scale", "L1_ffn_slot_embeds", "L1_ffn_Wg", "L1_ffn_Wu", "L1_ffn_Wd",
                 "L1_ffn_bd"):
        laid[name] = i[name]
    laid |= {
        "x": i["x"],
        "ctx_t": i["ctx_768"].transpose(0, 2, 1),
        "l1_wq": spread_heads(i["L1_xattn_q_w"]),
        "l1_wk": spread_heads(kv_w[:, :inner]),
        "l1_wv": kv_w[:, inner:],
        "l1_bq": column_tiles(spread_heads(i["L1_xattn_q_b"])),
        "l1_bk": column_tiles(spread_heads(kv_b[:inner])),
        "l1_bv": kv_b[inner:],
        "l1_bg": i["L1_ffn_bg"].reshape(SLOT_EXPERTS, SLOT_HID // P, P).transpose(2, 0, 1),
        "l1_bu": i["L1_ffn_bu"].reshape(SLOT_EXPERTS, SLOT_HID // P, P).transpose(2, 0, 1),
        "identity": _np.eye(P, dtype=_np.float32),
        "expert_numbers": _np.arange(EXPERTS, dtype=_np.float32),
    }

    nc = _bacc.Bacc("TRN2", target_bir_lowering=False, num_devices=1)
    arrays, args = {}, {}
    for name, value in laid.items():
        arrays[f"in_{name}"] = _np.ascontiguousarray(value)
        args[name] = nc.dram_tensor(f"in_{name}", value.shape, _mybir.dt.from_np(value.dtype),
                                    kind="ExternalInput").ap()
    out = nc.dram_tensor("out", (BATCH, SEQ, D), _mybir.dt.float32, kind="ExternalOutput").ap()
    two_layer_program(nc, args, out)
    return _run(nc, [arrays], core_ids=[0]).results[0]["out"]
```

```python
from contextlib import ExitStack

import concourse.bass as bass
from concourse import mybir

F32 = mybir.dt.float32
F32R = mybir.dt.float32r
I32 = mybir.dt.int32
U32 = mybir.dt.uint32
ALU = mybir.AluOpType
ACT = mybir.ActivationFunctionType
AX = mybir.AxisListType

P = 128
BATCH, SEQ, D = 8, 256, 256
CTX_D = 192
NT = SEQ // P
KD = D // P
CTX_K = (P, CTX_D - P)
LN_EPS = 1e-5
RSQRT_MAGIC = float(0x5F3759DF)
NEWTON = 3
CREDIT = 2


def nth(n):
    return n + 1 + CREDIT


def two_before(n):
    return n + 1



def pair_loop(eng, step, peel_first=False):
    if peel_first:
        step(0, 0, False)
        step(0, 1, False)
    with eng.Fori(1 if peel_first else 0, BATCH // 2 - 1) as pair:
        step(pair, 0, False)
        step(pair, 1, False)
    step(BATCH // 2 - 1, 0, False)
    step(BATCH // 2 - 1, 1, True)


NEWTON_STEPS = 4 * NEWTON


def newton_rsqrt(pool, step_done, base, y, half_v, tmp, three_halves):
    for n in range(NEWTON):
        pool.tensor_tensor(tmp, y, y, ALU.mult).then_inc(step_done, 1)
        pool.wait_ge(step_done, base + 4 * n + 1)
        pool.tensor_tensor(tmp, tmp, half_v, ALU.mult).then_inc(step_done, 1)
        pool.wait_ge(step_done, base + 4 * n + 2)
        pool.tensor_tensor(tmp, tmp, three_halves, ALU.add).then_inc(step_done, 1)
        pool.wait_ge(step_done, base + 4 * n + 3)
        pool.tensor_tensor(y, y, tmp, ALU.mult).then_inc(step_done, 1)
        pool.wait_ge(step_done, base + 4 * n + 4)


STATS_STEPS = 4


def row_stats(dve, step_done, base, x, stats, mean_var, half_v, seed_bits, seed):
    for t in range(x.shape[1]):
        ins = dve.bn_stats(stats[:, t, :], x[:, t, :])
    ins.then_inc(step_done, 1)
    dve.wait_ge(step_done, base + 1)
    dve.memset(half_v, 0.0)
    for t in range(x.shape[1]):
        ins = dve.bn_aggr(mean_var[:, t, :], stats[:, t, :])
    ins.then_inc(step_done, 1)
    dve.wait_ge(step_done, base + 2)
    dve.tensor_scalar(half_v, mean_var[:, :, 1], LN_EPS, None, ALU.add).then_inc(step_done, 1)
    dve.wait_ge(step_done, base + 3)
    dve.tensor_scalar(seed_bits, half_v.bitcast(I32), 1, None, ALU.logical_shift_right).then_inc(step_done, 1)
    dve.wait_ge(step_done, base + 4)
    dve.tensor_scalar(half_v, half_v, -0.5, None, ALU.mult)
    return dve.tensor_scalar(seed.bitcast(I32), seed_bits, -1.0, RSQRT_MAGIC, ALU.mult, ALU.add)


def cross_attention(nc, tag, x_in, ctx_t, wq, wk, wv, wo, out_bias, x_out, ident_in, heads, head_dim,
                    q_bias=None, k_bias=None, v_bias=None):
    H = heads
    HPT = H // 4
    R = P // HPT
    INNER = heads * head_dim
    SCALE = float(head_dim) ** -0.5
    biased = q_bias is not None
    PRO = 7
    SIDE = PRO + 1

    with ExitStack() as ctx:
        def sb(name, shape, dt=F32):
            return ctx.enter_context(nc.sbuf_tensor(f"{tag}_{name}", shape, dt))

        def pb(name, shape):
            return ctx.enter_context(nc.psum_tensor(f"{tag}_{name}", shape, F32))

        def sem(name):
            return ctx.enter_context(nc.semaphore(f"{tag}_{name}"))

        ident = sb("ident", [P, P])
        wq_sb = sb("wq", [P, KD, 4 * P])
        wk_sb = sb("wk", [P, 2, 4 * P])
        wv_sb = sb("wv", [P, 2, INNER])
        wo_sb = sb("wo", [P, 4, D])
        obias = sb("obias", [P, D])
        if biased:
            qb_sb = sb("qb", [P, 4])
            kb_sb = sb("kb", [P, 4])
            vb_sb = sb("vb", [P, INNER])
        x_sb = [sb(f"x{i}", [P, NT, D]) for i in range(2)]
        c_sb = [sb(f"c{i}", [P, 2, SEQ]) for i in range(2)]
        xb_sb = [sb(f"xb{i}", [P, NT, D]) for i in range(2)]
        xo_sb = [sb(f"xo{i}", [P, NT, D]) for i in range(2)]
        xn_sb = [sb(f"xn{i}", [P, NT, D]) for i in range(2)]
        xnt_sb = sb("xnt", [P, KD, SEQ])
        q_sb = [sb(f"q{i}", [P, 4, SEQ]) for i in range(2)]
        k_sb = [sb(f"k{i}", [P, 4, SEQ]) for i in range(2)]
        v_sb = [sb(f"v{i}", [P, 2, INNER]) for i in range(2)]
        prob = [sb(f"prob{i}", [P, NT, SEQ]) for i in range(2)]
        prob_t = [sb(f"probt{i}", [P, 2, SEQ]) for i in range(2)]
        neg_max = [sb(f"nmax{i}", [P, NT]) for i in range(2)]
        row_sum = [sb(f"rsum{i}", [P, NT]) for i in range(2)]
        inv_sum = [sb(f"inv{i}", [P, NT]) for i in range(2)]
        ot_sb = sb("ot", [P, 4, SEQ])
        stats = sb("stats", [P, NT, 6])
        mean_var = sb("mv", [P, NT, 2])
        half_v = sb("halfv", [P, NT])
        seed_bits = sb("seedb", [P, NT], I32)
        rstd = sb("rstd", [P, NT])
        nwt = sb("nwt", [P, NT])
        three_halves = sb("three_halves", [P, NT])

        score_ps = [pb(f"score{i}", [P, NT, SEQ]) for i in range(2)]
        trans_ps = [pb(f"trans{i}", [P, 2, SEQ]) for i in range(2)]
        out_ps = [pb(f"outp{i}", [P, 512]) for i in range(2)]
        side_ps = [pb(f"side{i}", [P, 512]) for i in range(2)]

        weights_in = sem("weights_in")
        x_loaded = [sem(f"x_loaded{i}") for i in range(2)]
        c_loaded = [sem(f"c_loaded{i}") for i in range(2)]
        constant_set = sem("constant_set")
        stats_step = sem("stats_step")
        seed_ready = sem("seed_ready")
        newton_step = sem("newton_step")
        xn_ready = sem("xn_ready")
        xn_turned = sem("xn_turned")
        c_used = sem("c_used")
        xb_ready = sem("xb_ready")
        side_full = [sem(f"side_full{i}") for i in range(2)]
        side_free = [sem(f"side_free{i}") for i in range(2)]
        qb_scaled = sem("qb_scaled")
        scores_done = sem("scores_done")
        max_done = sem("max_done")
        exp_done = sem("exp_done")
        turned = sem("turned")
        prob_t_ready = sem("prob_t_ready")
        pv_done = sem("pv_done")
        inv_ready = sem("inv_ready")
        prob_ready = sem("prob_ready")
        o_taken = sem("o_taken")
        xo_ready = sem("xo_ready")
        stored = [sem(f"stored{i}") for i in range(2)]

        x_dram = x_in.rearrange("b (t p) d -> b p t d", p=P)
        xo_dram = x_out.rearrange("b (t p) d -> b p t d", p=P)
        WEIGHTS = 16 * (8 + 3 * biased)

        TURNS = H + 4
        SIDE_AT = 4
        PROJECT_AT = 1
        assert SIDE_AT + PRO <= TURNS and SIDE % 2 == 0

        FREE_STEPS = [[j for j in range(SIDE - 1) if j % 2 == bank] for bank in range(2)]
        FULL_STEPS = [[j for j in range(SIDE) if j % 2 == bank and j not in (0, PRO - 1)] for bank in range(2)]

        def count(steps, b, j):
            skipped = sum(x < PRO for x in steps) if isinstance(b, int) and b == BATCH - 1 else 0
            return len(steps) * (b + 1) + steps.index(j) + 1 - skipped

        def full(b, j):
            if j == 0:
                return xn_turned, nth(b + 1)
            if j == PRO - 1:
                return c_used, nth(b + 1)
            return side_full[j % 2], count(FULL_STEPS[j % 2], b, j)

        def emptied(b, j):
            if j == SIDE - 1:
                return xo_ready, nth(b)
            return side_free[j % 2], count(FREE_STEPS[j % 2], b, j)

        def before(b, j):
            if isinstance(b, int) and b == BATCH - 1 and j == PRO:
                return emptied(b - 1, SIDE - 1)
            if j >= 2:
                return emptied(b, j - 2)
            return None if isinstance(b, int) and b < 0 else emptied(b - 1, SIDE - 2 + j)

        def ready(b, j):
            return side_free[j % 2], len(FREE_STEPS[j % 2]) * b + FREE_STEPS[j % 2].index(j) + 1

        def has_batch_before(pair, s):
            return not (isinstance(pair, int) and pair == 0 and s == 0)

        def batch_before(pair, s):
            return (pair, 0) if s else (pair - 1, 1)

        def head_rows(h):
            return h // HPT, slice((h % HPT) * R, (h % HPT) * R + head_dim)

        block = ctx.enter_context(nc.Block())

        @block.sync
        def _(sp):
            sp.sem_inc(stored[0], 16)
            sp.sem_inc(stored[1], 16)

            def load(pair, s):
                b = 2 * pair + s
                sp.wait_ge(xb_ready, two_before(b))
                sp.dma_start(x_sb[s][:], x_dram[b]).then_inc(x_loaded[s], 16)
                sp.wait_ge(c_used, two_before(b))
                for k, rows in enumerate(CTX_K):
                    sp.dma_start(c_sb[s][0:rows, k, :], ctx_t[b, k * P:k * P + rows, :]).then_inc(c_loaded[s], 16)

            def store(pair, s):
                sp.wait_ge(xo_ready, nth(2 * pair + s))
                sp.dma_start(xo_dram[2 * pair + s], xo_sb[s][:]).then_inc(stored[s], 16)

            load(0, 0)
            sp.dma_start(ident[:], ident_in).then_inc(weights_in, 16)
            sp.dma_start(wq_sb[:], wq.rearrange("(k p) n -> p k n", p=P)).then_inc(weights_in, 16)
            for k, rows in enumerate(CTX_K):
                sp.dma_start(wk_sb[0:rows, k, :], wk[k * P:k * P + rows, :]).then_inc(weights_in, 16)
                sp.dma_start(wv_sb[0:rows, k, :], wv[k * P:k * P + rows, :]).then_inc(weights_in, 16)
            sp.dma_start(wo_sb[:], wo.rearrange("(k p) n -> p k n", p=P)).then_inc(weights_in, 16)
            sp.dma_start(obias[:], out_bias.partition_broadcast(P)).then_inc(weights_in, 16)
            if biased:
                sp.dma_start(qb_sb[:], q_bias).then_inc(weights_in, 16)
                sp.dma_start(kb_sb[:], k_bias).then_inc(weights_in, 16)
                sp.dma_start(vb_sb[:], v_bias.partition_broadcast(P)).then_inc(weights_in, 16)
            load(0, 1)
            with sp.Fori(0, BATCH // 2 - 1) as pair:
                for s in range(2):
                    load(pair + 1, s)
                    store(pair, s)
            for s in range(2):
                store(BATCH // 2 - 1, s)
            for s in range(2):
                sp.wait_ge(stored[s], 16 * (BATCH // 2 + 1))

        @block.gpsimd
        def _(pool):
            pool.sem_inc(xb_ready, CREDIT)
            pool.memset(ot_sb[:], 0.0)
            pool.memset(three_halves[:], 1.5).then_inc(constant_set, 1)
            pool.wait_ge(constant_set, 1)
            pool.wait_ge(weights_in, WEIGHTS)

            def normalise(pair, s):
                b = 2 * pair + s
                pool.wait_ge(seed_ready, b + 1)
                newton_rsqrt(pool, newton_step, NEWTON_STEPS * b, rstd[:], half_v[:], nwt[:],
                             three_halves[:])
                pool.wait_ge(xn_turned, two_before(b))
                pool.wait_ge(xo_ready, two_before(b))
                pool.tensor_tensor(nwt[:], nwt[:], nwt[:], ALU.mult)
                for t in range(NT):
                    ins = pool.tensor_scalar(xn_sb[s][:, t, :], x_sb[s][:, t, :], mean_var[:, t, 0:1],
                                             rstd[:, t:t + 1], ALU.subtract, ALU.mult)
                ins.then_inc(xn_ready, 1)
                pool.tensor_tensor(xb_sb[s][:], x_sb[s][:], obias[:].unsqueeze(1).to_broadcast([P, NT, D]),
                                   ALU.add).then_inc(xb_ready, 1)

            with pool.Fori(0, BATCH // 2) as pair:
                normalise(pair, 0)
                normalise(pair, 1)

        @block.scalar
        def _(act):
            act.sem_inc(exp_done, CREDIT)
            act.sem_inc(o_taken, CREDIT)
            act.wait_ge(weights_in, WEIGHTS)

            def side(pair, s, j):
                b = 2 * pair + s
                bank = j % 2
                if j == 0:
                    act.wait_ge(*full(b, j))
                    act.activation(xnt_sb[:].rearrange("p k n -> p (k n)"), side_ps[bank][:], ACT.Copy)\
                       .then_inc(side_free[bank], 1)
                elif j in (1, 2):
                    act.wait_ge(*full(b, j))
                    q = q_sb[1 - s][:, 2 * (j - 1):2 * j, :]
                    if biased:
                        for n in range(2):
                            m = 2 * (j - 1) + n
                            ins = act.activation(q[:, n, :], side_ps[bank][:, n * SEQ:(n + 1) * SEQ],
                                                 ACT.Identity, bias=qb_sb[:, m:m + 1], scale=SCALE)
                    else:
                        ins = act.activation(q.rearrange("p k n -> p (k n)"), side_ps[bank][:], ACT.Copy,
                                             scale=SCALE)
                    ins.then_inc(side_free[bank], 1)

            def step(pair, s, last):
                b = 2 * pair + s
                for i in range(TURNS):
                    if i < H:
                        u = H * b + i
                        act.wait_ge(max_done, u + 1)
                        act.wait_ge(turned, two_before(u))
                        for t in range(NT):
                            ins = act.activation(prob[i % 2][:, t, :], score_ps[i % 2][:, t, :], ACT.Exp,
                                                 bias=neg_max[i % 2][:, t:t + 1],
                                                 accum_out=row_sum[i % 2][:, t:t + 1])
                        ins.then_inc(exp_done, 1)
                    if 0 <= i - SIDE_AT < PRO and not last:
                        side(pair, s, i - SIDE_AT)
                    if 0 <= i - 4 < H:
                        h = i - 4
                        m, rows = head_rows(h)
                        act.wait_ge(pv_done, nth(H * b + h))
                        act.activation(ot_sb[rows, m, :], out_ps[h % 2][rows, 0:SEQ], ACT.Copy)\
                           .then_inc(o_taken, 1)

            if biased:
                act.wait_ge(qb_scaled, 1)
            for j in range(PRO):
                side(-1, 1, j)
            act.wait_ge(constant_set, 1)
            pair_loop(act, step, peel_first=True)

        @block.tensor
        def _(pe):
            pe.sem_inc(c_used, CREDIT)
            pe.sem_inc(xn_turned, CREDIT)
            pe.sem_inc(turned, CREDIT)
            pe.sem_inc(pv_done, CREDIT)
            pe.wait_ge(weights_in, WEIGHTS)

            def side(pair, s, j):
                b = 2 * pair + s
                n, o = b + 1, 1 - s
                nth_of_slot = pair + s
                ps = side_ps[j % 2]
                if before(b, j) is not None:
                    pe.wait_ge(*before(b, j))
                if j == 0:
                    pe.wait_ge(xn_ready, n + 1)
                    for k in range(KD):
                        for t in range(NT):
                            ins = pe.transpose(ps[:, k * SEQ + t * P:k * SEQ + (t + 1) * P],
                                               xn_sb[o][:, t, k * P:(k + 1) * P], ident[:])
                elif j in (1, 2):
                    pe.wait_ge(*emptied(b, 0))
                    for m in range(2):
                        col = (2 * (j - 1) + m) * P
                        for k in range(KD):
                            ins = pe.matmul(ps[:, m * SEQ:(m + 1) * SEQ], wq_sb[:, k, col:col + P],
                                            xnt_sb[:, k, :], start=(k == 0), stop=(k == KD - 1))
                elif j in (3, 4):
                    pe.wait_ge(c_loaded[o], 32 * (nth_of_slot + 1))
                    for m in range(2):
                        col = (2 * (j - 3) + m) * P
                        for k, rows in enumerate(CTX_K):
                            ins = pe.matmul(ps[:, m * SEQ:(m + 1) * SEQ], wk_sb[0:rows, k, col:col + P],
                                            c_sb[o][0:rows, k, :], start=(k == 0), stop=(k == 1))
                elif j in (5, 6):
                    m = j - 5
                    for k, rows in enumerate(CTX_K):
                        ins = pe.matmul(ps[:, 0:INNER], c_sb[o][0:rows, k, m * P:(m + 1) * P],
                                        wv_sb[0:rows, k, :], start=(k == 0), stop=(k == 1))
                else:
                    pe.wait_ge(o_taken, nth(H * b + H - 1))
                    for t in range(NT):
                        for k in range(4):
                            ins = pe.matmul(ps[:, t * D:(t + 1) * D], ot_sb[:, k, t * P:(t + 1) * P],
                                            wo_sb[:, k, :], start=(k == 0), stop=(k == 3))
                ins.then_inc(full(b, j)[0], 1)

            def step(pair, s, last):
                b = 2 * pair + s
                for i in range(TURNS):
                    if i < H:
                        u = H * b + i
                        if i == 0:
                            for j in (3, 4):
                                pe.wait_ge(*ready(b, j))
                        pe.wait_ge(exp_done, two_before(u))
                        m, r = i // HPT, (i % HPT) * R
                        for t in range(NT):
                            ins = pe.matmul(score_ps[i % 2][:, t, :], q_sb[s][r:r + R, m, t * P:(t + 1) * P],
                                            k_sb[s][r:r + R, m, :], start=True, stop=True)
                        ins.then_inc(scores_done, 1)
                    if i == PROJECT_AT and has_batch_before(pair, s):
                        side(*batch_before(pair, s), PRO)
                    if 0 <= i - SIDE_AT < PRO and not last:
                        side(pair, s, i - SIDE_AT)
                    if 0 <= i - 2 < H:
                        h = i - 2
                        u = H * b + h
                        pe.wait_ge(prob_ready, u + 1)
                        pe.wait_ge(prob_t_ready, two_before(u))
                        for k in range(2):
                            for t in range(NT):
                                ins = pe.transpose(trans_ps[h % 2][:, k, t * P:(t + 1) * P],
                                                   prob[h % 2][:, t, k * P:(k + 1) * P], ident[:])
                        ins.then_inc(turned, 1)
                    if 0 <= i - 3 < H:
                        h = i - 3
                        u = H * b + h
                        _, rows = head_rows(h)
                        if h == 0:
                            for j in (5, 6):
                                pe.wait_ge(*ready(b, j))
                        pe.wait_ge(o_taken, two_before(u))
                        pe.wait_ge(prob_t_ready, nth(u))
                        for k in range(2):
                            ins = pe.matmul(out_ps[h % 2][rows, 0:SEQ],
                                            v_sb[s][:, k, h * head_dim:(h + 1) * head_dim],
                                            prob_t[h % 2][:, k, :], start=(k == 0), stop=(k == 1))
                        ins.then_inc(pv_done, 1)

            for j in range(PRO):
                side(-1, 1, j)
            pe.wait_ge(side_free[PRO % 2], len(FREE_STEPS[PRO % 2]))
            pe.sem_inc(side_full[PRO % 2], 1)
            pair_loop(pe, step, peel_first=True)
            side(BATCH // 2 - 1, 1, PRO)

        @block.vector
        def _(dve):
            dve.sem_inc(prob_t_ready, CREDIT)
            dve.sem_inc(xo_ready, CREDIT)
            dve.wait_ge(weights_in, WEIGHTS)
            if biased:
                dve.tensor_scalar(qb_sb[:], qb_sb[:], SCALE, None, ALU.mult).then_inc(qb_scaled, 1)

            def statistics(pair, s):
                n, o = 2 * pair + s + 1, 1 - s
                dve.wait_ge(x_loaded[o], 16 * (pair + s + 1))
                if not (isinstance(n, int) and n == 0):
                    dve.wait_ge(xn_ready, n)
                row_stats(dve, stats_step, STATS_STEPS * n, x_sb[o][:], stats[:], mean_var[:], half_v[:],
                          seed_bits[:], rstd[:]).then_inc(seed_ready, 1)

            def side(pair, s, j):
                b = 2 * pair + s
                o = 1 - s
                bank = j % 2
                ps = side_ps[bank]
                if j in (3, 4):
                    dve.wait_ge(*full(b, j))
                    k = k_sb[o][:, 2 * (j - 3):2 * (j - 3) + 2, :]
                    if biased:
                        for n in range(2):
                            m = 2 * (j - 3) + n
                            ins = dve.tensor_scalar(k[:, n, :], ps[:, n * SEQ:(n + 1) * SEQ],
                                                    kb_sb[:, m:m + 1], None, ALU.add)
                    else:
                        ins = dve.tensor_copy(k.rearrange("p k n -> p (k n)"), ps[:])
                    ins.then_inc(side_free[bank], 1)
                elif j in (5, 6):
                    dve.wait_ge(*full(b, j))
                    if biased:
                        ins = dve.tensor_tensor(v_sb[o][:, j - 5, :], ps[:, 0:INNER], vb_sb[:], ALU.add)
                    else:
                        ins = dve.tensor_copy(v_sb[o][:, j - 5, :], ps[:, 0:INNER])
                    ins.then_inc(side_free[bank], 1)
                elif j == SIDE - 1:
                    dve.wait_ge(*full(b, j))
                    dve.wait_ge(xb_ready, nth(b))
                    dve.wait_ge(stored[s], 16 * pair + 16)
                    dve.tensor_tensor(xo_sb[s][:].rearrange("p t d -> p (t d)"), ps[:],
                                      xb_sb[s][:].rearrange("p t d -> p (t d)"), ALU.add)\
                       .then_inc(xo_ready, 1)

            def step(pair, s, last):
                b = 2 * pair + s
                for i in range(TURNS):
                    if 0 <= i - 1 < H:
                        h = i - 1
                        u = H * b + h
                        dve.wait_ge(exp_done, nth(u))
                        dve.reciprocal(inv_sum[h % 2][:], row_sum[h % 2][:]).then_inc(inv_ready, 1)
                        dve.wait_ge(inv_ready, u + 1)
                        for t in range(NT):
                            ins = dve.tensor_scalar(prob[h % 2][:, t, :], prob[h % 2][:, t, :],
                                                    inv_sum[h % 2][:, t:t + 1], None, ALU.mult)
                        ins.then_inc(prob_ready, 1)
                    if i < H:
                        u = H * b + i
                        dve.wait_ge(scores_done, u + 1)
                        dve.tensor_reduce(neg_max[i % 2][:], score_ps[i % 2][:], AX.X, ALU.max, negate=True)\
                           .then_inc(max_done, 1)
                    if i == 0 and not last:
                        statistics(pair, s)
                    if i == PROJECT_AT and has_batch_before(pair, s):
                        side(*batch_before(pair, s), PRO)
                    if 0 <= i - SIDE_AT < PRO and not last:
                        side(pair, s, i - SIDE_AT)
                    if 0 <= i - 2 < H:
                        h = i - 2
                        u = H * b + h
                        dve.wait_ge(turned, nth(u))
                        dve.wait_ge(pv_done, two_before(u))
                        dve.tensor_copy(prob_t[h % 2][:], trans_ps[h % 2][:]).then_inc(prob_t_ready, 1)

            statistics(-1, 1)
            for j in range(PRO):
                side(-1, 1, j)
            pair_loop(dve, step, peel_first=True)
            side(BATCH // 2 - 1, 1, PRO)

EXPERTS, HID = 8, 1024
CHOICES = 2
TILES = BATCH * NT
TOKENS = TILES * P
DENOM_MIN = 1e-9
ROW_TILES = (CHOICES * TOKENS + CHOICES * (P - 1) + (EXPERTS - CHOICES) * P) // P


def routed_experts(nc, tag, x_in, w_gate, w_gate_up, w_down, x_out, ident_in, iota_in, tiles_in, below_in,
                   before_in):
    FT = HID // P
    HH = HID // 2
    PIECE = 2 * HID
    PIECES = KD + 1
    SLOT = PIECES * PIECE
    T = ROW_TILES
    GROUPS = TILES // 2
    assert FT * D == PIECE and T % 2 == 1

    with ExitStack() as ctx:
        def sb(name, shape, dt=F32):
            return ctx.enter_context(nc.sbuf_tensor(f"{tag}_{name}", shape, dt))

        def pb(name, shape):
            return ctx.enter_context(nc.psum_tensor(f"{tag}_{name}", shape, F32))

        def sem(name):
            return ctx.enter_context(nc.semaphore(f"{tag}_{name}"))

        sorted_x = nc.dram_tensor(f"{tag}_sorted_x", (T * P, D), F32, kind="Internal").ap()
        sorted_y = nc.dram_tensor(f"{tag}_sorted_y", (T * P, D), F32, kind="Internal").ap()

        ident = sb("ident", [P, P])
        below = sb("below", [P, P])
        ones = sb("ones", [P, P])
        zeros = sb("zeros", [P, D])
        iota = sb("iota", [P, EXPERTS])
        tile_no = sb("tile_no", [1, T])
        before = sb("before", [P, EXPERTS, EXPERTS])
        wg_sb = sb("wg", [P, KD, EXPERTS])
        x_sb = sb("x", [P, TILES, D])
        xn_sb = sb("xn", [P, TILES, D])
        xt_sb = [sb(f"xt{i}", [P, 2, KD, P]) for i in range(2)]
        stats = sb("stats", [P, TILES, 6])
        mean_var = sb("mv", [P, TILES, 2])
        half_v = sb("halfv", [P, TILES])
        seed_bits = sb("seedb", [P, TILES], I32)
        rstd = sb("rstd", [P, TILES])
        nwt = sb("nwt", [P, TILES])
        three_halves = sb("three_halves", [P, TILES])
        ex = sb("ex", [P, TILES, EXPERTS])
        left = sb("left", [P, TILES, EXPERTS])
        mask = [sb(f"mask{i}", [P, TILES, EXPERTS]) for i in range(CHOICES)]
        both = sb("both", [P, TILES, EXPERTS])
        cand = sb("cand", [P, TILES, EXPERTS])
        place = sb("place", [P, TILES, EXPERTS])
        red = sb("red", [P, TILES])
        gate = [sb(f"gate{i}", [P, TILES]) for i in range(CHOICES)]
        row_no = [sb(f"row{i}", [P, TILES], U32) for i in range(CHOICES)]
        own_count = sb("own_count", [P, EXPERTS])
        count_i = sb("count_i", [P, EXPERTS], I32)
        count_f = sb("count_f", [P, EXPERTS])
        earlier = sb("earlier", [P, EXPERTS, EXPERTS])
        start = sb("start", [P, EXPERTS])
        start_row = sb("start_row", [P, EXPERTS])
        start_halves = sb("start_halves", [1, EXPERTS], I32)
        begun = sb("begun", [1, T, EXPERTS])
        begun_count = sb("begun_count", [1, T])
        begun_i = sb("begun_i", [1, T], I32)
        tile_pieces = sb("tile_pieces", [1, T], I32)
        tile_slot = sb("tile_slot", [1, T], I32)

        w_hi = sb("w_hi", [P, 2 * SLOT], F32R)
        w_lo = sb("w_lo", [P, 2 * SLOT], F32R)
        stage = [sb(f"stage{i}", [P, PIECE]) for i in range(2)]
        row_sb = [sb(f"rows{i}", [P, D]) for i in range(2)]
        rt_hi = [sb(f"rt_hi{i}", [P, KD, P], F32R) for i in range(2)]
        rt_lo = [sb(f"rt_lo{i}", [P, KD, P], F32R) for i in range(2)]
        silu = [sb(f"silu{i}", [P, HH]) for i in range(2)]
        prod = [sb(f"prod{i}", [P, HH]) for i in range(2)]
        ht_hi = [sb(f"ht_hi{i}", [P, HH // P, P], F32R) for i in range(2)]
        ht_lo = [sb(f"ht_lo{i}", [P, HH // P, P], F32R) for i in range(2)]
        y_sb = [sb(f"y{i}", [P, D]) for i in range(2)]
        back = [[sb(f"back{i}{c}", [P, D]) for c in range(CHOICES)] for i in range(2)]
        tick = sb("tick", [P, 1])

        g_ps = [pb(f"g{i}", [P, HH]) for i in range(2)]
        u_ps = [pb(f"u{i}", [P, HH]) for i in range(2)]
        ht_ps = [pb(f"ht{i}", [P, HH // P, P]) for i in range(2)]
        y_ps = pb("yp", [P, 512])
        rt_ps = pb("rt", [P, KD, P])

        constants_in = sem("constants_in")
        x_loaded = sem("x_loaded")
        pool_set = sem("pool_set")
        zeroed = sem("zeroed")
        stats_step = sem("stats_step")
        newton_step = sem("newton_step")
        xn_ready = sem("xn_ready")
        turned = sem("turned")
        xt_copied = sem("xt_copied")
        logits_done = sem("logits_done")
        gate_step = sem("gate_step")
        chosen = sem("chosen")
        ranked = sem("ranked")
        tables_ready = sem("tables_ready")
        scattered = sem("scattered")
        staged = [sem(f"staged{i}") for i in range(2)]
        split_hi = sem("split_hi")
        split_done = sem("split_done")
        rows_in = [sem(f"rows_in{i}") for i in range(2)]
        rows_turned = sem("rows_turned")
        rt_hi_done = sem("rt_hi_done")
        rt_lo_done = sem("rt_lo_done")
        gu_done = sem("gu_done")
        silu_done = sem("silu_done")
        prod_done = sem("prod_done")
        h_turned = sem("h_turned")
        ht_hi_done = sem("ht_hi_done")
        ht_lo_done = sem("ht_lo_done")
        down_done = sem("down_done")
        y_copied = sem("y_copied")
        y_stored = [sem(f"y_stored{i}") for i in range(2)]
        gathered = [sem(f"gathered{i}") for i in range(2)]
        added = sem("added")
        stored = sem("stored")

        CONSTANTS = 16 * 6
        x_dram = x_in.rearrange("b (t p) d -> p (b t) d", p=P)
        xo_dram = x_out.rearrange("b (t p) d -> p (b t) d", p=P)
        trans_banks = [g_ps[0], g_ps[1], u_ps[0], u_ps[1]]

        block = ctx.enter_context(nc.Block())

        def tile_loop(eng, step):
            step(0, 0, 0)
            with eng.Fori(0, (T - 3) // 2) as pair:
                step(2 * pair + 1, 1, pair)
                step(2 * pair + 2, 0, pair + 1)
            step(T - 2, (T - 2) % 2, (T - 2) // 2)
            step(T - 1, (T - 1) % 2, (T - 1) // 2)

        def is_tile(i, n):
            return isinstance(i, int) and i == n

        @block.sync
        def _(sp):
            sp.dma_start(x_sb[:], x_dram).then_inc(x_loaded, 16)
            sp.dma_start(ident[:], ident_in).then_inc(constants_in, 16)
            sp.dma_start(below[:], below_in).then_inc(constants_in, 16)
            sp.dma_start(iota[:], iota_in.partition_broadcast(P)).then_inc(constants_in, 16)
            sp.dma_start(tile_no[:], tiles_in.unsqueeze(0)).then_inc(constants_in, 16)
            sp.dma_start(before[:].rearrange("p a b -> p (a b)"), before_in.partition_broadcast(P))\
              .then_inc(constants_in, 16)
            sp.dma_start(wg_sb[:], w_gate.rearrange("(k p) e -> p k e", p=P)).then_inc(constants_in, 16)
            sp.wait_ge(pool_set, 1)
            sp.dma_start(sorted_x.rearrange("(t p) d -> p t d", p=P),
                         zeros[:].unsqueeze(1).to_broadcast([P, T, D])).then_inc(zeroed, 16)
            sp.sem_inc(y_stored[0], 16)
            sp.sem_inc(y_stored[1], 16)

            def load(i, par):
                sp.dma_start(row_sb[par][:], sorted_x[bass.ts(i, P), :]).then_inc(rows_in[par], 16)

            def store(i, par):
                sp.wait_ge(y_copied, i + 1)
                sp.dma_start(sorted_y[bass.ts(i, P), :], y_sb[par][:]).then_inc(y_stored[par], 16)

            def step(i, par, half):
                if not (isinstance(i, int) and i > T - 3):
                    sp.wait_ge(rows_turned, i + 1)
                    load(i + 2, par)
                if not is_tile(i, 0):
                    store(i - 1, 1 - par)

            sp.wait_ge(scattered, 16 * CHOICES * TILES)
            load(0, 0)
            load(1, 1)
            tile_loop(sp, step)
            store(T - 1, (T - 1) % 2)
            for t in range(GROUPS):
                sp.wait_ge(added, 2 * t + 2)
                sp.dma_start(xo_dram[:, 2 * t:2 * t + 2, :], x_sb[:, 2 * t:2 * t + 2, :]).then_inc(stored, 16)
            sp.wait_ge(stored, 16 * GROUPS)

        @block.gpsimd
        def _(pool):
            pool.memset(zeros[:], 0.0).then_inc(pool_set, 1)
            pool.memset(ones[:], 1.0)
            pool.memset(tick[:], 0.0)
            pool.memset(three_halves[:], 1.5).then_inc(pool_set, 1)

            def load_piece(e, i, slot):
                if i < KD:
                    pool.dma_start(stage[slot][:], w_gate_up[e, i * P:(i + 1) * P, :]).then_inc(staged[slot], 16)
                else:
                    pool.dma_start(stage[slot][:].rearrange("p (f d) -> p f d", d=D),
                                   w_down[e].rearrange("(f p) d -> p f d", p=P)).then_inc(staged[slot], 16)

            def split(pair, s, last=False):
                e = 2 * pair + s
                for i in range(PIECES):
                    n = e * PIECES + i
                    slot = (s * PIECES + i) % 2
                    cols = slice(s * SLOT + i * PIECE, s * SLOT + (i + 1) * PIECE)
                    pool.wait_ge(staged[slot], 16 * (PIECES * pair + (s * PIECES + i) // 2 + 1))
                    pool.tensor_tensor(tick[:], tick[:], tick[:], ALU.mult)
                    pool.tensor_copy(w_hi[:, cols], stage[slot][:]).then_inc(split_hi, 1)
                    pool.wait_ge(split_hi, n + 1)
                    pool.tensor_tensor(w_lo[:, cols], stage[slot][:], w_hi[:, cols].bitcast(F32),
                                       ALU.subtract).then_inc(split_done, 1)
                    if not (last and i + 2 >= PIECES):
                        pool.wait_ge(split_done, n + 1)
                        load_piece(e + (i + 2) // PIECES, (i + 2) % PIECES, slot)

            def slot_free(e):
                halves = pool.value_load(start_halves[0:1, bass.ds(e - 1, 1)], min_val=2, max_val=2 * T)
                pool.wait_ge(down_done, halves)

            load_piece(0, 0, 0)
            load_piece(0, 1, 1)
            pool.wait_ge(pool_set, 2)
            pool.wait_ge(stats_step, STATS_STEPS + 1)
            newton_rsqrt(pool, newton_step, 0, rstd[:], half_v[:], nwt[:], three_halves[:])
            split(0, 0)
            pool.wait_ge(zeroed, 16)
            pool.wait_ge(xn_ready, GROUPS)
            pool.wait_ge(tables_ready, 1)
            for t in range(TILES):
                for c in range(CHOICES):
                    pool.indirect_dma_start(sorted_x, bass.IndirectOffsetOnAxis(row_no[c][:, t:t + 1], 0),
                                            xn_sb[:, t, :], None).then_inc(scattered, 16)
            split(0, 1)
            pool.wait_ge(tables_ready, 2)
            with pool.Fori(1, EXPERTS // 2 - 1) as pair:
                for s in range(2):
                    slot_free(2 * pair + s)
                    split(pair, s)
            for s in range(2):
                slot_free(EXPERTS - 2 + s)
                split(EXPERTS // 2 - 1, s, last=(s == 1))
            for par in range(2):
                pool.wait_ge(y_stored[par], 16 * ((T + 1 - par) // 2 + 1))
            for t in range(TILES):
                if t >= 2:
                    pool.wait_ge(added, t - 1)
                for c in range(CHOICES):
                    pool.indirect_dma_start(back[t % 2][c][:], None, sorted_y,
                                            bass.IndirectOffsetOnAxis(row_no[c][:, t:t + 1], 0))\
                        .then_inc(gathered[t % 2], 16)

        @block.scalar
        def _(act):
            for j in range(GROUPS):
                act.wait_ge(turned, j + 1)
                if j >= 2:
                    act.wait_ge(logits_done, j - 1)
                act.activation(xt_sb[j % 2][:].rearrange("p t k n -> p (t k n)"), trans_banks[j % 4][:], ACT.Copy)\
                   .then_inc(xt_copied, 1)
            act.wait_ge(gate_step, 2)
            act.activation(ex[:], ex[:], ACT.Exp).then_inc(xt_copied, 1)

            def split_rows(i, par):
                act.wait_ge(rows_turned, i + 1)
                if not (isinstance(i, int) and i < 2):
                    act.wait_ge(gu_done, 2 * i - 2)
                act.activation(rt_hi[par][:], rt_ps[:], ACT.Copy).then_inc(rt_hi_done, 1)

            def split_hidden(i, h):
                act.wait_ge(h_turned, 2 * i + h + 1)
                act.activation(ht_hi[h][:], ht_ps[h][:], ACT.Copy).then_inc(ht_hi_done, 1)

            def take_output(i, par, half):
                act.wait_ge(down_done, 2 * i + 2)
                act.wait_ge(y_stored[par], 16 * (half + 1))
                act.activation(y_sb[par][:], y_ps[:, 0:D], ACT.Copy).then_inc(y_copied, 1)

            def gate_half(i, h):
                act.wait_ge(gu_done, 2 * i + h + 1)
                if not is_tile(i, 0):
                    act.wait_ge(prod_done, 2 * i + h - 1)
                act.activation(silu[h][:], g_ps[h][:], ACT.Silu).then_inc(silu_done, 1)

            def step(i, par, half):
                gate_half(i, 0)
                if not is_tile(i, T - 1):
                    split_rows(i + 1, 1 - par)
                if not is_tile(i, 0):
                    split_hidden(i - 1, 1)
                gate_half(i, 1)
                split_hidden(i, 0)
                if not is_tile(i, 0):
                    take_output(i - 1, 1 - par, half - 1 + par)

            split_rows(0, 0)
            tile_loop(act, step)
            split_hidden(T - 1, 1)
            take_output(T - 1, (T - 1) % 2, (T - 1) // 2)

        @block.tensor
        def _(pe):
            def three_passes(out, a_hi, a_lo, b_hi, b_lo, start, stop):
                pe.matmul(out, a_hi, b_hi, start=start, stop=False)
                pe.matmul(out, a_lo, b_hi, start=False, stop=False)
                return pe.matmul(out, a_hi, b_lo, start=False, stop=stop)

            pe.wait_ge(constants_in, CONSTANTS)
            pe.wait_ge(pool_set, 2)

            def logits(j):
                pe.wait_ge(xt_copied, j + 1)
                for t in range(2):
                    tile = 2 * j + t
                    for k in range(KD):
                        ins = pe.matmul(y_ps[:, tile * EXPERTS:(tile + 1) * EXPERTS], xt_sb[j % 2][:, t, k, :],
                                        wg_sb[:, k, :], start=(k == 0), stop=(k == KD - 1))
                ins.then_inc(logits_done, 1)

            for j in range(GROUPS):
                pe.wait_ge(xn_ready, j + 1)
                if j >= 4:
                    pe.wait_ge(xt_copied, j - 3)
                bank = trans_banks[j % 4]
                for t in range(2):
                    for k in range(KD):
                        first = (t * KD + k) * P
                        ins = pe.transpose(bank[:, first:first + P], xn_sb[:, 2 * j + t, k * P:(k + 1) * P],
                                           ident[:])
                ins.then_inc(turned, 1)
                if j >= 1:
                    logits(j - 1)
            logits(GROUPS - 1)

            rank = ht_ps[0][:].rearrange("p a b -> p (a b)")
            flat = both[:].rearrange("p t e -> p (t e)")
            pe.wait_ge(chosen, 1)
            pe.matmul(rank[:, 0:TILES * EXPERTS], below[:], flat, start=True, stop=False, skip_group_check=True)
            for back_by in range(1, TILES):
                ins = pe.matmul(rank[:, back_by * EXPERTS:TILES * EXPERTS], ones[:],
                                flat[:, 0:(TILES - back_by) * EXPERTS], start=False, stop=(back_by == TILES - 1),
                                skip_group_check=True)
            pe.wait_ge(chosen, 2)
            pe.matmul(ht_ps[1][:, 0, 0:EXPERTS], ones[:], own_count[:], start=True, stop=True)\
              .then_inc(ranked, 1)
            pe.wait_ge(tables_ready, 2)

            def first_column(i):
                return pe.value_load(tile_slot[0:1, bass.ds(i, 1)], min_val=0, max_val=SLOT)

            def turn_rows(i, par, half):
                pe.wait_ge(rows_in[par], 16 * (half + 1))
                if not is_tile(i, 0):
                    pe.wait_ge(rt_lo_done, i)
                for k in range(KD):
                    ins = pe.transpose(rt_ps[:, k, :], row_sb[par][:, k * P:(k + 1) * P], ident[:])
                ins.then_inc(rows_turned, 1)

            def gate_up(i, par, h, w):
                if h == 0:
                    pieces = pe.value_load(tile_pieces[0:1, bass.ds(i, 1)], min_val=PIECES,
                                           max_val=PIECES * EXPERTS)
                    pe.wait_ge(rt_lo_done, i + 1)
                    pe.wait_ge(split_done, pieces)
                if not is_tile(i, 0):
                    pe.wait_ge(prod_done, 2 * i + h - 1)
                for ps, first in ((g_ps[h], h * HH), (u_ps[h], HID + h * HH)):
                    for k in range(KD):
                        cols = bass.ds(w + (k * PIECE + first), HH)
                        ins = three_passes(ps[:], rt_hi[par][:, k, :], rt_lo[par][:, k, :], w_hi[:, cols],
                                           w_lo[:, cols], k == 0, k == KD - 1)
                ins.then_inc(gu_done, 1)

            def turn_hidden(i, h):
                pe.wait_ge(prod_done, 2 * i + h + 1)
                if not is_tile(i, 0):
                    pe.wait_ge(ht_lo_done, 2 * i + h - 1)
                for f in range(HH // P):
                    ins = pe.transpose(ht_ps[h][:, f, :], prod[h][:, f * P:(f + 1) * P], ident[:])
                ins.then_inc(h_turned, 1)

            def down(i, h, w):
                pe.wait_ge(ht_lo_done, 2 * i + h + 1)
                if h == 0 and not is_tile(i, 0):
                    pe.wait_ge(y_copied, i)
                for f in range(HH // P):
                    cols = bass.ds(w + (KD * PIECE + (h * HH // P + f) * D), D)
                    ins = three_passes(y_ps[:, 0:D], ht_hi[h][:, f, :], ht_lo[h][:, f, :], w_hi[:, cols],
                                       w_lo[:, cols], h == 0 and f == 0, h == 1 and f == HH // P - 1)
                ins.then_inc(down_done, 1)

            def step(i, par, half):
                w = first_column(i)
                gate_up(i, par, 0, w)
                if not is_tile(i, T - 1):
                    turn_rows(i + 1, 1 - par, half + par)
                if not is_tile(i, 0):
                    w_before = first_column(i - 1)
                    turn_hidden(i - 1, 1)
                    down(i - 1, 0, w_before)
                gate_up(i, par, 1, w)
                turn_hidden(i, 0)
                if not is_tile(i, 0):
                    down(i - 1, 1, w_before)

            turn_rows(0, 0, 0)
            tile_loop(pe, step)
            w_last = first_column(T - 1)
            turn_hidden(T - 1, 1)
            down(T - 1, 0, w_last)
            down(T - 1, 1, w_last)

        @block.vector
        def _(dve):
            dve.wait_ge(x_loaded, 16)
            row_stats(dve, stats_step, 0, x_sb[:], stats[:], mean_var[:], half_v[:], seed_bits[:],
                      rstd[:]).then_inc(stats_step, 1)
            dve.wait_ge(newton_step, NEWTON_STEPS)
            for t in range(TILES):
                ins = dve.tensor_scalar(xn_sb[:, t, :], x_sb[:, t, :], mean_var[:, t, 0:1],
                                        rstd[:, t:t + 1], ALU.subtract, ALU.mult)
                if t % 2 == 1:
                    ins.then_inc(xn_ready, 1)

            def wide(ap):
                return ap.unsqueeze(2).to_broadcast([P, TILES, EXPERTS])

            def by_expert(ap):
                return ap.unsqueeze(1).to_broadcast([P, TILES, EXPERTS])

            iota_w = by_expert(iota[:])
            logits = y_ps[:, 0:TILES * EXPERTS].rearrange("p (t e) -> p t e", e=EXPERTS)
            dve.wait_ge(constants_in, CONSTANTS)
            dve.wait_ge(logits_done, GROUPS)
            dve.tensor_reduce(red[:], logits, AX.X, ALU.max).then_inc(gate_step, 1)
            dve.wait_ge(gate_step, 1)
            dve.tensor_tensor(ex[:], logits, wide(red[:]), ALU.subtract).then_inc(gate_step, 1)
            dve.wait_ge(xt_copied, GROUPS + 1)
            dve.tensor_reduce(red[:], ex[:], AX.X, ALU.add).then_inc(gate_step, 1)
            dve.wait_ge(gate_step, 3)
            dve.reciprocal(red[:], red[:]).then_inc(gate_step, 1)
            dve.wait_ge(gate_step, 4)
            dve.tensor_tensor(ex[:], ex[:], wide(red[:]), ALU.mult).then_inc(gate_step, 1)
            dve.wait_ge(gate_step, 5)
            dve.tensor_copy(left[:], ex[:]).then_inc(gate_step, 1)
            dve.wait_ge(gate_step, 6)
            at = 6
            for m in mask:
                dve.tensor_reduce(red[:], left[:], AX.X, ALU.max).then_inc(gate_step, 1)
                dve.wait_ge(gate_step, at + 1)
                dve.tensor_tensor(cand[:], left[:], wide(red[:]), ALU.is_lt).then_inc(gate_step, 1)
                dve.wait_ge(gate_step, at + 2)
                dve.scalar_tensor_tensor(cand[:], cand[:], float(EXPERTS), iota_w, ALU.mult, ALU.add)\
                   .then_inc(gate_step, 1)
                dve.wait_ge(gate_step, at + 3)
                dve.tensor_reduce(red[:], cand[:], AX.X, ALU.min).then_inc(gate_step, 1)
                dve.wait_ge(gate_step, at + 4)
                dve.tensor_tensor(m[:], iota_w, wide(red[:]), ALU.is_equal).then_inc(gate_step, 1)
                dve.wait_ge(gate_step, at + 5)
                dve.scalar_tensor_tensor(left[:], m[:], -2.0, left[:], ALU.mult, ALU.add)\
                   .then_inc(gate_step, 1)
                dve.wait_ge(gate_step, at + 6)
                at += 6
            dve.tensor_tensor(both[:], mask[0][:], mask[1][:], ALU.add).then_inc(chosen, 1)
            dve.wait_ge(chosen, 1)
            dve.tensor_reduce(own_count[:], both[:].rearrange("p t e -> p e t"), AX.X, ALU.add)\
               .then_inc(chosen, 1)
            dve.tensor_tensor(cand[:], ex[:], mask[0][:], ALU.mult)
            dve.tensor_tensor(left[:], ex[:], mask[1][:], ALU.mult).then_inc(gate_step, 1)
            dve.wait_ge(gate_step, at + 1)
            dve.tensor_reduce(gate[0][:], cand[:], AX.X, ALU.add)
            dve.tensor_reduce(gate[1][:], left[:], AX.X, ALU.add).then_inc(gate_step, 1)
            dve.wait_ge(gate_step, at + 2)
            dve.tensor_tensor(red[:], gate[0][:], gate[1][:], ALU.add).then_inc(gate_step, 1)
            dve.wait_ge(gate_step, at + 3)
            dve.tensor_scalar(red[:], red[:], DENOM_MIN, None, ALU.max).then_inc(gate_step, 1)
            dve.wait_ge(gate_step, at + 4)
            dve.reciprocal(red[:], red[:]).then_inc(gate_step, 1)
            dve.wait_ge(gate_step, at + 5)
            dve.tensor_tensor(gate[0][:], gate[0][:], red[:], ALU.mult)
            dve.tensor_tensor(gate[1][:], gate[1][:], red[:], ALU.mult).then_inc(gate_step, 1)
            at += 6
            dve.wait_ge(ranked, 1)
            dve.tensor_scalar(count_i[:], ht_ps[1][:, 0, 0:EXPERTS], float(P - 1), None, ALU.add)\
               .then_inc(gate_step, 1)
            dve.wait_ge(gate_step, at + 1)
            dve.tensor_scalar(count_i[:], count_i[:], P.bit_length() - 1, None, ALU.logical_shift_right)\
               .then_inc(gate_step, 1)
            dve.wait_ge(gate_step, at + 2)
            dve.tensor_copy(count_f[:], count_i[:]).then_inc(gate_step, 1)
            dve.wait_ge(gate_step, at + 3)
            dve.tensor_scalar(count_f[:], count_f[:], 1.0, None, ALU.max).then_inc(gate_step, 1)
            dve.wait_ge(gate_step, at + 4)
            dve.tensor_tensor(earlier[:], before[:], count_f[:].unsqueeze(1).to_broadcast([P, EXPERTS, EXPERTS]),
                              ALU.mult).then_inc(gate_step, 1)
            dve.wait_ge(gate_step, at + 5)
            dve.tensor_reduce(start[:], earlier[:], AX.X, ALU.add).then_inc(gate_step, 1)
            dve.wait_ge(gate_step, at + 6)
            dve.tensor_scalar(start_row[:], start[:], float(P), None, ALU.mult).then_inc(gate_step, 1)
            dve.wait_ge(gate_step, at + 7)
            rank = ht_ps[0][:].rearrange("p a b -> p (a b)")[:, 0:TILES * EXPERTS]
            dve.tensor_tensor(place[:], rank.rearrange("p (t e) -> p t e", e=EXPERTS), by_expert(start_row[:]),
                              ALU.add).then_inc(gate_step, 1)
            dve.wait_ge(gate_step, at + 8)
            dve.tensor_tensor(cand[:], place[:], mask[0][:], ALU.mult)
            dve.tensor_tensor(left[:], place[:], mask[1][:], ALU.mult).then_inc(gate_step, 1)
            dve.wait_ge(gate_step, at + 9)
            dve.tensor_reduce(red[:], cand[:], AX.X, ALU.add)
            dve.tensor_reduce(nwt[:], left[:], AX.X, ALU.add).then_inc(gate_step, 1)
            dve.wait_ge(gate_step, at + 10)
            dve.tensor_copy(row_no[0][:], red[:])
            dve.tensor_copy(row_no[1][:], nwt[:]).then_inc(tables_ready, 1)
            dve.tensor_tensor(begun[:], tile_no[:].unsqueeze(2).to_broadcast([1, T, EXPERTS]),
                              start[0:1].unsqueeze(1).to_broadcast([1, T, EXPERTS]), ALU.is_ge)\
               .then_inc(gate_step, 1)
            dve.wait_ge(gate_step, at + 11)
            dve.tensor_reduce(begun_count[:], begun[:], AX.X, ALU.add).then_inc(gate_step, 1)
            dve.wait_ge(gate_step, at + 12)
            dve.tensor_scalar(tile_pieces[:], begun_count[:], float(PIECES), None, ALU.mult)
            dve.tensor_scalar(start_halves[:], start[0:1], 2.0, None, ALU.mult)
            dve.tensor_copy(begun_i[:], begun_count[:]).then_inc(gate_step, 1)
            dve.wait_ge(gate_step, at + 13)
            dve.tensor_scalar(begun_i[:], begun_i[:], 1, None, ALU.bitwise_and).then_inc(gate_step, 1)
            dve.wait_ge(gate_step, at + 14)
            dve.tensor_scalar(tile_slot[:], begun_i[:], -float(SLOT), float(SLOT), ALU.mult, ALU.add)\
               .then_inc(tables_ready, 1)

            def split_rows(i, par):
                dve.wait_ge(rt_hi_done, i + 1)
                dve.tensor_tensor(rt_lo[par][:], rt_ps[:], rt_hi[par][:].bitcast(F32), ALU.subtract)\
                   .then_inc(rt_lo_done, 1)

            def split_hidden(i, h):
                dve.wait_ge(ht_hi_done, 2 * i + h + 1)
                dve.tensor_tensor(ht_lo[h][:], ht_ps[h][:], ht_hi[h][:].bitcast(F32), ALU.subtract)\
                   .then_inc(ht_lo_done, 1)

            def product(i, h):
                dve.wait_ge(silu_done, 2 * i + h + 1)
                if not is_tile(i, 0):
                    dve.wait_ge(h_turned, 2 * i + h - 1)
                dve.tensor_tensor(prod[h][:], silu[h][:], u_ps[h][:], ALU.mult).then_inc(prod_done, 1)

            def step(i, par, half):
                product(i, 0)
                if not is_tile(i, T - 1):
                    split_rows(i + 1, 1 - par)
                if not is_tile(i, 0):
                    split_hidden(i - 1, 1)
                product(i, 1)
                split_hidden(i, 0)

            split_rows(0, 0)
            tile_loop(dve, step)
            split_hidden(T - 1, 1)
            for t in range(TILES):
                dve.wait_ge(gathered[t % 2], 16 * CHOICES * (t // 2 + 1))
                dve.scalar_tensor_tensor(x_sb[:, t, :], back[t % 2][0][:], gate[0][:, t:t + 1], x_sb[:, t, :],
                                         ALU.mult, ALU.add).then_inc(gate_step, 1)
                dve.wait_ge(gate_step, at + 15 + t)
                dve.scalar_tensor_tensor(x_sb[:, t, :], back[t % 2][1][:], gate[1][:, t:t + 1], x_sb[:, t, :],
                                         ALU.mult, ALU.add).then_inc(added, 1)


SLOT_EXPERTS, SLOTS, SLOT_HID = 16, 64, 512
ALL_SLOTS = SLOT_EXPERTS * SLOTS
ST = ALL_SLOTS // P
SF = SLOT_HID // P
NS = BATCH * SLOTS
RANGE = KD * NS
PAIR_COLS = 2 * RANGE


def normalise_slots(nc, tag, slot_embeds, slot_g, slot_b, scale, ident_in, se_t, se_sw):
    with ExitStack() as ctx:
        def sb(name, shape, dt=F32):
            return ctx.enter_context(nc.sbuf_tensor(f"{tag}_{name}", shape, dt))

        def sem(name):
            return ctx.enter_context(nc.semaphore(f"{tag}_{name}"))

        ident = sb("ident", [P, P])
        rows = sb("rows", [P, ST, D])
        g_sb = sb("g", [P, D])
        b_sb = sb("b", [P, D])
        scale_sb = sb("scale", [P, 1])
        stats = sb("stats", [P, ST, 6])
        mean_var = sb("mv", [P, ST, 2])
        half_v = sb("halfv", [P, ST])
        seed_bits = sb("seedb", [P, ST], I32)
        rstd = sb("rstd", [P, ST])
        nwt = sb("nwt", [P, ST])
        three_halves = sb("three_halves", [P, ST])
        turn_ps = [ctx.enter_context(nc.psum_tensor(f"{tag}_turn{i}", [P, 4, P], F32)) for i in range(4)]

        loaded = sem("loaded")
        constant_set = sem("constant_set")
        stats_step = sem("stats_step")
        seed_ready = sem("seed_ready")
        newton_step = sem("newton_step")
        normed = sem("normed")
        turned = sem("turned")
        taken = sem("taken")

        block = ctx.enter_context(nc.Block())

        @block.sync
        def _(sp):
            sp.dma_start(rows[:], slot_embeds.rearrange("e s d -> (e s) d").rearrange("(t p) d -> p t d", p=P))\
              .then_inc(loaded, 16)
            sp.dma_start(ident[:], ident_in).then_inc(loaded, 16)
            sp.dma_start(g_sb[:], slot_g.partition_broadcast(P)).then_inc(loaded, 16)
            sp.dma_start(b_sb[:], slot_b.partition_broadcast(P)).then_inc(loaded, 16)
            sp.dma_start(scale_sb[:], scale.partition_broadcast(P)).then_inc(loaded, 16)

        @block.gpsimd
        def _(pool):
            pool.memset(three_halves[:], 1.5).then_inc(constant_set, 1)
            pool.wait_ge(constant_set, 1)
            pool.wait_ge(seed_ready, 1)
            newton_rsqrt(pool, newton_step, 0, rstd[:], half_v[:], nwt[:], three_halves[:])

        @block.vector
        def _(dve):
            dve.wait_ge(loaded, 80)
            row_stats(dve, stats_step, 0, rows[:], stats[:], mean_var[:], half_v[:], seed_bits[:],
                      rstd[:]).then_inc(seed_ready, 1)
            dve.wait_ge(newton_step, NEWTON_STEPS)
            for t in range(ST):
                ins = dve.tensor_scalar(rows[:, t, :], rows[:, t, :], mean_var[:, t, 0:1], rstd[:, t:t + 1],
                                        ALU.subtract, ALU.mult)
            ins.then_inc(normed, 1)
            dve.wait_ge(normed, 1)
            dve.tensor_tensor(rows[:], rows[:], g_sb[:].unsqueeze(1).to_broadcast([P, ST, D]), ALU.mult)\
               .then_inc(normed, 1)
            dve.wait_ge(normed, 2)
            dve.tensor_tensor(rows[:], rows[:], b_sb[:].unsqueeze(1).to_broadcast([P, ST, D]), ALU.add)\
               .then_inc(normed, 1)
            dve.wait_ge(normed, 3)
            dve.tensor_scalar(rows[:], rows[:], scale_sb[:], None, ALU.mult).then_inc(normed, 1)

        @block.tensor
        def _(pe):
            pe.wait_ge(normed, 4)
            for k in range(KD):
                for half in range(2):
                    for t in range(4):
                        ins = pe.transpose(turn_ps[2 * k + half][:, t, :],
                                           rows[:, 4 * half + t, k * P:(k + 1) * P], ident[:])
                    ins.then_inc(turned, 1)

        @block.scalar
        def _(act):
            for k in range(KD):
                for half in range(2):
                    n = 2 * k + half
                    act.wait_ge(turned, n + 1)
                    cols = slice(half * 4 * P, (half + 1) * 4 * P)
                    act.activation(se_t[:, k, cols], turn_ps[n][:].rearrange("p t s -> p (t s)"), ACT.Copy)
                    src = turn_ps[n][:].rearrange("p t (r s) -> p t r s", r=2)
                    dst = se_sw[:, k, cols].rearrange("p (t r s) -> p t r s", t=4, r=2)
                    for r in range(2):
                        act.activation(dst[:, :, r, :], src[:, :, 1 - r, :], ACT.Copy)


def dispatch_tokens(nc, tag, x_in, norm_g, norm_b, ident_in, se_t, se_sw, arena, inv_rows, comb_dram):
    HALF = ALL_SLOTS // 2
    QUARTERS = 4
    EH = SLOT_EXPERTS // 4
    SLOTS_CREDIT = 8
    COMB_CREDIT = 4
    DISP_CREDIT = 2

    with ExitStack() as ctx:
        def sb(name, shape, dt=F32):
            return ctx.enter_context(nc.sbuf_tensor(f"{tag}_{name}", shape, dt))

        def pb(name, shape):
            return ctx.enter_context(nc.psum_tensor(f"{tag}_{name}", shape, F32))

        def sem(name):
            return ctx.enter_context(nc.semaphore(f"{tag}_{name}"))

        ident = sb("ident", [P, P])
        g_sb = sb("g", [P, D])
        b_sb = sb("b", [P, D])
        x_sb = [sb(f"x{i}", [P, NT, D]) for i in range(2)]
        xh_sb = [sb(f"xh{i}", [P, NT, D]) for i in range(2)]
        xt_sb = [sb(f"xt{i}", [P, KD, SEQ]) for i in range(2)]
        comb = [sb(f"comb{i}", [P, ALL_SLOTS]) for i in range(2)]
        comb_t = [sb(f"combt{i}", [P, ST, P]) for i in range(2)]
        disp_t = [sb(f"dispt{i}", [P, 2, SEQ]) for i in range(2)]
        disp = sb("disp", [P, NT, ALL_SLOTS])
        stats = sb("stats", [P, NT, 6])
        mean_var = sb("mv", [P, NT, 2])
        half_v = sb("halfv", [P, NT])
        seed_bits = sb("seedb", [P, NT], I32)
        rstd = sb("rstd", [P, NT])
        nwt = sb("nwt", [P, NT])
        three_halves = sb("three_halves", [P, NT])
        neg_max_c = [sb(f"nmaxc{i}", [P, 1]) for i in range(2)]
        sum_c = [sb(f"sumc{i}", [P, 1]) for i in range(2)]
        neg_max_d = [sb(f"nmaxd{i}", [P, 2]) for i in range(2)]
        sum_d = [sb(f"sumd{i}", [P, 2]) for i in range(2)]
        inv_d = [sb(f"invd{i}", [P, 2]) for i in range(2)]

        comb_ps = pb("combp", [P, 2, HALF])
        disp_ps = [pb(f"dispp{i}", [P, 2, SEQ]) for i in range(2)]
        turn_ps = [pb(f"turn{i}", [P, 4, P]) for i in range(2)]
        slot_ps = [pb(f"slot{i}", [P, HALF]) for i in range(2)]

        weights_in = sem("weights_in")
        x_loaded = [sem(f"x_loaded{i}") for i in range(2)]
        constant_set = sem("constant_set")
        stats_step = sem("stats_step")
        seed_ready = sem("seed_ready")
        newton_step = sem("newton_step")
        norm_step = sem("norm_step")
        gained = sem("gained")
        xh_ready = sem("xh_ready")
        xt_turned = sem("xt_turned")
        xt_ready = sem("xt_ready")
        comb_logits = sem("comb_logits")
        comb_max = sem("comb_max")
        comb_exp = sem("comb_exp")
        inv_step = sem("inv_step")
        comb_turned = sem("comb_turned")
        comb_taken = sem("comb_taken")
        comb_stored = [sem(f"comb_stored{i}") for i in range(2)]
        disp_logits = sem("disp_logits")
        disp_max = sem("disp_max")
        disp_exp = sem("disp_exp")
        inv_d_ready = sem("inv_d_ready")
        disp_ready = sem("disp_ready")
        disp_turned = sem("disp_turned")
        disp_taken = sem("disp_taken")
        slots_done = sem("slots_done")
        slots_taken = sem("slots_taken")

        x_dram = x_in.rearrange("b (t p) d -> b p t d", p=P)
        block = ctx.enter_context(nc.Block())

        def has_batch_before(pair, s):
            return not (isinstance(pair, int) and pair == 0 and s == 0)

        def batch_before(pair, s):
            return (pair, 0) if s else (pair - 1, 1)

        @block.sync
        def _(sp):
            sp.sem_inc(comb_stored[0], 16)
            sp.sem_inc(comb_stored[1], 16)
            sp.dma_start(ident[:], ident_in).then_inc(weights_in, 16)
            sp.dma_start(g_sb[:], norm_g.partition_broadcast(P)).then_inc(weights_in, 16)
            sp.dma_start(b_sb[:], norm_b.partition_broadcast(P)).then_inc(weights_in, 16)

            def load(pair, s):
                if not isinstance(pair, int):
                    sp.wait_ge(xh_ready, 2 * pair + s - 1)
                sp.dma_start(x_sb[s][:], x_dram[2 * pair + s]).then_inc(x_loaded[s], 16)

            def store(pair, s):
                for t in range(NT):
                    n = (2 * pair + s) * NT + t
                    sp.wait_ge(comb_taken, nth(2 * n + 1))
                    sp.dma_start(comb_dram[2 * pair + s, :, :, t * P:(t + 1) * P].rearrange("i s n -> s i n"),
                                 comb_t[t][:]).then_inc(comb_stored[t], 16)

            load(0, 0)
            load(0, 1)
            with sp.Fori(0, BATCH // 2 - 1) as pair:
                for s in range(2):
                    load(pair + 1, s)
                    store(pair, s)
            for s in range(2):
                store(BATCH // 2 - 1, s)
            for t in range(NT):
                sp.wait_ge(comb_stored[t], 16 * (BATCH + 1))

        @block.gpsimd
        def _(pool):
            pool.memset(three_halves[:], 1.5).then_inc(constant_set, 1)
            pool.wait_ge(constant_set, 1)
            pool.wait_ge(weights_in, 48)

            def normalise(pair, s):
                b = 2 * pair + s
                for twice in range(2):
                    pool.wait_ge(seed_ready, 2 * b + twice + 1)
                    newton_rsqrt(pool, newton_step, NEWTON_STEPS * (2 * b + twice), rstd[:], half_v[:], nwt[:],
                                 three_halves[:])
                pool.wait_ge(norm_step, 2 * b + 2)
                pool.tensor_tensor(xh_sb[s][:], xh_sb[s][:], g_sb[:].unsqueeze(1).to_broadcast([P, NT, D]),
                                   ALU.mult).then_inc(gained, 1)
                pool.wait_ge(gained, b + 1)
                pool.tensor_tensor(xh_sb[s][:], xh_sb[s][:], b_sb[:].unsqueeze(1).to_broadcast([P, NT, D]),
                                   ALU.add).then_inc(xh_ready, 1)

            with pool.Fori(0, BATCH // 2) as pair:
                normalise(pair, 0)
                normalise(pair, 1)

        @block.scalar
        def _(act):
            act.sem_inc(comb_exp, CREDIT)
            act.sem_inc(slots_taken, CREDIT)

            def slots_take(pair, s, n):
                k, half = n // 2, n % 2
                act.wait_ge(slots_done, SLOTS_CREDIT + 4 * (2 * pair + s) + n + 1)
                src = slot_ps[half][:].rearrange("p (i r s) -> p i r s", r=2, s=SLOTS)
                for r in range(2):
                    at = r * RANGE + k * NS
                    first = (2 * pair + (s if r == 0 else 1 - s)) * SLOTS
                    dst = arena[:, half * EH:(half + 1) * EH, at:at + NS]
                    ins = act.activation(dst[:, :, bass.ds(first, SLOTS)], src[:, :, r, :], ACT.Copy)
                ins.then_inc(slots_taken, 1)

            def step(pair, s, last):
                b = 2 * pair + s
                act.wait_ge(xt_turned, b + 1)
                act.activation(xt_sb[s][:], turn_ps[0][:].rearrange("p (k t) n -> p k (t n)", k=KD), ACT.Copy)\
                   .then_inc(xt_ready, 1)

                def comb_exp_of(t):
                    n = NT * b + t
                    act.wait_ge(comb_max, n + 1)
                    act.wait_ge(comb_turned, 2 * n - 2 + COMB_CREDIT)
                    act.activation(comb[t][:], comb_ps[:].rearrange("p a s -> p (a s)"), ACT.Exp,
                                   bias=neg_max_c[t][:], accum_out=sum_c[t][:]).then_inc(comb_exp, 1)

                def disp_exp_of(q):
                    n = QUARTERS * b + q
                    i = q % 2
                    act.wait_ge(disp_max, n + 1)
                    act.wait_ge(disp_turned, two_before(n))
                    for j in range(2):
                        ins = act.activation(disp_t[i][:, j, :], disp_ps[i][:, j, :], ACT.Exp,
                                             bias=neg_max_d[i][:, j:j + 1], accum_out=sum_d[i][:, j:j + 1])
                    ins.then_inc(disp_exp, 1)

                def disp_take(q):
                    n = QUARTERS * b + q
                    act.wait_ge(disp_turned, nth(n))
                    act.activation(disp[:, :, q * 2 * P:(q + 1) * 2 * P],
                                   turn_ps[1][:].rearrange("p (t j) s -> p t (j s)", t=NT), ACT.Copy)\
                       .then_inc(disp_taken, 1)

                comb_exp_of(0)
                disp_exp_of(0)
                if has_batch_before(pair, s):
                    slots_take(*batch_before(pair, s), 0)
                    slots_take(*batch_before(pair, s), 1)
                comb_exp_of(1)
                disp_exp_of(1)
                if has_batch_before(pair, s):
                    slots_take(*batch_before(pair, s), 2)
                    slots_take(*batch_before(pair, s), 3)
                disp_take(0)
                disp_exp_of(2)
                disp_take(1)
                disp_exp_of(3)
                disp_take(2)
                disp_take(3)

            pair_loop(act, step, peel_first=True)
            for n in range(4):
                slots_take(BATCH // 2 - 1, 1, n)

        @block.tensor
        def _(pe):
            pe.sem_inc(slots_done, SLOTS_CREDIT)
            pe.sem_inc(comb_turned, COMB_CREDIT)
            pe.sem_inc(disp_turned, CREDIT)
            pe.wait_ge(weights_in, 48)

            def slots(pair, s, part):
                b = 2 * pair + s
                k, half = part // 2, part % 2
                pe.wait_ge(slots_taken, two_before(4 * b + part))
                if part == 0:
                    pe.wait_ge(disp_taken, DISP_CREDIT + QUARTERS * (b + 1))
                for t in range(NT):
                    ins = pe.matmul(slot_ps[half][:], xh_sb[s][:, t, k * P:(k + 1) * P],
                                    disp[:, t, half * HALF:(half + 1) * HALF],
                                    start=(t == 0), stop=(t == NT - 1))
                ins.then_inc(slots_done, 1)

            def step(pair, s, last):
                b = 2 * pair + s
                se = se_sw if s else se_t
                pe.wait_ge(comb_taken, nth(4 * b - 1))
                pe.wait_ge(xh_ready, b + 1)
                for k in range(KD):
                    for t in range(NT):
                        ins = pe.transpose(turn_ps[0][:, 2 * k + t, :], xh_sb[s][:, t, k * P:(k + 1) * P],
                                           ident[:])
                ins.then_inc(xt_turned, 1)
                pe.wait_ge(xt_ready, b + 1)

                def comb_scores(t):
                    n = NT * b + t
                    pe.wait_ge(comb_exp, n + CREDIT)
                    for half in range(2):
                        for k in range(KD):
                            ins = pe.matmul(comb_ps[:, half, :], xt_sb[s][:, k, t * P:(t + 1) * P],
                                            se[:, k, half * HALF:(half + 1) * HALF],
                                            start=(k == 0), stop=(k == KD - 1))
                    ins.then_inc(comb_logits, 1)

                def comb_turn(t):
                    n = NT * b + t
                    pe.wait_ge(comb_exp, nth(n))
                    for half in range(2):
                        pe.wait_ge(comb_taken, nth(2 * n + half - 1))
                        for i in range(4):
                            c = (4 * half + i) * P
                            ins = pe.transpose(turn_ps[0][:, i, :], comb[t][:, c:c + P], ident[:])
                        ins.then_inc(comb_turned, 1)

                def disp_scores(q):
                    n = QUARTERS * b + q
                    pe.wait_ge(disp_exp, DISP_CREDIT + n - 1)
                    for j in range(2):
                        for k in range(KD):
                            ins = pe.matmul(disp_ps[q % 2][:, j, :], se_t[:, k, (2 * q + j) * P:(2 * q + j + 1) * P],
                                            xt_sb[s][:, k, :], start=(k == 0), stop=(k == KD - 1))
                    ins.then_inc(disp_logits, 1)

                def disp_turn(q):
                    n = QUARTERS * b + q
                    pe.wait_ge(disp_ready, n + 1)
                    pe.wait_ge(disp_taken, DISP_CREDIT + n - 1 + 1)
                    for t in range(NT):
                        for j in range(2):
                            ins = pe.transpose(turn_ps[1][:, 2 * t + j, :], disp_t[q % 2][:, j, t * P:(t + 1) * P],
                                               ident[:])
                    ins.then_inc(disp_turned, 1)

                comb_scores(0)
                disp_scores(0)
                if has_batch_before(pair, s):
                    slots(*batch_before(pair, s), 0)
                    slots(*batch_before(pair, s), 1)
                comb_scores(1)
                disp_scores(1)
                if has_batch_before(pair, s):
                    slots(*batch_before(pair, s), 2)
                    slots(*batch_before(pair, s), 3)
                comb_turn(0)
                disp_turn(0)
                disp_scores(2)
                comb_turn(1)
                disp_turn(1)
                disp_scores(3)
                disp_turn(2)
                disp_turn(3)

            pair_loop(pe, step, peel_first=True)
            for part in range(4):
                slots(BATCH // 2 - 1, 1, part)

        @block.vector
        def _(dve):
            dve.sem_inc(disp_exp, DISP_CREDIT)
            dve.sem_inc(disp_taken, DISP_CREDIT)
            dve.sem_inc(comb_taken, CREDIT)

            def statistics(pair, s, twice):
                n, o = 2 * pair + s + 1, 1 - s
                if twice:
                    dve.wait_ge(norm_step, 2 * n + 1)
                else:
                    dve.wait_ge(x_loaded[o], 16 * (pair + s + 1))
                row_stats(dve, stats_step, STATS_STEPS * (2 * n + twice), x_sb[o][:],
                          stats[:], mean_var[:], half_v[:], seed_bits[:], rstd[:]).then_inc(seed_ready, 1)

            def normalise(pair, s, twice):
                n, o = 2 * pair + s + 1, 1 - s
                if twice:
                    dve.wait_ge(slots_done, SLOTS_CREDIT + 4 * (n - 1))
                dve.wait_ge(newton_step, NEWTON_STEPS * (2 * n + twice + 1))
                dst = xh_sb[o] if twice else x_sb[o]
                for t in range(NT):
                    ins = dve.tensor_scalar(dst[:, t, :], x_sb[o][:, t, :], mean_var[:, t, 0:1],
                                            rstd[:, t:t + 1], ALU.subtract, ALU.mult)
                ins.then_inc(norm_step, 1)

            def step(pair, s, last):
                b = 2 * pair + s

                def comb_max_of(t):
                    n = NT * b + t
                    dve.wait_ge(comb_logits, n + 1)
                    dve.tensor_reduce(neg_max_c[t][:], comb_ps[:].rearrange("p a s -> p (a s)"), AX.X, ALU.max,
                                      negate=True).then_inc(comb_max, 1)

                def comb_take(t):
                    n = NT * b + t
                    dve.wait_ge(comb_exp, nth(n))
                    dve.reciprocal(inv_rows[:, bass.ds(n, 1)], sum_c[t][:])
                    dve.wait_ge(comb_stored[t], 16 * (b + 1))
                    for half in range(2):
                        dve.wait_ge(comb_turned, COMB_CREDIT + 2 * n + half + 1)
                        dve.tensor_copy(comb_t[t][:, 4 * half:4 * half + 4, :], turn_ps[0][:])\
                           .then_inc(comb_taken, 1)

                def disp_max_of(q):
                    n = QUARTERS * b + q
                    dve.wait_ge(disp_logits, n + 1)
                    dve.tensor_reduce(neg_max_d[q % 2][:], disp_ps[q % 2][:], AX.X, ALU.max, negate=True)\
                       .then_inc(disp_max, 1)

                def disp_divide(q):
                    n = QUARTERS * b + q
                    i = q % 2
                    dve.wait_ge(disp_exp, DISP_CREDIT + n + 1)
                    dve.reciprocal(inv_d[i][:], sum_d[i][:]).then_inc(inv_d_ready, 1)
                    dve.wait_ge(inv_d_ready, n + 1)
                    for j in range(2):
                        ins = dve.tensor_scalar(disp_t[i][:, j, :], disp_t[i][:, j, :], inv_d[i][:, j:j + 1],
                                                None, ALU.mult)
                    ins.then_inc(disp_ready, 1)

                comb_max_of(0)
                disp_max_of(0)
                disp_divide(0)
                if not last:
                    statistics(pair, s, 0)
                comb_max_of(1)
                disp_max_of(1)
                disp_divide(1)
                if not last:
                    normalise(pair, s, 0)
                    statistics(pair, s, 1)
                comb_take(0)
                disp_max_of(2)
                comb_take(1)
                if not last:
                    normalise(pair, s, 1)
                disp_divide(2)
                disp_max_of(3)
                disp_divide(3)

            for twice in range(2):
                statistics(-1, 1, twice)
                normalise(-1, 1, twice)
            pair_loop(dve, step)


def slot_experts(nc, tag, wg, wu, wd, bg, bu, bd, arena):
    W = KD * SLOT_HID
    PART = 3 * W // SF
    GU_PARTS = -(-2 * W // PART)
    E = SLOT_EXPERTS
    assert W == SF * D and NS == 4 * P

    with ExitStack() as ctx:
        def sb(name, shape, dt=F32):
            return ctx.enter_context(nc.sbuf_tensor(f"{tag}_{name}", shape, dt))

        def pb(name, shape):
            return ctx.enter_context(nc.psum_tensor(f"{tag}_{name}", shape, F32))

        def sem(name):
            return ctx.enter_context(nc.semaphore(f"{tag}_{name}"))

        w_hi = [sb(f"w_hi{i}", [P, 3 * W], F32R) for i in range(2)]
        w_lo = [sb(f"w_lo{i}", [P, 3 * W], F32R) for i in range(2)]
        stage = [sb(f"stage{i}", [P, 3 * W]) for i in range(2)]
        bd_sb = [sb(f"bd{i}", [P, D]) for i in range(2)]
        bg_sb = sb("bg", [P, E, SF])
        bu_sb = sb("bu", [P, E, SF])
        xs_hi = [sb(f"xs_hi{i}", [P, RANGE], F32R) for i in range(2)]
        xs_lo = [sb(f"xs_lo{i}", [P, RANGE], F32R) for i in range(2)]
        gelu = [sb(f"gelu{i}", [P, NS]) for i in range(2)]
        prod = [sb(f"prod{i}", [P, NS]) for i in range(2)]
        h_hi = [sb(f"h_hi{i}", [P, NS], F32R) for i in range(2)]
        h_lo = [sb(f"h_lo{i}", [P, NS], F32R) for i in range(2)]
        tick = sb("tick", [P, 1])
        g_ps = [pb(f"g{i}", [P, NS]) for i in range(2)]
        u_ps = [pb(f"u{i}", [P, NS]) for i in range(2)]
        y_ps = [pb(f"y{i}", [P, 4, D]) for i in range(2)]

        biases_in = sem("biases_in")
        staged = [sem(f"staged{i}") for i in range(2)]
        bd_in = [sem(f"bd_in{i}") for i in range(2)]
        w_hi_done = sem("w_hi_done")
        w_lo_done = sem("w_lo_done")
        x_hi_done = sem("x_hi_done")
        x_lo_done = sem("x_lo_done")
        gu_done = sem("gu_done")
        gelu_done = sem("gelu_done")
        prod_done = sem("prod_done")
        hi_done = sem("hi_done")
        lo_done = sem("lo_done")
        down_done = sem("down_done")
        y_taken = sem("y_taken")

        def slots_of(pair, s):
            return arena[:, bass.ds(pair, 1), s * RANGE:(s + 1) * RANGE].rearrange("p i c -> p (i c)")

        def expert_loop(eng, step, peel_first=False):
            if peel_first:
                step(0, 0, False)
                step(0, 1, False)
            with eng.Fori(1 if peel_first else 0, E // 2 - 1) as pair:
                step(pair, 0, False)
                step(pair, 1, False)
            step(E // 2 - 1, 0, False)
            step(E // 2 - 1, 1, True)

        block = ctx.enter_context(nc.Block())

        @block.sync
        def _(sp):
            sp.sem_inc(w_lo_done, 2 * SF)
            with sp.Fori(0, E // 2) as pair:
                for s in range(2):
                    e = 2 * pair + s
                    sp.wait_ge(w_lo_done, SF * e + SF)
                    for n, (w, parts) in enumerate(((wg, KD), (wu, KD), (wd, SF))):
                        dst = stage[s][:, n * W:(n + 1) * W].rearrange("p (k n) -> p k n", k=parts)
                        sp.dma_start(dst, w[e].rearrange("(k p) n -> p k n", p=P)).then_inc(staged[s], 16)
                    sp.wait_ge(y_taken, two_before(e))
                    sp.dma_start(bd_sb[s][:], bd[e].partition_broadcast(P)).then_inc(bd_in[s], 16)

        @block.gpsimd
        def _(pool):
            def split(pair, s):
                for f in range(SF):
                    part = slice(f * PART, (f + 1) * PART)
                    pool.wait_ge(w_hi_done, SF * (2 * pair + s) + f + 1)
                    pool.tensor_tensor(w_lo[s][:, part], stage[s][:, part], w_hi[s][:, part].bitcast(F32),
                                       ALU.subtract).then_inc(w_lo_done, 1)

            with pool.Fori(0, E // 2) as pair:
                split(pair, 0)
                split(pair, 1)

        @block.scalar
        def _(act):
            act.dma_start(bg_sb[:], bg).then_inc(biases_in, 16)
            act.dma_start(bu_sb[:], bu).then_inc(biases_in, 16)

            def split_weights(pair, s, f):
                o = 1 - s
                part = slice(f * PART, (f + 1) * PART)
                if f == 0:
                    act.wait_ge(staged[o], 48 * (pair + s + 1))
                    if not (isinstance(pair, int) and pair < 0):
                        act.wait_ge(down_done, CREDIT + SF * (2 * pair + s))
                act.activation(w_hi[o][:, part], stage[o][:, part], ACT.Copy).then_inc(w_hi_done, 1)

            def split_slots(pair, s):
                act.activation(xs_hi[1 - s][:], slots_of(pair + s, 1 - s), ACT.Copy).then_inc(x_hi_done, 1)

            def expert(pair, s, last):
                for f in range(SF):
                    n = (2 * pair + s) * SF + f
                    i = f % 2
                    act.wait_ge(prod_done, two_before(n))
                    act.wait_ge(gu_done, n + 1)
                    act.activation(gelu[i][:], g_ps[i][:], ACT.Gelu,
                                   bias=bg_sb[:, bass.ds(2 * pair + s, 1), f]).then_inc(gelu_done, 1)
                    if not last:
                        split_weights(pair, s, f)
                    act.wait_ge(down_done, two_before(n))
                    act.wait_ge(prod_done, nth(n))
                    act.activation(h_hi[i][:], prod[i][:], ACT.Copy).then_inc(hi_done, 1)
                    if f == 1 and not last:
                        split_slots(pair, s)

            for f in range(SF):
                split_weights(-1, 1, f)
            split_slots(-1, 1)
            act.wait_ge(biases_in, 32)
            expert_loop(act, expert)

        @block.tensor
        def _(pe):
            pe.sem_inc(down_done, CREDIT)

            def three_passes(out, a_hi, a_lo, b_hi, b_lo, start, stop):
                pe.matmul(out, a_hi, b_hi, start=start, stop=False, skip_group_check=True)
                pe.matmul(out, a_lo, b_hi, start=False, stop=False, skip_group_check=True)
                return pe.matmul(out, a_hi, b_lo, start=False, stop=stop, skip_group_check=True)

            def gate_up(pair, s, f):
                e = 2 * pair + s
                n = e * SF + f
                if f == 0:
                    pe.wait_ge(w_lo_done, 2 * SF + SF * e + GU_PARTS)
                    pe.wait_ge(x_lo_done, e + 1)
                pe.wait_ge(prod_done, two_before(n))
                for ps, first in ((g_ps[f % 2], 0), (u_ps[f % 2], W)):
                    for k in range(KD):
                        a = slice(first + k * SLOT_HID + f * P, first + k * SLOT_HID + (f + 1) * P)
                        x = slice(k * NS, (k + 1) * NS)
                        ins = three_passes(ps[:], w_hi[s][:, a], w_lo[s][:, a], xs_hi[s][:, x], xs_lo[s][:, x],
                                           k == 0, k == KD - 1)
                ins.then_inc(gu_done, 1)

            def down(pair, s, f):
                e = 2 * pair + s
                n = e * SF + f
                i = f % 2
                if f == 0:
                    pe.wait_ge(w_lo_done, 2 * SF + SF * e + SF)
                    pe.wait_ge(y_taken, two_before(e))
                pe.wait_ge(lo_done, n + 1)
                for t in range(4):
                    a, c = slice(t * P, (t + 1) * P), slice(2 * W + f * D, 2 * W + (f + 1) * D)
                    ins = three_passes(y_ps[s][:, t, :], h_hi[i][:, a], h_lo[i][:, a], w_hi[s][:, c],
                                       w_lo[s][:, c], f == 0 and t % 2 == 0, f == SF - 1)
                ins.then_inc(down_done, 1)

            def expert(pair, s, last):
                for f in range(1, SF):
                    gate_up(pair, s, f)
                    down(pair, s, f - 1)
                if not last:
                    gate_up(pair + s, 1 - s, 0)
                down(pair, s, SF - 1)

            gate_up(0, 0, 0)
            expert_loop(pe, expert)

        @block.vector
        def _(dve):
            dve.sem_inc(prod_done, CREDIT)
            dve.sem_inc(y_taken, CREDIT)

            def split_slots(pair, s):
                o = 1 - s
                dve.wait_ge(x_hi_done, 2 * pair + s + 2)
                dve.tensor_tensor(xs_lo[o][:], slots_of(pair + s, o), xs_hi[o][:].bitcast(F32), ALU.subtract)\
                   .then_inc(x_lo_done, 1)

            def take(pair, s):
                dve.wait_ge(bd_in[s], 16 * (pair + 1))
                dve.wait_ge(down_done, nth(SF * (2 * pair + s) + SF - 1))
                for half in range(2):
                    rows = slice(half * SLOTS, (half + 1) * SLOTS)
                    dst = arena[rows, bass.ds(pair, 1), :].rearrange("p i (j r d) -> p (i j) r d", r=2, d=D)
                    ins = dve.tensor_tensor(dst[:, :, half ^ s, :], y_ps[s][rows, :, :],
                                            bd_sb[s][rows, :].unsqueeze(1).to_broadcast([SLOTS, 4, D]), ALU.add)
                ins.then_inc(y_taken, 1)

            def expert(pair, s, last):
                e = 2 * pair + s
                for f in range(SF):
                    n = e * SF + f
                    i = f % 2
                    dve.wait_ge(gelu_done, n + 1)
                    dve.scalar_tensor_tensor(prod[i][:], u_ps[i][:], bu_sb[:, bass.ds(e, 1), f], gelu[i][:],
                                             ALU.add, ALU.mult).then_inc(prod_done, 1)
                    dve.wait_ge(hi_done, n + 1)
                    dve.tensor_tensor(h_lo[i][:], prod[i][:], h_hi[i][:].bitcast(F32), ALU.subtract)\
                       .then_inc(lo_done, 1)
                    if f == 0 and not (isinstance(e, int) and e == 0):
                        take(*((pair, 0) if s else (pair - 1, 1)))
                    if f == 2 and not last:
                        split_slots(pair, s)

            dve.wait_ge(biases_in, 32)
            split_slots(-1, 1)
            expert_loop(dve, expert, peel_first=True)
            take(E // 2 - 1, 1)


def combine_slots(nc, tag, x_in, comb_dram, inv_rows, arena, x_out):
    with ExitStack() as ctx:
        def sb(name, shape, dt=F32):
            return ctx.enter_context(nc.sbuf_tensor(f"{tag}_{name}", shape, dt))

        def sem(name):
            return ctx.enter_context(nc.semaphore(f"{tag}_{name}"))

        x_sb = [sb(f"x{i}", [P, NT, D]) for i in range(2)]
        xo_sb = [sb(f"xo{i}", [P, NT, D]) for i in range(2)]
        ct_sb = [sb(f"ct{i}", [P, ST, SEQ]) for i in range(2)]
        out_ps = [ctx.enter_context(nc.psum_tensor(f"{tag}_out{i}", [P, NT, D], F32)) for i in range(2)]

        loaded = [sem(f"loaded{i}") for i in range(2)]
        out_done = sem("out_done")
        xo_ready = sem("xo_ready")
        stored = [sem(f"stored{i}") for i in range(2)]

        x_dram = x_in.rearrange("b (t p) d -> b p t d", p=P)
        xo_dram = x_out.rearrange("b (t p) d -> b p t d", p=P)
        block = ctx.enter_context(nc.Block())

        def pairs(eng, step):
            with eng.Fori(0, BATCH // 2) as pair:
                step(pair, 0)
                step(pair, 1)

        @block.sync
        def _(sp):
            sp.sem_inc(stored[0], 16)
            sp.sem_inc(stored[1], 16)

            def load(pair, s):
                b = 2 * pair + s
                sp.wait_ge(out_done, two_before(b))
                sp.dma_start(ct_sb[s][:], comb_dram[b].rearrange("i s n -> s i n")).then_inc(loaded[s], 16)
                sp.wait_ge(xo_ready, two_before(b))
                sp.dma_start(x_sb[s][:], x_dram[b]).then_inc(loaded[s], 16)

            def store(pair, s):
                sp.wait_ge(xo_ready, nth(2 * pair + s))
                sp.dma_start(xo_dram[2 * pair + s], xo_sb[s][:]).then_inc(stored[s], 16)

            load(0, 0)
            load(0, 1)
            with sp.Fori(0, BATCH // 2 - 1) as pair:
                for s in range(2):
                    store(pair, s)
                    load(pair + 1, s)
            for s in range(2):
                store(BATCH // 2 - 1, s)
            for s in range(2):
                sp.wait_ge(stored[s], 16 * (BATCH // 2 + 1))

        @block.tensor
        def _(pe):
            pe.sem_inc(out_done, CREDIT)

            def step(pair, s):
                b = 2 * pair + s
                pe.wait_ge(loaded[s], 32 * (pair + 1))
                pe.wait_ge(xo_ready, two_before(b))
                for t in range(NT):
                    for i in range(ST):
                        ins = pe.matmul(out_ps[s][:, t, :], ct_sb[s][:, i, t * P:(t + 1) * P],
                                        arena[:, i, bass.ts(b, D)], start=(i == 0), stop=(i == ST - 1))
                ins.then_inc(out_done, 1)

            pairs(pe, step)

        @block.vector
        def _(dve):
            dve.sem_inc(xo_ready, CREDIT)

            def step(pair, s):
                b = 2 * pair + s
                dve.wait_ge(out_done, nth(b))
                dve.wait_ge(stored[s], 16 * (pair + 1))
                for t in range(NT):
                    ins = dve.scalar_tensor_tensor(xo_sb[s][:, t, :], out_ps[s][:, t, :],
                                                   inv_rows[:, bass.ds(NT * b + t, 1)], x_sb[s][:, t, :],
                                                   ALU.mult, ALU.add)
                ins.then_inc(xo_ready, 1)

            pairs(dve, step)


def slot_mixture(nc, tag, x_in, norm_g, norm_b, slot_g, slot_b, scale, slot_embeds, wg, bg, wu, bu, wd, bd,
                 x_out, ident_in):
    comb_dram = nc.dram_tensor(f"{tag}_comb", (BATCH, ST, P, SEQ), F32, kind="Internal").ap()
    with ExitStack() as ctx:
        arena = ctx.enter_context(nc.sbuf_tensor(f"{tag}_arena", [P, SLOT_EXPERTS // 2, PAIR_COLS], F32))
        inv_rows = ctx.enter_context(nc.sbuf_tensor(f"{tag}_inv_rows", [P, TILES], F32))
        with ExitStack() as inner:
            se_t = inner.enter_context(nc.sbuf_tensor(f"{tag}_se_t", [P, KD, ALL_SLOTS], F32))
            se_sw = inner.enter_context(nc.sbuf_tensor(f"{tag}_se_sw", [P, KD, ALL_SLOTS], F32))
            normalise_slots(nc, f"{tag}n", slot_embeds, slot_g, slot_b, scale, ident_in, se_t, se_sw)
            dispatch_tokens(nc, f"{tag}d", x_in, norm_g, norm_b, ident_in, se_t, se_sw, arena, inv_rows, comb_dram)
        slot_experts(nc, f"{tag}e", wg, wu, wd, bg, bu, bd, arena)
        combine_slots(nc, f"{tag}c", x_in, comb_dram, inv_rows, arena, x_out)


def two_layer_program(nc, a, out):
    hidden = [nc.dram_tensor(f"hidden{i}", (BATCH, SEQ, D), F32, kind="Internal").ap() for i in range(3)]
    cross_attention(nc, "l0", a["x"], a["ctx_t"], a["L0_xattn_Wq"], a["L0_xattn_Wk"], a["L0_xattn_Wv"],
                    a["L0_xattn_Wo"], a["L0_xattn_bo"], hidden[0], a["identity"], heads=8, head_dim=64)
    routed_experts(nc, "l0f", hidden[0], a["L0_ffn_w_gate"], a["L0_ffn_w_gate_up"], a["L0_ffn_w_down"],
                   hidden[1], a["identity"], a["expert_numbers"], a["row_tile_numbers"], a["rows_below"],
                   a["experts_before"])
    cross_attention(nc, "l1", hidden[1], a["ctx_t"], a["l1_wq"], a["l1_wk"], a["l1_wv"],
                    a["l1_wo"], a["L1_xattn_proj_b"], hidden[2], a["identity"], heads=16, head_dim=16,
                    q_bias=a["l1_bq"], k_bias=a["l1_bk"], v_bias=a["l1_bv"])
    slot_mixture(nc, "l1f", hidden[2], a["L1_ffn_norm_g"], a["L1_ffn_norm_b"], a["L1_ffn_slot_g"],
                 a["L1_ffn_slot_b"], a["L1_ffn_scale"], a["L1_ffn_slot_embeds"], a["L1_ffn_Wg"], a["l1_bg"],
                 a["L1_ffn_Wu"], a["l1_bu"], a["L1_ffn_Wd"], a["L1_ffn_bd"], out, a["identity"])


def kernel(**inputs):
    import numpy as _np
    import concourse.bacc as _bacc
    from concourse import mybir as _mybir
    from concourse.bass_utils import run_bass_kernel_spmd as _run

    heads, head_dim, row_group = 16, 16, 32

    def spread_heads(w):
        out = _np.zeros((*w.shape[:-1], heads, row_group), w.dtype)
        out[..., :head_dim] = w.reshape(*w.shape[:-1], heads, head_dim)
        return out.reshape(*w.shape[:-1], heads * row_group)

    def column_tiles(b):
        return b.reshape(-1, P).T

    i = {k: _np.asarray(v) for k, v in inputs.items()}
    inner = heads * head_dim
    kv_w, kv_b = i["L1_xattn_kv_w"], i["L1_xattn_kv_b"]
    laid = {k: v for k, v in i.items() if k.startswith("L0_")}
    for name in ("L1_xattn_proj_b", "L1_ffn_norm_g", "L1_ffn_norm_b", "L1_ffn_slot_g",
                 "L1_ffn_slot_b", "L1_ffn_scale", "L1_ffn_slot_embeds", "L1_ffn_Wg", "L1_ffn_Wu", "L1_ffn_Wd",
                 "L1_ffn_bd"):
        laid[name] = i[name]
    laid |= {
        "x": i["x"],
        "ctx_t": i["ctx_768"].transpose(0, 2, 1),
        "l1_wq": spread_heads(i["L1_xattn_q_w"]),
        "l1_wk": spread_heads(kv_w[:, :inner]),
        "l1_wv": kv_w[:, inner:],
        "l1_wo": spread_heads(i["L1_xattn_proj_w"].T).T,
        "l1_bq": column_tiles(spread_heads(i["L1_xattn_q_b"])),
        "l1_bk": column_tiles(spread_heads(kv_b[:inner])),
        "l1_bv": kv_b[inner:],
        "l1_bg": i["L1_ffn_bg"].reshape(SLOT_EXPERTS, SLOT_HID // P, P).transpose(2, 0, 1),
        "l1_bu": i["L1_ffn_bu"].reshape(SLOT_EXPERTS, SLOT_HID // P, P).transpose(2, 0, 1),
        "identity": _np.eye(P, dtype=_np.float32),
        "expert_numbers": _np.arange(EXPERTS, dtype=_np.float32),
        "row_tile_numbers": _np.arange(ROW_TILES, dtype=_np.float32),
        "rows_below": _np.triu(_np.ones((P, P), _np.float32), 1),
        "experts_before": _np.tril(_np.ones((EXPERTS, EXPERTS), _np.float32), -1).reshape(-1),
    }

    nc = _bacc.Bacc("TRN2", target_bir_lowering=False, num_devices=1)
    arrays, args = {}, {}
    for name, value in laid.items():
        arrays[f"in_{name}"] = _np.ascontiguousarray(value)
        args[name] = nc.dram_tensor(f"in_{name}", value.shape, _mybir.dt.from_np(value.dtype),
                                    kind="ExternalInput").ap()
    out = nc.dram_tensor("out", (BATCH, SEQ, D), _mybir.dt.float32, kind="ExternalOutput").ap()
    two_layer_program(nc, args, out)
    return _run(nc, [arrays], core_ids=[0]).results[0]["out"]
```

```python
from contextlib import ExitStack

import concourse.bass as bass
from concourse import mybir

F32 = mybir.dt.float32
F32R = mybir.dt.float32r
I32 = mybir.dt.int32
U32 = mybir.dt.uint32
ALU = mybir.AluOpType
ACT = mybir.ActivationFunctionType
AX = mybir.AxisListType

P = 128
BATCH, SEQ, D = 8, 256, 256
CTX_D = 192
NT = SEQ // P
KD = D // P
CTX_K = (P, CTX_D - P)
LN_EPS = 1e-5
RSQRT_MAGIC = float(0x5F3759DF)
NEWTON = 3
CREDIT = 2


def nth(n):
    return n + 1 + CREDIT


def two_before(n):
    return n + 1



def pair_loop(eng, step, peel_first=False):
    if peel_first:
        step(0, 0, False)
        step(0, 1, False)
    with eng.Fori(1 if peel_first else 0, BATCH // 2 - 1) as pair:
        step(pair, 0, False)
        step(pair, 1, False)
    step(BATCH // 2 - 1, 0, False)
    step(BATCH // 2 - 1, 1, True)


NEWTON_STEPS = 4 * NEWTON


def newton_rsqrt(pool, step_done, base, y, half_v, tmp, three_halves):
    for n in range(NEWTON):
        pool.tensor_tensor(tmp, y, y, ALU.mult).then_inc(step_done, 1)
        pool.wait_ge(step_done, base + 4 * n + 1)
        pool.tensor_tensor(tmp, tmp, half_v, ALU.mult).then_inc(step_done, 1)
        pool.wait_ge(step_done, base + 4 * n + 2)
        pool.tensor_tensor(tmp, tmp, three_halves, ALU.add).then_inc(step_done, 1)
        pool.wait_ge(step_done, base + 4 * n + 3)
        pool.tensor_tensor(y, y, tmp, ALU.mult).then_inc(step_done, 1)
        pool.wait_ge(step_done, base + 4 * n + 4)


STATS_STEPS = 4


def row_stats(dve, step_done, base, x, stats, mean_var, half_v, seed_bits, seed):
    for t in range(x.shape[1]):
        ins = dve.bn_stats(stats[:, t, :], x[:, t, :])
    ins.then_inc(step_done, 1)
    dve.wait_ge(step_done, base + 1)
    dve.memset(half_v, 0.0)
    for t in range(x.shape[1]):
        ins = dve.bn_aggr(mean_var[:, t, :], stats[:, t, :])
    ins.then_inc(step_done, 1)
    dve.wait_ge(step_done, base + 2)
    dve.tensor_scalar(half_v, mean_var[:, :, 1], LN_EPS, None, ALU.add).then_inc(step_done, 1)
    dve.wait_ge(step_done, base + 3)
    dve.tensor_scalar(seed_bits, half_v.bitcast(I32), 1, None, ALU.logical_shift_right).then_inc(step_done, 1)
    dve.wait_ge(step_done, base + 4)
    dve.tensor_scalar(half_v, half_v, -0.5, None, ALU.mult)
    return dve.tensor_scalar(seed.bitcast(I32), seed_bits, -1.0, RSQRT_MAGIC, ALU.mult, ALU.add)


def cross_attention(nc, tag, x_in, ctx_t, wq, wk, wv, wo, out_bias, x_out, ident_in, heads, head_dim,
                    q_bias=None, k_bias=None, v_bias=None, slots=None, routed=None):
    H = heads
    HPT = H // 4
    R = P // HPT
    INNER = heads * head_dim
    SCALE = float(head_dim) ** -0.5
    biased = q_bias is not None
    PRO = 7
    SIDE = PRO + 1

    with ExitStack() as ctx:
        def sb(name, shape, dt=F32):
            return ctx.enter_context(nc.sbuf_tensor(f"{tag}_{name}", shape, dt))

        def pb(name, shape):
            return ctx.enter_context(nc.psum_tensor(f"{tag}_{name}", shape, F32))

        def sem(name):
            return ctx.enter_context(nc.semaphore(f"{tag}_{name}"))

        ident = sb("ident", [P, P])
        wq_sb = sb("wq", [P, KD, 4 * P])
        wk_sb = sb("wk", [P, 2, 4 * P])
        wv_sb = sb("wv", [P, 2, INNER])
        wo_sb = sb("wo", [P, 4, D])
        obias = sb("obias", [P, D])
        if biased:
            qb_sb = sb("qb", [P, 4])
            kb_sb = sb("kb", [P, 4])
            vb_sb = sb("vb", [P, INNER])
        x_sb = [sb(f"x{i}", [P, NT, D]) for i in range(2)]
        if routed is not None:
            x_before, sorted_y, row_no, gate = routed
            CHOICES = len(gate)
            back = [[[sb(f"back{i}{t}{c}", [P, D]) for c in range(CHOICES)] for t in range(NT)] for i in range(2)]
            tick = sb("tick", [P, NT])
            place = [sb(f"place{i}", [P, CHOICES, NT], U32) for i in range(2)]
            placed = sem("placed")
            gathered = [sem(f"gathered{i}") for i in range(2)]
            first_added = sem("first_added")
            x_made = sem("x_made")
        c_sb = [sb(f"c{i}", [P, 2, SEQ]) for i in range(2)]
        xb_sb = [sb(f"xb{i}", [P, NT, D]) for i in range(2)]
        xo_sb = [sb(f"xo{i}", [P, NT, D]) for i in range(2)]
        xn_sb = [sb(f"xn{i}", [P, NT, D]) for i in range(2)]
        xnt_sb = sb("xnt", [P, KD, SEQ])
        q_sb = [sb(f"q{i}", [P, 4, SEQ]) for i in range(2)]
        k_sb = [sb(f"k{i}", [P, 4, SEQ]) for i in range(2)]
        v_sb = [sb(f"v{i}", [P, 2, INNER]) for i in range(2)]
        prob = [sb(f"prob{i}", [P, NT, SEQ]) for i in range(2)]
        prob_t = [sb(f"probt{i}", [P, 2, SEQ]) for i in range(2)]
        neg_max = [sb(f"nmax{i}", [P, NT]) for i in range(2)]
        row_sum = [sb(f"rsum{i}", [P, NT]) for i in range(2)]
        inv_sum = [sb(f"inv{i}", [P, NT]) for i in range(2)]
        ot_sb = sb("ot", [P, 4, SEQ])
        stats = sb("stats", [P, NT, 6])
        mean_var = sb("mv", [P, NT, 2])
        half_v = sb("halfv", [P, NT])
        seed_bits = sb("seedb", [P, NT], I32)
        rstd = sb("rstd", [P, NT])
        nwt = sb("nwt", [P, NT])
        three_halves = sb("three_halves", [P, NT])

        if slots is not None:
            slot_rows, slot_in, slot_gain, slot_bias, slot_scale = slots
            SR = slot_rows.shape[1]
            sg_sb = sb("sg", [P, D])
            sbias_sb = sb("sbias", [P, D])
            sscale_sb = sb("sscale", [P, 1])
            s_stats = sb("s_stats", [P, SR, 6])
            s_mv = sb("s_mv", [P, SR, 2])
            s_half_v = sb("s_halfv", [P, SR])
            s_seed_bits = sb("s_seedb", [P, SR], I32)
            s_rstd = sb("s_rstd", [P, SR])
            s_tmp = sb("s_tmp", [P, SR])
            s_three_halves = sb("s_three_halves", [P, SR])
            slots_loaded = sem("slots_loaded")
            slot_stats = sem("slot_stats")
            slot_step = sem("slot_step")

        score_ps = [pb(f"score{i}", [P, NT, SEQ]) for i in range(2)]
        trans_ps = [pb(f"trans{i}", [P, 2, SEQ]) for i in range(2)]
        out_ps = [pb(f"outp{i}", [P, 512]) for i in range(2)]
        side_ps = [pb(f"side{i}", [P, 512]) for i in range(2)]

        weights_in = sem("weights_in")
        if routed is None:
            x_loaded = [sem(f"x_loaded{i}") for i in range(2)]
        c_loaded = [sem(f"c_loaded{i}") for i in range(2)]
        constant_set = sem("constant_set")
        stats_step = sem("stats_step")
        seed_ready = sem("seed_ready")
        newton_step = sem("newton_step")
        xn_ready = sem("xn_ready")
        xn_turned = sem("xn_turned")
        c_used = sem("c_used")
        xb_ready = sem("xb_ready")
        side_full = [sem(f"side_full{i}") for i in range(2)]
        side_free = [sem(f"side_free{i}") for i in range(2)]
        if biased:
            qb_scaled = sem("qb_scaled")
        scores_done = sem("scores_done")
        max_done = sem("max_done")
        exp_done = sem("exp_done")
        turned = sem("turned")
        prob_t_ready = sem("prob_t_ready")
        pv_done = sem("pv_done")
        inv_ready = sem("inv_ready")
        prob_ready = sem("prob_ready")
        o_taken = sem("o_taken")
        xo_ready = sem("xo_ready")
        stored = [sem(f"stored{i}") for i in range(2)]

        x_dram = None if x_in is None else x_in.rearrange("b (t p) d -> b p t d", p=P)
        xo_dram = x_out.rearrange("b (t p) d -> b p t d", p=P)
        WEIGHTS = 16 * (8 + 3 * biased)

        TURNS = H + 4
        SIDE_IN = {5 + j * (H // 8): j for j in range(PRO)}
        PROJECT_AT = 1
        assert max(SIDE_IN) < TURNS and SIDE % 2 == 0

        FREE_STEPS = [[j for j in range(SIDE - 1) if j % 2 == bank] for bank in range(2)]
        FULL_STEPS = [[j for j in range(SIDE) if j % 2 == bank and j not in (0, PRO - 1)] for bank in range(2)]

        def count(steps, b, j):
            skipped = sum(x < PRO for x in steps) if isinstance(b, int) and b == BATCH - 1 else 0
            return len(steps) * (b + 1) + steps.index(j) + 1 - skipped

        def full(b, j):
            if j == 0:
                return xn_turned, nth(b + 1)
            if j == PRO - 1:
                return c_used, nth(b + 1)
            return side_full[j % 2], count(FULL_STEPS[j % 2], b, j)

        def emptied(b, j):
            if j == SIDE - 1:
                return xo_ready, nth(b)
            return side_free[j % 2], count(FREE_STEPS[j % 2], b, j)

        def before(b, j):
            if isinstance(b, int) and b == BATCH - 1 and j == PRO:
                return emptied(b - 1, SIDE - 1)
            if j >= 2:
                return emptied(b, j - 2)
            return None if isinstance(b, int) and b < 0 else emptied(b - 1, SIDE - 2 + j)

        def ready(b, j):
            return side_free[j % 2], len(FREE_STEPS[j % 2]) * b + FREE_STEPS[j % 2].index(j) + 1

        def has_batch_before(pair, s):
            return not (isinstance(pair, int) and pair == 0 and s == 0)

        def batch_before(pair, s):
            return (pair, 0) if s else (pair - 1, 1)

        def head_rows(h):
            return h // HPT, slice((h % HPT) * R, (h % HPT) * R + head_dim)

        block = ctx.enter_context(nc.Block())

        @block.sync
        def _(sp):
            sp.sem_inc(stored[0], 16)
            sp.sem_inc(stored[1], 16)

            def load(pair, s):
                b = 2 * pair + s
                if routed is None:
                    sp.wait_ge(xb_ready, two_before(b))
                    sp.dma_start(x_sb[s][:], x_dram[b]).then_inc(x_loaded[s], 16)
                sp.wait_ge(c_used, two_before(b))
                for k, rows in enumerate(CTX_K):
                    sp.dma_start(c_sb[s][0:rows, k, :], ctx_t[b, k * P:k * P + rows, :]).then_inc(c_loaded[s], 16)

            def store(pair, s):
                sp.wait_ge(xo_ready, nth(2 * pair + s))
                sp.dma_start(xo_dram[2 * pair + s], xo_sb[s][:]).then_inc(stored[s], 16)

            load(0, 0)
            sp.dma_start(ident[:], ident_in).then_inc(weights_in, 16)
            sp.dma_start(wq_sb[:], wq.rearrange("(k p) n -> p k n", p=P)).then_inc(weights_in, 16)
            for k, rows in enumerate(CTX_K):
                sp.dma_start(wk_sb[0:rows, k, :], wk[k * P:k * P + rows, :]).then_inc(weights_in, 16)
                sp.dma_start(wv_sb[0:rows, k, :], wv[k * P:k * P + rows, :]).then_inc(weights_in, 16)
            sp.dma_start(wo_sb[:], wo.rearrange("(k p) n -> p k n", p=P)).then_inc(weights_in, 16)
            sp.dma_start(obias[:], out_bias.partition_broadcast(P)).then_inc(weights_in, 16)
            if biased:
                sp.dma_start(qb_sb[:], q_bias).then_inc(weights_in, 16)
                sp.dma_start(kb_sb[:], k_bias).then_inc(weights_in, 16)
                sp.dma_start(vb_sb[:], v_bias.partition_broadcast(P)).then_inc(weights_in, 16)
            load(0, 1)
            if slots is not None:
                sp.dma_start(slot_rows[:], slot_in.rearrange("e s d -> (e s) d").rearrange("(t p) d -> p t d", p=P))\
                  .then_inc(slots_loaded, 16)
                sp.dma_start(sg_sb[:], slot_gain.partition_broadcast(P)).then_inc(slots_loaded, 16)
                sp.dma_start(sbias_sb[:], slot_bias.partition_broadcast(P)).then_inc(slots_loaded, 16)
                sp.dma_start(sscale_sb[:], slot_scale.partition_broadcast(P)).then_inc(slots_loaded, 16)
            with sp.Fori(0, BATCH // 2 - 1) as pair:
                for s in range(2):
                    load(pair + 1, s)
                    store(pair, s)
            for s in range(2):
                store(BATCH // 2 - 1, s)
            for s in range(2):
                sp.wait_ge(stored[s], 16 * (BATCH // 2 + 1))

        @block.gpsimd
        def _(pool):
            pool.sem_inc(xb_ready, CREDIT)
            pool.memset(ot_sb[:], 0.0)
            if slots is not None:
                pool.memset(s_three_halves[:], 1.5)
            pool.memset(three_halves[:], 1.5).then_inc(constant_set, 1)
            pool.wait_ge(constant_set, 1)

            def gather(pair, s):
                pool.wait_ge(placed, 2 * pair + s + 1)
                if not isinstance(pair, int):
                    pool.tensor_tensor(tick[:], three_halves[:], three_halves[:], ALU.mult)
                for t in range(NT):
                    for c in range(CHOICES):
                        pool.indirect_dma_start(back[s][t][c][:], None, sorted_y,
                                                bass.IndirectOffsetOnAxis(place[s][:, c, t:t + 1], 0))\
                            .then_inc(gathered[s], 16)

            def normalise(pair, s):
                b = 2 * pair + s
                pool.wait_ge(seed_ready, b + 1)
                newton_rsqrt(pool, newton_step, NEWTON_STEPS * b, rstd[:], half_v[:], nwt[:],
                             three_halves[:])
                pool.wait_ge(xn_turned, two_before(b))
                pool.wait_ge(xo_ready, two_before(b))
                pool.tensor_tensor(nwt[:], nwt[:], nwt[:], ALU.mult)
                for t in range(NT):
                    ins = pool.tensor_scalar(xn_sb[s][:, t, :], x_sb[s][:, t, :], mean_var[:, t, 0:1],
                                             rstd[:, t:t + 1], ALU.subtract, ALU.mult)
                ins.then_inc(xn_ready, 1)
                pool.wait_ge(weights_in, WEIGHTS)
                pool.tensor_tensor(xb_sb[s][:], x_sb[s][:], obias[:].unsqueeze(1).to_broadcast([P, NT, D]),
                                   ALU.add).then_inc(xb_ready, 1)

            if routed is None:
                with pool.Fori(0, BATCH // 2) as pair:
                    normalise(pair, 0)
                    normalise(pair, 1)
            else:
                gather(0, 0)
                with pool.Fori(0, BATCH // 2 - 1) as pair:
                    normalise(pair, 0)
                    gather(pair, 1)
                    normalise(pair, 1)
                    gather(pair + 1, 0)
                normalise(BATCH // 2 - 1, 0)
                gather(BATCH // 2 - 1, 1)
                normalise(BATCH // 2 - 1, 1)

            if slots is not None:
                pool.wait_ge(slot_stats, STATS_STEPS + 1)
                newton_rsqrt(pool, slot_step, 0, s_rstd[:], s_half_v[:], s_tmp[:], s_three_halves[:])
                for t in range(SR):
                    ins = pool.tensor_scalar(slot_rows[:, t, :], slot_rows[:, t, :], s_mv[:, t, 0:1],
                                             s_rstd[:, t:t + 1], ALU.subtract, ALU.mult)
                ins.then_inc(slot_step, 1)
                pool.wait_ge(slot_step, NEWTON_STEPS + 1)
                pool.tensor_tensor(slot_rows[:], slot_rows[:], sg_sb[:].unsqueeze(1).to_broadcast([P, SR, D]),
                                   ALU.mult).then_inc(slot_step, 1)
                pool.wait_ge(slot_step, NEWTON_STEPS + 2)
                pool.tensor_tensor(slot_rows[:], slot_rows[:],
                                   sbias_sb[:].unsqueeze(1).to_broadcast([P, SR, D]), ALU.add)\
                    .then_inc(slot_step, 1)
                pool.wait_ge(slot_step, NEWTON_STEPS + 3)
                pool.tensor_scalar(slot_rows[:], slot_rows[:], sscale_sb[:], None, ALU.mult)

        @block.scalar
        def _(act):
            act.sem_inc(exp_done, CREDIT)
            act.sem_inc(o_taken, CREDIT)

            def side(pair, s, j):
                b = 2 * pair + s
                bank = j % 2
                if j == 0:
                    act.wait_ge(*full(b, j))
                    act.activation(xnt_sb[:].rearrange("p k n -> p (k n)"), side_ps[bank][:], ACT.Copy)\
                       .then_inc(side_free[bank], 1)
                elif j in (1, 2):
                    act.wait_ge(*full(b, j))
                    q = q_sb[1 - s][:, 2 * (j - 1):2 * j, :]
                    if biased:
                        for n in range(2):
                            m = 2 * (j - 1) + n
                            ins = act.activation(q[:, n, :], side_ps[bank][:, n * SEQ:(n + 1) * SEQ],
                                                 ACT.Identity, bias=qb_sb[:, m:m + 1], scale=SCALE)
                    else:
                        ins = act.activation(q.rearrange("p k n -> p (k n)"), side_ps[bank][:], ACT.Copy,
                                             scale=SCALE)
                    ins.then_inc(side_free[bank], 1)

            def step(pair, s, last):
                b = 2 * pair + s
                for i in range(TURNS):
                    if i < H:
                        u = H * b + i
                        act.wait_ge(max_done, u + 1)
                        act.wait_ge(turned, two_before(u))
                        for t in range(NT):
                            ins = act.activation(prob[i % 2][:, t, :], score_ps[i % 2][:, t, :], ACT.Exp,
                                                 bias=neg_max[i % 2][:, t:t + 1],
                                                 accum_out=row_sum[i % 2][:, t:t + 1])
                        ins.then_inc(exp_done, 1)
                    if i in SIDE_IN and not last:
                        side(pair, s, SIDE_IN[i])
                    if 0 <= i - 4 < H:
                        h = i - 4
                        m, rows = head_rows(h)
                        act.wait_ge(pv_done, nth(H * b + h))
                        act.activation(ot_sb[rows, m, :], out_ps[h % 2][rows, 0:SEQ], ACT.Copy)\
                           .then_inc(o_taken, 1)

            if biased:
                act.wait_ge(qb_scaled, 1)
            for j in range(PRO):
                side(-1, 1, j)
            act.wait_ge(constant_set, 1)
            pair_loop(act, step, peel_first=True)

        @block.tensor
        def _(pe):
            pe.sem_inc(c_used, CREDIT)
            pe.sem_inc(xn_turned, CREDIT)
            pe.sem_inc(turned, CREDIT)
            pe.sem_inc(pv_done, CREDIT)
            pe.wait_ge(weights_in, WEIGHTS)

            def side(pair, s, j):
                b = 2 * pair + s
                n, o = b + 1, 1 - s
                nth_of_slot = pair + s
                ps = side_ps[j % 2]
                if before(b, j) is not None:
                    pe.wait_ge(*before(b, j))
                if j == 0:
                    pe.wait_ge(xn_ready, n + 1)
                    for k in range(KD):
                        for t in range(NT):
                            ins = pe.transpose(ps[:, k * SEQ + t * P:k * SEQ + (t + 1) * P],
                                               xn_sb[o][:, t, k * P:(k + 1) * P], ident[:])
                elif j in (1, 2):
                    pe.wait_ge(*emptied(b, 0))
                    for m in range(2):
                        col = (2 * (j - 1) + m) * P
                        for k in range(KD):
                            ins = pe.matmul(ps[:, m * SEQ:(m + 1) * SEQ], wq_sb[:, k, col:col + P],
                                            xnt_sb[:, k, :], start=(k == 0), stop=(k == KD - 1))
                elif j in (3, 4):
                    pe.wait_ge(c_loaded[o], 32 * (nth_of_slot + 1))
                    for m in range(2):
                        col = (2 * (j - 3) + m) * P
                        for k, rows in enumerate(CTX_K):
                            ins = pe.matmul(ps[:, m * SEQ:(m + 1) * SEQ], wk_sb[0:rows, k, col:col + P],
                                            c_sb[o][0:rows, k, :], start=(k == 0), stop=(k == 1))
                elif j in (5, 6):
                    m = j - 5
                    for k, rows in enumerate(CTX_K):
                        ins = pe.matmul(ps[:, 0:INNER], c_sb[o][0:rows, k, m * P:(m + 1) * P],
                                        wv_sb[0:rows, k, :], start=(k == 0), stop=(k == 1))
                else:
                    pe.wait_ge(o_taken, nth(H * b + H - 1))
                    for t in range(NT):
                        for k in range(4):
                            ins = pe.matmul(ps[:, t * D:(t + 1) * D], ot_sb[:, k, t * P:(t + 1) * P],
                                            wo_sb[:, k, :], start=(k == 0), stop=(k == 3))
                ins.then_inc(full(b, j)[0], 1)

            def step(pair, s, last):
                b = 2 * pair + s
                for i in range(TURNS):
                    if i < H:
                        u = H * b + i
                        if i == 0:
                            for j in (3, 4):
                                pe.wait_ge(*ready(b, j))
                        pe.wait_ge(exp_done, two_before(u))
                        m, r = i // HPT, (i % HPT) * R
                        for t in range(NT):
                            ins = pe.matmul(score_ps[i % 2][:, t, :], q_sb[s][r:r + R, m, t * P:(t + 1) * P],
                                            k_sb[s][r:r + R, m, :], start=True, stop=True)
                        ins.then_inc(scores_done, 1)
                    if i == PROJECT_AT and has_batch_before(pair, s):
                        side(*batch_before(pair, s), PRO)
                    if i in SIDE_IN and not last:
                        side(pair, s, SIDE_IN[i])
                    if 0 <= i - 2 < H:
                        h = i - 2
                        u = H * b + h
                        pe.wait_ge(prob_ready, u + 1)
                        pe.wait_ge(prob_t_ready, two_before(u))
                        for k in range(2):
                            for t in range(NT):
                                ins = pe.transpose(trans_ps[h % 2][:, k, t * P:(t + 1) * P],
                                                   prob[h % 2][:, t, k * P:(k + 1) * P], ident[:])
                        ins.then_inc(turned, 1)
                    if 0 <= i - 3 < H:
                        h = i - 3
                        u = H * b + h
                        _, rows = head_rows(h)
                        if h == 0:
                            for j in (5, 6):
                                pe.wait_ge(*ready(b, j))
                        pe.wait_ge(o_taken, two_before(u))
                        pe.wait_ge(prob_t_ready, nth(u))
                        for k in range(2):
                            ins = pe.matmul(out_ps[h % 2][rows, 0:SEQ],
                                            v_sb[s][:, k, h * head_dim:(h + 1) * head_dim],
                                            prob_t[h % 2][:, k, :], start=(k == 0), stop=(k == 1))
                        ins.then_inc(pv_done, 1)

            for j in range(PRO):
                side(-1, 1, j)
            pe.wait_ge(side_free[PRO % 2], len(FREE_STEPS[PRO % 2]))
            pe.sem_inc(side_full[PRO % 2], 1)
            pair_loop(pe, step, peel_first=True)
            side(BATCH // 2 - 1, 1, PRO)

        @block.vector
        def _(dve):
            dve.sem_inc(prob_t_ready, CREDIT)
            dve.sem_inc(xo_ready, CREDIT)

            def place_rows(n, slot):
                for c in range(CHOICES):
                    ins = dve.tensor_copy(place[slot][:, c, :], row_no[c][:, bass.ts(n, NT)])
                ins.then_inc(placed, 1)

            def statistics(pair, s):
                n, o = 2 * pair + s + 1, 1 - s
                if routed is None:
                    dve.wait_ge(x_loaded[o], 16 * (pair + s + 1))
                else:
                    dve.wait_ge(gathered[o], 16 * NT * CHOICES * (pair + s + 1))
                    dve.wait_ge(xb_ready, two_before(n))
                    for c in range(CHOICES):
                        if c == 1:
                            dve.wait_ge(first_added, n + 1)
                        for t in range(NT):
                            tile = n * NT + t
                            x = x_sb[o][:, t, :]
                            before_x = x_before[:, bass.ds(tile, 1), :].rearrange("p a d -> p (a d)")
                            ins = dve.scalar_tensor_tensor(x, back[o][t][c][:], gate[c][:, bass.ds(tile, 1)],
                                                           before_x if c == 0 else x, ALU.mult, ALU.add)
                        ins.then_inc(first_added if c == 0 else x_made, 1)
                    dve.wait_ge(x_made, n + 1)
                    if not (isinstance(n, int) and n == BATCH - 1):
                        place_rows(n + 1, s)
                if not (isinstance(n, int) and n == 0):
                    dve.wait_ge(xn_ready, n)
                row_stats(dve, stats_step, STATS_STEPS * n, x_sb[o][:], stats[:], mean_var[:], half_v[:],
                          seed_bits[:], rstd[:]).then_inc(seed_ready, 1)

            def side(pair, s, j):
                b = 2 * pair + s
                o = 1 - s
                bank = j % 2
                ps = side_ps[bank]
                if j in (3, 4):
                    dve.wait_ge(*full(b, j))
                    k = k_sb[o][:, 2 * (j - 3):2 * (j - 3) + 2, :]
                    if biased:
                        for n in range(2):
                            m = 2 * (j - 3) + n
                            ins = dve.tensor_scalar(k[:, n, :], ps[:, n * SEQ:(n + 1) * SEQ],
                                                    kb_sb[:, m:m + 1], None, ALU.add)
                    else:
                        ins = dve.tensor_copy(k.rearrange("p k n -> p (k n)"), ps[:])
                    ins.then_inc(side_free[bank], 1)
                elif j in (5, 6):
                    dve.wait_ge(*full(b, j))
                    if biased:
                        ins = dve.tensor_tensor(v_sb[o][:, j - 5, :], ps[:, 0:INNER], vb_sb[:], ALU.add)
                    else:
                        ins = dve.tensor_copy(v_sb[o][:, j - 5, :], ps[:, 0:INNER])
                    ins.then_inc(side_free[bank], 1)
                elif j == SIDE - 1:
                    dve.wait_ge(*full(b, j))
                    dve.wait_ge(xb_ready, nth(b))
                    dve.wait_ge(stored[s], 16 * pair + 16)
                    dve.tensor_tensor(xo_sb[s][:].rearrange("p t d -> p (t d)"), ps[:],
                                      xb_sb[s][:].rearrange("p t d -> p (t d)"), ALU.add)\
                       .then_inc(xo_ready, 1)

            def step(pair, s, last):
                b = 2 * pair + s
                for i in range(TURNS):
                    if i < H:
                        u = H * b + i
                        dve.wait_ge(scores_done, u + 1)
                        dve.tensor_reduce(neg_max[i % 2][:], score_ps[i % 2][:], AX.X, ALU.max, negate=True)\
                           .then_inc(max_done, 1)
                    if 0 <= i - 1 < H:
                        h = i - 1
                        u = H * b + h
                        dve.wait_ge(exp_done, nth(u))
                        dve.reciprocal(inv_sum[h % 2][:], row_sum[h % 2][:]).then_inc(inv_ready, 1)
                        dve.wait_ge(inv_ready, u + 1)
                        for t in range(NT):
                            ins = dve.tensor_scalar(prob[h % 2][:, t, :], prob[h % 2][:, t, :],
                                                    inv_sum[h % 2][:, t:t + 1], None, ALU.mult)
                        ins.then_inc(prob_ready, 1)
                    if i == 0 and not last:
                        statistics(pair, s)
                    if i == PROJECT_AT and has_batch_before(pair, s):
                        side(*batch_before(pair, s), PRO)
                    if i in SIDE_IN and not last:
                        side(pair, s, SIDE_IN[i])
                    if 0 <= i - 2 < H:
                        h = i - 2
                        u = H * b + h
                        dve.wait_ge(turned, nth(u))
                        dve.wait_ge(pv_done, two_before(u))
                        dve.tensor_copy(prob_t[h % 2][:], trans_ps[h % 2][:]).then_inc(prob_t_ready, 1)

            if routed is not None:
                place_rows(0, 0)
            statistics(-1, 1)
            dve.wait_ge(weights_in, WEIGHTS)
            if biased:
                dve.tensor_scalar(qb_sb[:], qb_sb[:], SCALE, None, ALU.mult).then_inc(qb_scaled, 1)
            for j in range(PRO):
                side(-1, 1, j)
            if slots is not None:
                dve.wait_ge(slots_loaded, 64)
                row_stats(dve, slot_stats, 0, slot_rows[:], s_stats[:], s_mv[:], s_half_v[:], s_seed_bits[:],
                          s_rstd[:]).then_inc(slot_stats, 1)
            pair_loop(dve, step, peel_first=True)
            side(BATCH // 2 - 1, 1, PRO)

EXPERTS, HID = 8, 1024
CHOICES = 2
TILES = BATCH * NT
TOKENS = TILES * P
DENOM_MIN = 1e-9
ROW_TILES = (CHOICES * TOKENS + CHOICES * (P - 1) + (EXPERTS - CHOICES) * P) // P


def routed_experts(nc, tag, x_in, w_gate, w_gate_up, w_down, ident_in, iota_in, tiles_in, below_in,
                   before_in, routed):
    FT = HID // P
    HH = HID // 2
    PIECE = 2 * HID
    PIECES = KD + 1
    SLOT = PIECES * PIECE
    T = ROW_TILES
    GROUPS = TILES // 2
    assert FT * D == PIECE and T % 2 == 1

    with ExitStack() as ctx:
        def sb(name, shape, dt=F32):
            return ctx.enter_context(nc.sbuf_tensor(f"{tag}_{name}", shape, dt))

        def pb(name, shape):
            return ctx.enter_context(nc.psum_tensor(f"{tag}_{name}", shape, F32))

        def sem(name):
            return ctx.enter_context(nc.semaphore(f"{tag}_{name}"))

        sorted_x = nc.dram_tensor(f"{tag}_sorted_x", (T * P, D), F32, kind="Internal").ap()
        x_sb, sorted_y, row_no, gate = routed

        ident = sb("ident", [P, P])
        below = sb("below", [P, P])
        ones = sb("ones", [P, P])
        zeros = sb("zeros", [P, D])
        iota = sb("iota", [P, EXPERTS])
        tile_no = sb("tile_no", [1, T])
        before = sb("before", [P, EXPERTS, EXPERTS])
        wg_sb = sb("wg", [P, KD, EXPERTS])
        xn_sb = sb("xn", [P, TILES, D])
        xt_sb = [sb(f"xt{i}", [P, 2, KD, P]) for i in range(2)]
        stats = sb("stats", [P, TILES, 6])
        mean_var = sb("mv", [P, TILES, 2])
        half_v = sb("halfv", [P, TILES])
        seed_bits = sb("seedb", [P, TILES], I32)
        rstd = sb("rstd", [P, TILES])
        nwt = sb("nwt", [P, TILES])
        three_halves = sb("three_halves", [P, TILES])
        ex = sb("ex", [P, TILES, EXPERTS])
        left = sb("left", [P, TILES, EXPERTS])
        mask = [sb(f"mask{i}", [P, TILES, EXPERTS]) for i in range(CHOICES)]
        both = sb("both", [P, TILES, EXPERTS])
        cand = sb("cand", [P, TILES, EXPERTS])
        place = sb("place", [P, TILES, EXPERTS])
        red = sb("red", [P, TILES])
        own_count = sb("own_count", [P, EXPERTS])
        count_i = sb("count_i", [P, EXPERTS], I32)
        count_f = sb("count_f", [P, EXPERTS])
        earlier = sb("earlier", [P, EXPERTS, EXPERTS])
        start = sb("start", [P, EXPERTS])
        start_row = sb("start_row", [P, EXPERTS])
        start_halves = sb("start_halves", [1, EXPERTS], I32)
        begun = sb("begun", [1, T, EXPERTS])
        begun_count = sb("begun_count", [1, T])
        begun_i = sb("begun_i", [1, T], I32)
        tile_pieces = sb("tile_pieces", [1, T], I32)
        tile_slot = sb("tile_slot", [1, T], I32)

        w_hi = sb("w_hi", [P, 2 * SLOT], F32R)
        w_lo = sb("w_lo", [P, 2 * SLOT], F32R)
        stage = [sb(f"stage{i}", [P, PIECE]) for i in range(2)]
        row_sb = [sb(f"rows{i}", [P, D]) for i in range(2)]
        rt_hi = [sb(f"rt_hi{i}", [P, KD, P], F32R) for i in range(2)]
        rt_lo = [sb(f"rt_lo{i}", [P, KD, P], F32R) for i in range(2)]
        silu = [sb(f"silu{i}", [P, HH]) for i in range(2)]
        prod = [sb(f"prod{i}", [P, HH]) for i in range(2)]
        ht_hi = [sb(f"ht_hi{i}", [P, HH // P, P], F32R) for i in range(2)]
        ht_lo = [sb(f"ht_lo{i}", [P, HH // P, P], F32R) for i in range(2)]
        y_sb = [sb(f"y{i}", [P, D]) for i in range(2)]
        tick = sb("tick", [P, 1])

        g_ps = [pb(f"g{i}", [P, HH]) for i in range(2)]
        u_ps = [pb(f"u{i}", [P, HH]) for i in range(2)]
        ht_ps = [pb(f"ht{i}", [P, HH // P, P]) for i in range(2)]
        y_ps = pb("yp", [P, 512])
        rt_ps = pb("rt", [P, KD, P])

        constants_in = sem("constants_in")
        x_loaded = sem("x_loaded")
        pool_set = sem("pool_set")
        zeroed = sem("zeroed")
        stats_step = sem("stats_step")
        newton_step = sem("newton_step")
        xn_ready = sem("xn_ready")
        turned = sem("turned")
        xt_copied = sem("xt_copied")
        logits_done = sem("logits_done")
        gate_step = sem("gate_step")
        chosen = sem("chosen")
        ranked = sem("ranked")
        tables_ready = sem("tables_ready")
        scattered = sem("scattered")
        staged = [sem(f"staged{i}") for i in range(2)]
        split_hi = sem("split_hi")
        split_done = sem("split_done")
        rows_in = [sem(f"rows_in{i}") for i in range(2)]
        rows_turned = sem("rows_turned")
        rt_hi_done = sem("rt_hi_done")
        rt_lo_done = sem("rt_lo_done")
        gu_done = sem("gu_done")
        silu_done = sem("silu_done")
        prod_done = sem("prod_done")
        h_turned = sem("h_turned")
        ht_hi_done = sem("ht_hi_done")
        ht_lo_done = sem("ht_lo_done")
        down_done = sem("down_done")
        y_copied = sem("y_copied")
        y_stored = [sem(f"y_stored{i}") for i in range(2)]

        CONSTANTS = 16 * 6
        PIECE_AT = {4: 2 * PIECES - 1, 8: 2 * PIECES, 12: 2 * PIECES + 1}
        x_dram = x_in.rearrange("b (t p) d -> p (b t) d", p=P)
        trans_banks = [g_ps[0], g_ps[1], u_ps[0], u_ps[1]]

        block = ctx.enter_context(nc.Block())

        def tile_loop(eng, step):
            step(0, 0, 0)
            with eng.Fori(0, (T - 3) // 2) as pair:
                step(2 * pair + 1, 1, pair)
                step(2 * pair + 2, 0, pair + 1)
            step(T - 2, (T - 2) % 2, (T - 2) // 2)
            step(T - 1, (T - 1) % 2, (T - 1) // 2)

        def is_tile(i, n):
            return isinstance(i, int) and i == n

        @block.sync
        def _(sp):
            sp.dma_start(x_sb[:], x_dram).then_inc(x_loaded, 16)
            sp.dma_start(ident[:], ident_in).then_inc(constants_in, 16)
            sp.dma_start(below[:], below_in).then_inc(constants_in, 16)
            sp.dma_start(iota[:], iota_in.partition_broadcast(P)).then_inc(constants_in, 16)
            sp.dma_start(tile_no[:], tiles_in.unsqueeze(0)).then_inc(constants_in, 16)
            sp.dma_start(before[:].rearrange("p a b -> p (a b)"), before_in.partition_broadcast(P))\
              .then_inc(constants_in, 16)
            sp.dma_start(wg_sb[:], w_gate.rearrange("(k p) e -> p k e", p=P)).then_inc(constants_in, 16)
            sp.wait_ge(pool_set, 1)
            sp.dma_start(sorted_x.rearrange("(t p) d -> p t d", p=P),
                         zeros[:].unsqueeze(1).to_broadcast([P, T, D])).then_inc(zeroed, 16)
            sp.sem_inc(y_stored[0], 16)
            sp.sem_inc(y_stored[1], 16)

            def load(i, par):
                sp.dma_start(row_sb[par][:], sorted_x[bass.ts(i, P), :]).then_inc(rows_in[par], 16)

            def store(i, par):
                sp.wait_ge(y_copied, i + 1)
                sp.dma_start(sorted_y[bass.ts(i, P), :], y_sb[par][:]).then_inc(y_stored[par], 16)

            def step(i, par, half):
                if not (isinstance(i, int) and i > T - 3):
                    sp.wait_ge(rows_turned, i + 1)
                    load(i + 2, par)
                if not is_tile(i, 0):
                    store(i - 1, 1 - par)

            sp.wait_ge(scattered, 16 * CHOICES * TILES)
            load(0, 0)
            load(1, 1)
            tile_loop(sp, step)
            store(T - 1, (T - 1) % 2)
            for par in range(2):
                sp.wait_ge(y_stored[par], 16 * ((T + 1 - par) // 2 + 1))

        @block.gpsimd
        def _(pool):
            pool.memset(zeros[:], 0.0).then_inc(pool_set, 1)
            pool.memset(ones[:], 1.0)
            pool.memset(tick[:], 0.0)
            pool.memset(three_halves[:], 1.5).then_inc(pool_set, 1)

            def load_piece(e, i, slot):
                if i < KD:
                    pool.dma_start(stage[slot][:], w_gate_up[e, i * P:(i + 1) * P, :]).then_inc(staged[slot], 16)
                else:
                    pool.dma_start(stage[slot][:].rearrange("p (f d) -> p f d", d=D),
                                   w_down[e].rearrange("(f p) d -> p f d", p=P)).then_inc(staged[slot], 16)

            def split(pair, s, reuse, last=False):
                e = 2 * pair + s
                if reuse:
                    halves = pool.value_load(start_halves[0:1, bass.ds(e - 1, 1)], min_val=2, max_val=2 * T)
                    pool.wait_ge(gu_done, halves)
                for i in range(PIECES):
                    if reuse and i == KD:
                        pool.wait_ge(down_done, halves)
                    n = e * PIECES + i
                    slot = (s * PIECES + i) % 2
                    cols = slice(s * SLOT + i * PIECE, s * SLOT + (i + 1) * PIECE)
                    pool.wait_ge(staged[slot], 16 * (PIECES * pair + (s * PIECES + i) // 2 + 1))
                    pool.tensor_tensor(tick[:], tick[:], tick[:], ALU.mult)
                    pool.tensor_copy(w_hi[:, cols], stage[slot][:]).then_inc(split_hi, 1)
                    pool.wait_ge(split_hi, n + 1)
                    pool.tensor_tensor(w_lo[:, cols], stage[slot][:], w_hi[:, cols].bitcast(F32),
                                       ALU.subtract).then_inc(split_done, 1)
                    if not (last and i + 2 >= PIECES):
                        pool.wait_ge(split_done, n + 1)
                        load_piece(e + (i + 2) // PIECES, (i + 2) % PIECES, slot)

            load_piece(0, 0, 0)
            load_piece(0, 1, 1)
            pool.wait_ge(pool_set, 2)
            pool.wait_ge(stats_step, STATS_STEPS + 1)
            newton_rsqrt(pool, newton_step, 0, rstd[:], half_v[:], nwt[:], three_halves[:])
            split(0, 0, False)
            pool.wait_ge(zeroed, 16)
            pool.wait_ge(xn_ready, GROUPS)
            pool.wait_ge(tables_ready, 1)
            for t in range(TILES):
                if t in PIECE_AT:
                    n = PIECE_AT[t]
                    pool.wait_ge(split_done, n - 1)
                    load_piece(n // PIECES, n % PIECES, n % 2)
                for c in range(CHOICES):
                    pool.indirect_dma_start(sorted_x, bass.IndirectOffsetOnAxis(row_no[c][:, t:t + 1], 0),
                                            xn_sb[:, t, :], None).then_inc(scattered, 16)
            pool.wait_ge(split_done, 2 * PIECES)
            pool.wait_ge(tables_ready, 2)
            with pool.Fori(1, EXPERTS // 2 - 1) as pair:
                for s in range(2):
                    split(pair, s, True)
            for s in range(2):
                split(EXPERTS // 2 - 1, s, True, last=(s == 1))

        @block.scalar
        def _(act):
            for j in range(GROUPS):
                act.wait_ge(turned, j + 1)
                if j >= 2:
                    act.wait_ge(logits_done, j - 1)
                act.activation(xt_sb[j % 2][:].rearrange("p t k n -> p (t k n)"), trans_banks[j % 4][:], ACT.Copy)\
                   .then_inc(xt_copied, 1)
            act.wait_ge(gate_step, 2)
            act.activation(ex[:], ex[:], ACT.Exp).then_inc(xt_copied, 1)
            act.wait_ge(split_done, PIECES)
            for n in range(PIECES, 2 * PIECES):
                act.wait_ge(staged[n % 2], 16 * (n // 2 + 1))
                act.activation(w_hi[:, n * PIECE:(n + 1) * PIECE], stage[n % 2][:], ACT.Copy)\
                   .then_inc(split_hi, 1)

            def split_rows(i, par):
                act.wait_ge(rows_turned, i + 1)
                if not (isinstance(i, int) and i < 2):
                    act.wait_ge(gu_done, 2 * i - 2)
                act.activation(rt_hi[par][:], rt_ps[:], ACT.Copy).then_inc(rt_hi_done, 1)

            def split_hidden(i, h):
                act.wait_ge(h_turned, 2 * i + h + 1)
                act.activation(ht_hi[h][:], ht_ps[h][:], ACT.Copy).then_inc(ht_hi_done, 1)

            def take_output(i, par, half):
                act.wait_ge(down_done, 2 * i + 2)
                act.wait_ge(y_stored[par], 16 * (half + 1))
                act.activation(y_sb[par][:], y_ps[:, 0:D], ACT.Copy).then_inc(y_copied, 1)

            def gate_half(i, h):
                act.wait_ge(gu_done, 2 * i + h + 1)
                if not is_tile(i, 0):
                    act.wait_ge(prod_done, 2 * i + h - 1)
                act.activation(silu[h][:], g_ps[h][:], ACT.Silu).then_inc(silu_done, 1)

            def step(i, par, half):
                gate_half(i, 0)
                if not is_tile(i, T - 1):
                    split_rows(i + 1, 1 - par)
                if not is_tile(i, 0):
                    split_hidden(i - 1, 1)
                gate_half(i, 1)
                split_hidden(i, 0)
                if not is_tile(i, 0):
                    take_output(i - 1, 1 - par, half - 1 + par)

            split_rows(0, 0)
            tile_loop(act, step)
            split_hidden(T - 1, 1)
            take_output(T - 1, (T - 1) % 2, (T - 1) // 2)

        @block.tensor
        def _(pe):
            def three_passes(out, a_hi, a_lo, b_hi, b_lo, start, stop):
                pe.matmul(out, a_hi, b_hi, start=start, stop=False)
                pe.matmul(out, a_lo, b_hi, start=False, stop=False)
                return pe.matmul(out, a_hi, b_lo, start=False, stop=stop)

            pe.wait_ge(constants_in, CONSTANTS)
            pe.wait_ge(pool_set, 2)

            def logits(j):
                pe.wait_ge(xt_copied, j + 1)
                for t in range(2):
                    tile = 2 * j + t
                    for k in range(KD):
                        ins = pe.matmul(y_ps[:, tile * EXPERTS:(tile + 1) * EXPERTS], xt_sb[j % 2][:, t, k, :],
                                        wg_sb[:, k, :], start=(k == 0), stop=(k == KD - 1))
                ins.then_inc(logits_done, 1)

            for j in range(GROUPS):
                pe.wait_ge(xn_ready, j + 1)
                if j >= 4:
                    pe.wait_ge(xt_copied, j - 3)
                bank = trans_banks[j % 4]
                for t in range(2):
                    for k in range(KD):
                        first = (t * KD + k) * P
                        ins = pe.transpose(bank[:, first:first + P], xn_sb[:, 2 * j + t, k * P:(k + 1) * P],
                                           ident[:])
                ins.then_inc(turned, 1)
                if j >= 1:
                    logits(j - 1)
            logits(GROUPS - 1)

            rank = ht_ps[0][:].rearrange("p a b -> p (a b)")
            flat = both[:].rearrange("p t e -> p (t e)")
            pe.wait_ge(chosen, 1)
            pe.matmul(rank[:, 0:TILES * EXPERTS], below[:], flat, start=True, stop=False, skip_group_check=True)
            for back_by in range(1, TILES):
                ins = pe.matmul(rank[:, back_by * EXPERTS:TILES * EXPERTS], ones[:],
                                flat[:, 0:(TILES - back_by) * EXPERTS], start=False, stop=(back_by == TILES - 1),
                                skip_group_check=True)
            pe.wait_ge(chosen, 2)
            pe.matmul(ht_ps[1][:, 0, 0:EXPERTS], ones[:], own_count[:], start=True, stop=True)\
              .then_inc(ranked, 1)
            pe.wait_ge(tables_ready, 2)

            def first_column(i):
                return pe.value_load(tile_slot[0:1, bass.ds(i, 1)], min_val=0, max_val=SLOT)

            def pieces_split(i):
                return pe.value_load(tile_pieces[0:1, bass.ds(i, 1)], min_val=KD, max_val=PIECES * EXPERTS)

            def turn_rows(i, par, half):
                pe.wait_ge(rows_in[par], 16 * (half + 1))
                if not is_tile(i, 0):
                    pe.wait_ge(rt_lo_done, i)
                for k in range(KD):
                    ins = pe.transpose(rt_ps[:, k, :], row_sb[par][:, k * P:(k + 1) * P], ident[:])
                ins.then_inc(rows_turned, 1)

            def gate_up(i, par, h, w):
                if h == 0:
                    pieces = pieces_split(i)
                    pe.wait_ge(rt_lo_done, i + 1)
                    pe.wait_ge(split_done, pieces)
                if not is_tile(i, 0):
                    pe.wait_ge(prod_done, 2 * i + h - 1)
                for ps, first in ((g_ps[h], h * HH), (u_ps[h], HID + h * HH)):
                    for k in range(KD):
                        cols = bass.ds(w + (k * PIECE + first), HH)
                        ins = three_passes(ps[:], rt_hi[par][:, k, :], rt_lo[par][:, k, :], w_hi[:, cols],
                                           w_lo[:, cols], k == 0, k == KD - 1)
                ins.then_inc(gu_done, 1)

            def turn_hidden(i, h):
                pe.wait_ge(prod_done, 2 * i + h + 1)
                if not is_tile(i, 0):
                    pe.wait_ge(ht_lo_done, 2 * i + h - 1)
                for f in range(HH // P):
                    ins = pe.transpose(ht_ps[h][:, f, :], prod[h][:, f * P:(f + 1) * P], ident[:])
                ins.then_inc(h_turned, 1)

            def down(i, h, w):
                if h == 0:
                    pe.wait_ge(split_done, pieces_split(i) + 1)
                pe.wait_ge(ht_lo_done, 2 * i + h + 1)
                if h == 0 and not is_tile(i, 0):
                    pe.wait_ge(y_copied, i)
                for f in range(HH // P):
                    cols = bass.ds(w + (KD * PIECE + (h * HH // P + f) * D), D)
                    ins = three_passes(y_ps[:, 0:D], ht_hi[h][:, f, :], ht_lo[h][:, f, :], w_hi[:, cols],
                                       w_lo[:, cols], h == 0 and f == 0, h == 1 and f == HH // P - 1)
                ins.then_inc(down_done, 1)

            def step(i, par, half):
                w = first_column(i)
                gate_up(i, par, 0, w)
                if not is_tile(i, T - 1):
                    turn_rows(i + 1, 1 - par, half + par)
                if not is_tile(i, 0):
                    w_before = first_column(i - 1)
                    turn_hidden(i - 1, 1)
                    down(i - 1, 0, w_before)
                gate_up(i, par, 1, w)
                turn_hidden(i, 0)
                if not is_tile(i, 0):
                    down(i - 1, 1, w_before)

            turn_rows(0, 0, 0)
            tile_loop(pe, step)
            w_last = first_column(T - 1)
            turn_hidden(T - 1, 1)
            down(T - 1, 0, w_last)
            down(T - 1, 1, w_last)

        @block.vector
        def _(dve):
            dve.wait_ge(x_loaded, 16)
            row_stats(dve, stats_step, 0, x_sb[:], stats[:], mean_var[:], half_v[:], seed_bits[:],
                      rstd[:]).then_inc(stats_step, 1)
            dve.wait_ge(newton_step, NEWTON_STEPS)
            for t in range(TILES):
                ins = dve.tensor_scalar(xn_sb[:, t, :], x_sb[:, t, :], mean_var[:, t, 0:1],
                                        rstd[:, t:t + 1], ALU.subtract, ALU.mult)
                if t % 2 == 1:
                    ins.then_inc(xn_ready, 1)

            def wide(ap):
                return ap.unsqueeze(2).to_broadcast([P, TILES, EXPERTS])

            def by_expert(ap):
                return ap.unsqueeze(1).to_broadcast([P, TILES, EXPERTS])

            iota_w = by_expert(iota[:])
            logits = y_ps[:, 0:TILES * EXPERTS].rearrange("p (t e) -> p t e", e=EXPERTS)
            dve.wait_ge(constants_in, CONSTANTS)
            dve.wait_ge(logits_done, GROUPS)
            dve.tensor_reduce(red[:], logits, AX.X, ALU.max).then_inc(gate_step, 1)
            dve.wait_ge(gate_step, 1)
            dve.tensor_tensor(ex[:], logits, wide(red[:]), ALU.subtract).then_inc(gate_step, 1)
            dve.wait_ge(xt_copied, GROUPS + 1)
            dve.tensor_reduce(red[:], ex[:], AX.X, ALU.add).then_inc(gate_step, 1)
            dve.wait_ge(gate_step, 3)
            dve.reciprocal(red[:], red[:]).then_inc(gate_step, 1)
            dve.wait_ge(gate_step, 4)
            dve.tensor_tensor(ex[:], ex[:], wide(red[:]), ALU.mult).then_inc(gate_step, 1)
            dve.wait_ge(gate_step, 5)
            dve.tensor_copy(left[:], ex[:]).then_inc(gate_step, 1)
            dve.wait_ge(gate_step, 6)
            at = 6
            for m in mask:
                dve.tensor_reduce(red[:], left[:], AX.X, ALU.max).then_inc(gate_step, 1)
                dve.wait_ge(gate_step, at + 1)
                dve.tensor_tensor(cand[:], left[:], wide(red[:]), ALU.is_lt).then_inc(gate_step, 1)
                dve.wait_ge(gate_step, at + 2)
                dve.scalar_tensor_tensor(cand[:], cand[:], float(EXPERTS), iota_w, ALU.mult, ALU.add)\
                   .then_inc(gate_step, 1)
                dve.wait_ge(gate_step, at + 3)
                dve.tensor_reduce(red[:], cand[:], AX.X, ALU.min).then_inc(gate_step, 1)
                dve.wait_ge(gate_step, at + 4)
                dve.tensor_tensor(m[:], iota_w, wide(red[:]), ALU.is_equal).then_inc(gate_step, 1)
                dve.wait_ge(gate_step, at + 5)
                dve.scalar_tensor_tensor(left[:], m[:], -2.0, left[:], ALU.mult, ALU.add)\
                   .then_inc(gate_step, 1)
                dve.wait_ge(gate_step, at + 6)
                at += 6
            dve.tensor_tensor(both[:], mask[0][:], mask[1][:], ALU.add).then_inc(chosen, 1)
            dve.wait_ge(chosen, 1)
            dve.tensor_reduce(own_count[:], both[:].rearrange("p t e -> p e t"), AX.X, ALU.add)\
               .then_inc(chosen, 1)
            dve.tensor_tensor(cand[:], ex[:], mask[0][:], ALU.mult)
            dve.tensor_tensor(left[:], ex[:], mask[1][:], ALU.mult).then_inc(gate_step, 1)
            dve.wait_ge(gate_step, at + 1)
            dve.tensor_reduce(gate[0][:], cand[:], AX.X, ALU.add)
            dve.tensor_reduce(gate[1][:], left[:], AX.X, ALU.add).then_inc(gate_step, 1)
            dve.wait_ge(gate_step, at + 2)
            dve.tensor_tensor(red[:], gate[0][:], gate[1][:], ALU.add).then_inc(gate_step, 1)
            dve.wait_ge(gate_step, at + 3)
            dve.tensor_scalar(red[:], red[:], DENOM_MIN, None, ALU.max).then_inc(gate_step, 1)
            dve.wait_ge(gate_step, at + 4)
            dve.reciprocal(red[:], red[:]).then_inc(gate_step, 1)
            dve.wait_ge(gate_step, at + 5)
            dve.tensor_tensor(gate[0][:], gate[0][:], red[:], ALU.mult)
            dve.tensor_tensor(gate[1][:], gate[1][:], red[:], ALU.mult).then_inc(gate_step, 1)
            at += 6
            dve.wait_ge(ranked, 1)
            dve.tensor_scalar(count_i[:], ht_ps[1][:, 0, 0:EXPERTS], float(P - 1), None, ALU.add)\
               .then_inc(gate_step, 1)
            dve.wait_ge(gate_step, at + 1)
            dve.tensor_scalar(count_i[:], count_i[:], P.bit_length() - 1, None, ALU.logical_shift_right)\
               .then_inc(gate_step, 1)
            dve.wait_ge(gate_step, at + 2)
            dve.tensor_copy(count_f[:], count_i[:]).then_inc(gate_step, 1)
            dve.wait_ge(gate_step, at + 3)
            dve.tensor_scalar(count_f[:], count_f[:], 1.0, None, ALU.max).then_inc(gate_step, 1)
            dve.wait_ge(gate_step, at + 4)
            dve.tensor_tensor(earlier[:], before[:], count_f[:].unsqueeze(1).to_broadcast([P, EXPERTS, EXPERTS]),
                              ALU.mult).then_inc(gate_step, 1)
            dve.wait_ge(gate_step, at + 5)
            dve.tensor_reduce(start[:], earlier[:], AX.X, ALU.add).then_inc(gate_step, 1)
            dve.wait_ge(gate_step, at + 6)
            dve.tensor_scalar(start_row[:], start[:], float(P), None, ALU.mult).then_inc(gate_step, 1)
            dve.wait_ge(gate_step, at + 7)
            rank = ht_ps[0][:].rearrange("p a b -> p (a b)")[:, 0:TILES * EXPERTS]
            dve.tensor_tensor(place[:], rank.rearrange("p (t e) -> p t e", e=EXPERTS), by_expert(start_row[:]),
                              ALU.add).then_inc(gate_step, 1)
            dve.wait_ge(gate_step, at + 8)
            dve.tensor_tensor(cand[:], place[:], mask[0][:], ALU.mult)
            dve.tensor_tensor(left[:], place[:], mask[1][:], ALU.mult).then_inc(gate_step, 1)
            dve.wait_ge(gate_step, at + 9)
            dve.tensor_reduce(red[:], cand[:], AX.X, ALU.add)
            dve.tensor_reduce(nwt[:], left[:], AX.X, ALU.add).then_inc(gate_step, 1)
            dve.wait_ge(gate_step, at + 10)
            dve.tensor_copy(row_no[0][:], red[:])
            dve.tensor_copy(row_no[1][:], nwt[:]).then_inc(tables_ready, 1)
            dve.tensor_tensor(begun[:], tile_no[:].unsqueeze(2).to_broadcast([1, T, EXPERTS]),
                              start[0:1].unsqueeze(1).to_broadcast([1, T, EXPERTS]), ALU.is_ge)\
               .then_inc(gate_step, 1)
            dve.wait_ge(gate_step, at + 11)
            dve.tensor_reduce(begun_count[:], begun[:], AX.X, ALU.add).then_inc(gate_step, 1)
            dve.wait_ge(gate_step, at + 12)
            dve.tensor_scalar(tile_pieces[:], begun_count[:], float(PIECES), -1.0, ALU.mult, ALU.add)
            dve.tensor_scalar(start_halves[:], start[0:1], 2.0, None, ALU.mult)
            dve.tensor_copy(begun_i[:], begun_count[:]).then_inc(gate_step, 1)
            dve.wait_ge(gate_step, at + 13)
            dve.tensor_scalar(begun_i[:], begun_i[:], 1, None, ALU.bitwise_and).then_inc(gate_step, 1)
            dve.wait_ge(gate_step, at + 14)
            dve.tensor_scalar(tile_slot[:], begun_i[:], -float(SLOT), float(SLOT), ALU.mult, ALU.add)\
               .then_inc(tables_ready, 1)
            for n in range(PIECES, 2 * PIECES):
                cols = slice(n * PIECE, (n + 1) * PIECE)
                dve.wait_ge(split_hi, n + 1)
                dve.tensor_tensor(w_lo[:, cols], stage[n % 2][:], w_hi[:, cols].bitcast(F32), ALU.subtract)\
                   .then_inc(split_done, 1)

            def split_rows(i, par):
                dve.wait_ge(rt_hi_done, i + 1)
                dve.tensor_tensor(rt_lo[par][:], rt_ps[:], rt_hi[par][:].bitcast(F32), ALU.subtract)\
                   .then_inc(rt_lo_done, 1)

            def split_hidden(i, h):
                dve.wait_ge(ht_hi_done, 2 * i + h + 1)
                dve.tensor_tensor(ht_lo[h][:], ht_ps[h][:], ht_hi[h][:].bitcast(F32), ALU.subtract)\
                   .then_inc(ht_lo_done, 1)

            def product(i, h):
                dve.wait_ge(silu_done, 2 * i + h + 1)
                if not is_tile(i, 0):
                    dve.wait_ge(h_turned, 2 * i + h - 1)
                dve.tensor_tensor(prod[h][:], silu[h][:], u_ps[h][:], ALU.mult).then_inc(prod_done, 1)

            def step(i, par, half):
                product(i, 0)
                if not is_tile(i, T - 1):
                    split_rows(i + 1, 1 - par)
                if not is_tile(i, 0):
                    split_hidden(i - 1, 1)
                product(i, 1)
                split_hidden(i, 0)

            split_rows(0, 0)
            tile_loop(dve, step)
            split_hidden(T - 1, 1)


SLOT_EXPERTS, SLOTS, SLOT_HID = 16, 64, 512
ALL_SLOTS = SLOT_EXPERTS * SLOTS
ST = ALL_SLOTS // P
SF = SLOT_HID // P
NS = BATCH * SLOTS
W = KD * SLOT_HID
RANGE = KD * NS
PAIR_COLS = 2 * RANGE


def dispatch_tokens(nc, tag, x_in, norm_g, norm_b, ident_in, slot_rows, arena, inv_rows, comb_dram,
                    load_first_weights):
    HALF = ALL_SLOTS // 2
    QUARTERS = 4
    EH = SLOT_EXPERTS // 4
    SLOTS_CREDIT = 8
    COMB_CREDIT = 4
    DISP_CREDIT = 2

    with ExitStack() as ctx:
        def sb(name, shape, dt=F32):
            return ctx.enter_context(nc.sbuf_tensor(f"{tag}_{name}", shape, dt))

        def pb(name, shape):
            return ctx.enter_context(nc.psum_tensor(f"{tag}_{name}", shape, F32))

        def sem(name):
            return ctx.enter_context(nc.semaphore(f"{tag}_{name}"))

        se_hi = sb("se_hi", [P, KD, ALL_SLOTS], F32R)
        se_lo = sb("se_lo", [P, KD, ALL_SLOTS], F32R)
        sw_hi = sb("sw_hi", [P, KD, ALL_SLOTS], F32R)
        sw_lo = sb("sw_lo", [P, KD, ALL_SLOTS], F32R)
        ident = sb("ident", [P, P])
        g_sb = sb("g", [P, D])
        b_sb = sb("b", [P, D])
        x_sb = [sb(f"x{i}", [P, NT, D]) for i in range(2)]
        xh_sb = [sb(f"xh{i}", [P, NT, D]) for i in range(2)]
        xt_hi = [sb(f"xt_hi{i}", [P, KD, SEQ], F32R) for i in range(2)]
        xt_lo = [sb(f"xt_lo{i}", [P, KD, SEQ], F32R) for i in range(2)]
        comb = [sb(f"comb{i}", [P, ALL_SLOTS]) for i in range(2)]
        comb_t = [sb(f"combt{i}", [P, ST, P]) for i in range(2)]
        disp_t = [sb(f"dispt{i}", [P, 2, SEQ]) for i in range(2)]
        disp = sb("disp", [P, NT, ALL_SLOTS])
        stats = sb("stats", [P, NT, 6])
        mean_var = sb("mv", [P, NT, 2])
        half_v = sb("halfv", [P, NT])
        seed_bits = sb("seedb", [P, NT], I32)
        rstd = sb("rstd", [P, NT])
        nwt = sb("nwt", [P, NT])
        three_halves = sb("three_halves", [P, NT])
        neg_max_c = [sb(f"nmaxc{i}", [P, 1]) for i in range(2)]
        sum_c = [sb(f"sumc{i}", [P, 1]) for i in range(2)]
        neg_max_d = [sb(f"nmaxd{i}", [P, 2]) for i in range(2)]
        sum_d = [sb(f"sumd{i}", [P, 2]) for i in range(2)]
        inv_d = [sb(f"invd{i}", [P, 2]) for i in range(2)]

        comb_ps = pb("combp", [P, 2, HALF])
        disp_ps = [pb(f"dispp{i}", [P, 2, SEQ]) for i in range(2)]
        turn_ps = [pb(f"turn{i}", [P, 4, P]) for i in range(2)]
        slot_ps = [pb(f"slot{i}", [P, HALF]) for i in range(2)]

        weights_in = sem("weights_in")
        x_loaded = [sem(f"x_loaded{i}") for i in range(2)]
        constant_set = sem("constant_set")
        stats_step = sem("stats_step")
        seed_ready = sem("seed_ready")
        newton_step = sem("newton_step")
        norm_step = sem("norm_step")
        gained = sem("gained")
        xh_ready = sem("xh_ready")
        se_turned = sem("se_turned")
        se_hi_done = sem("se_hi_done")
        se_ready = sem("se_ready")
        xt_turned = sem("xt_turned")
        xt_hi_done = sem("xt_hi_done")
        xt_ready = sem("xt_ready")
        comb_logits = sem("comb_logits")
        comb_max = sem("comb_max")
        comb_exp = sem("comb_exp")
        inv_step = sem("inv_step")
        comb_turned = sem("comb_turned")
        comb_taken = sem("comb_taken")
        comb_stored = [sem(f"comb_stored{i}") for i in range(2)]
        disp_logits = sem("disp_logits")
        disp_max = sem("disp_max")
        disp_exp = sem("disp_exp")
        inv_d_ready = sem("inv_d_ready")
        disp_ready = sem("disp_ready")
        disp_turned = sem("disp_turned")
        disp_taken = sem("disp_taken")
        slots_done = sem("slots_done")
        slots_taken = sem("slots_taken")

        x_dram = x_in.rearrange("b (t p) d -> b p t d", p=P)
        se_banks = [turn_ps[0][:].rearrange("p a b -> p (a b)"), turn_ps[1][:].rearrange("p a b -> p (a b)"),
                    slot_ps[0][:], slot_ps[1][:]]
        block = ctx.enter_context(nc.Block())

        def pairs_of(ap):
            return ap.rearrange("p (t r s) -> p t r s", t=4, r=2)

        def has_batch_before(pair, s):
            return not (isinstance(pair, int) and pair == 0 and s == 0)

        def batch_before(pair, s):
            return (pair, 0) if s else (pair - 1, 1)

        @block.sync
        def _(sp):
            sp.sem_inc(comb_stored[0], 16)
            sp.sem_inc(comb_stored[1], 16)

            def load(pair, s):
                if not isinstance(pair, int):
                    sp.wait_ge(xh_ready, 2 * pair + s - 1)
                sp.dma_start(x_sb[s][:], x_dram[2 * pair + s]).then_inc(x_loaded[s], 16)

            def store(pair, s):
                for t in range(NT):
                    n = (2 * pair + s) * NT + t
                    sp.wait_ge(comb_taken, nth(2 * n + 1))
                    sp.dma_start(comb_dram[2 * pair + s, :, :, t * P:(t + 1) * P].rearrange("i s n -> s i n"),
                                 comb_t[t][:]).then_inc(comb_stored[t], 16)

            load(0, 0)
            sp.dma_start(ident[:], ident_in).then_inc(weights_in, 16)
            sp.dma_start(g_sb[:], norm_g.partition_broadcast(P)).then_inc(weights_in, 16)
            sp.dma_start(b_sb[:], norm_b.partition_broadcast(P)).then_inc(weights_in, 16)
            load(0, 1)
            with sp.Fori(0, BATCH // 2 - 1) as pair:
                for s in range(2):
                    load(pair + 1, s)
                    store(pair, s)
            load_first_weights(sp)
            for s in range(2):
                store(BATCH // 2 - 1, s)
            for t in range(NT):
                sp.wait_ge(comb_stored[t], 16 * (BATCH + 1))

        @block.gpsimd
        def _(pool):
            pool.memset(three_halves[:], 1.5).then_inc(constant_set, 1)
            pool.wait_ge(constant_set, 1)

            def normalise(pair, s):
                b = 2 * pair + s
                for twice in range(2):
                    pool.wait_ge(seed_ready, 2 * b + twice + 1)
                    newton_rsqrt(pool, newton_step, NEWTON_STEPS * (2 * b + twice), rstd[:], half_v[:], nwt[:],
                                 three_halves[:])
                pool.wait_ge(weights_in, 48)
                pool.wait_ge(norm_step, 2 * b + 2)
                pool.tensor_tensor(xh_sb[s][:], xh_sb[s][:], g_sb[:].unsqueeze(1).to_broadcast([P, NT, D]),
                                   ALU.mult).then_inc(gained, 1)
                pool.wait_ge(gained, b + 1)
                pool.tensor_tensor(xh_sb[s][:], xh_sb[s][:], b_sb[:].unsqueeze(1).to_broadcast([P, NT, D]),
                                   ALU.add).then_inc(xh_ready, 1)

            with pool.Fori(0, BATCH // 2) as pair:
                normalise(pair, 0)
                normalise(pair, 1)

        @block.scalar
        def _(act):
            act.sem_inc(comb_exp, CREDIT)
            act.sem_inc(slots_taken, CREDIT)

            def slots_take(pair, s, n):
                k, half = n // 2, n % 2
                act.wait_ge(slots_done, SLOTS_CREDIT + 4 * (2 * pair + s) + n + 1)
                src = slot_ps[half][:].rearrange("p (i r s) -> p i r s", r=2, s=SLOTS)
                for r in range(2):
                    at = r * RANGE + k * NS
                    first = (2 * pair + (s if r == 0 else 1 - s)) * SLOTS
                    dst = arena[:, half * EH:(half + 1) * EH, at:at + NS]
                    ins = act.activation(dst[:, :, bass.ds(first, SLOTS)], src[:, :, r, :], ACT.Copy)
                ins.then_inc(slots_taken, 1)

            def step(pair, s, last):
                b = 2 * pair + s
                act.wait_ge(xt_turned, b + 1)
                act.activation(xt_hi[s][:], turn_ps[0][:].rearrange("p (k t) n -> p k (t n)", k=KD), ACT.Copy)\
                   .then_inc(xt_hi_done, 1)

                def comb_exp_of(t):
                    n = NT * b + t
                    act.wait_ge(comb_max, n + 1)
                    act.wait_ge(comb_turned, 2 * n - 2 + COMB_CREDIT)
                    act.activation(comb[t][:], comb_ps[:].rearrange("p a s -> p (a s)"), ACT.Exp,
                                   bias=neg_max_c[t][:], accum_out=sum_c[t][:]).then_inc(comb_exp, 1)

                def disp_exp_of(q):
                    n = QUARTERS * b + q
                    i = q % 2
                    act.wait_ge(disp_max, n + 1)
                    act.wait_ge(disp_turned, two_before(n))
                    for j in range(2):
                        ins = act.activation(disp_t[i][:, j, :], disp_ps[i][:, j, :], ACT.Exp,
                                             bias=neg_max_d[i][:, j:j + 1], accum_out=sum_d[i][:, j:j + 1])
                    ins.then_inc(disp_exp, 1)

                def disp_take(q):
                    n = QUARTERS * b + q
                    act.wait_ge(disp_turned, nth(n))
                    act.activation(disp[:, :, q * 2 * P:(q + 1) * 2 * P],
                                   turn_ps[1][:].rearrange("p (t j) s -> p t (j s)", t=NT), ACT.Copy)\
                       .then_inc(disp_taken, 1)

                comb_exp_of(0)
                disp_exp_of(0)
                if has_batch_before(pair, s):
                    slots_take(*batch_before(pair, s), 0)
                    slots_take(*batch_before(pair, s), 1)
                comb_exp_of(1)
                disp_exp_of(1)
                if has_batch_before(pair, s):
                    slots_take(*batch_before(pair, s), 2)
                    slots_take(*batch_before(pair, s), 3)
                disp_take(0)
                disp_exp_of(2)
                disp_take(1)
                disp_exp_of(3)
                disp_take(2)
                disp_take(3)

            for n in range(4):
                act.wait_ge(se_turned, n + 1)
                k, cols = n // 2, slice((n % 2) * 4 * P, (n % 2 + 1) * 4 * P)
                act.activation(se_hi[:, k, cols], se_banks[n], ACT.Copy)
                for r in range(2):
                    ins = act.activation(pairs_of(sw_hi[:, k, cols])[:, :, r, :],
                                         pairs_of(se_banks[n])[:, :, 1 - r, :], ACT.Copy)
                ins.then_inc(se_hi_done, 1)
            pair_loop(act, step, peel_first=True)
            for n in range(4):
                slots_take(BATCH // 2 - 1, 1, n)

        @block.tensor
        def _(pe):
            pe.sem_inc(slots_done, SLOTS_CREDIT)
            pe.sem_inc(comb_turned, COMB_CREDIT)
            pe.sem_inc(disp_turned, CREDIT)
            pe.wait_ge(weights_in, 48)

            def three_passes(out, a_hi, a_lo, b_hi, b_lo, start, stop):
                pe.matmul(out, a_hi, b_hi, start=start, stop=False)
                pe.matmul(out, a_lo, b_hi, start=False, stop=False)
                return pe.matmul(out, a_hi, b_lo, start=False, stop=stop)

            def slots(pair, s, part):
                b = 2 * pair + s
                k, half = part // 2, part % 2
                pe.wait_ge(slots_taken, two_before(4 * b + part))
                if part == 0:
                    pe.wait_ge(disp_taken, DISP_CREDIT + QUARTERS * (b + 1))
                for t in range(NT):
                    ins = pe.matmul(slot_ps[half][:], xh_sb[s][:, t, k * P:(k + 1) * P],
                                    disp[:, t, half * HALF:(half + 1) * HALF],
                                    start=(t == 0), stop=(t == NT - 1))
                ins.then_inc(slots_done, 1)

            def step(pair, s, last):
                b = 2 * pair + s
                sc_hi, sc_lo = (sw_hi, sw_lo) if s else (se_hi, se_lo)
                pe.wait_ge(comb_taken, nth(4 * b - 1))
                pe.wait_ge(xh_ready, b + 1)
                for k in range(KD):
                    for t in range(NT):
                        ins = pe.transpose(turn_ps[0][:, 2 * k + t, :], xh_sb[s][:, t, k * P:(k + 1) * P],
                                           ident[:])
                ins.then_inc(xt_turned, 1)
                pe.wait_ge(xt_ready, b + 1)

                def comb_scores(t):
                    n = NT * b + t
                    pe.wait_ge(comb_exp, n + CREDIT)
                    for half in range(2):
                        for k in range(KD):
                            rows, cols = slice(t * P, (t + 1) * P), slice(half * HALF, (half + 1) * HALF)
                            ins = three_passes(comb_ps[:, half, :], xt_hi[s][:, k, rows], xt_lo[s][:, k, rows],
                                               sc_hi[:, k, cols], sc_lo[:, k, cols], k == 0, k == KD - 1)
                    ins.then_inc(comb_logits, 1)

                def comb_turn(t):
                    n = NT * b + t
                    pe.wait_ge(comb_exp, nth(n))
                    for half in range(2):
                        pe.wait_ge(comb_taken, nth(2 * n + half - 1))
                        for i in range(4):
                            c = (4 * half + i) * P
                            ins = pe.transpose(turn_ps[0][:, i, :], comb[t][:, c:c + P], ident[:])
                        ins.then_inc(comb_turned, 1)

                def disp_scores(q):
                    n = QUARTERS * b + q
                    pe.wait_ge(disp_exp, DISP_CREDIT + n - 1)
                    for j in range(2):
                        for k in range(KD):
                            cols = slice((2 * q + j) * P, (2 * q + j + 1) * P)
                            ins = three_passes(disp_ps[q % 2][:, j, :], se_hi[:, k, cols], se_lo[:, k, cols],
                                               xt_hi[s][:, k, :], xt_lo[s][:, k, :], k == 0, k == KD - 1)
                    ins.then_inc(disp_logits, 1)

                def disp_turn(q):
                    n = QUARTERS * b + q
                    pe.wait_ge(disp_ready, n + 1)
                    pe.wait_ge(disp_taken, DISP_CREDIT + n - 1 + 1)
                    for t in range(NT):
                        for j in range(2):
                            ins = pe.transpose(turn_ps[1][:, 2 * t + j, :], disp_t[q % 2][:, j, t * P:(t + 1) * P],
                                               ident[:])
                    ins.then_inc(disp_turned, 1)

                comb_scores(0)
                disp_scores(0)
                if has_batch_before(pair, s):
                    slots(*batch_before(pair, s), 0)
                    slots(*batch_before(pair, s), 1)
                comb_scores(1)
                disp_scores(1)
                if has_batch_before(pair, s):
                    slots(*batch_before(pair, s), 2)
                    slots(*batch_before(pair, s), 3)
                comb_turn(0)
                disp_turn(0)
                disp_scores(2)
                comb_turn(1)
                disp_turn(1)
                disp_scores(3)
                disp_turn(2)
                disp_turn(3)

            for n in range(4):
                for t in range(4):
                    k, tile = n // 2, 4 * (n % 2) + t
                    ins = pe.transpose(se_banks[n][:, t * P:(t + 1) * P], slot_rows[:, tile, k * P:(k + 1) * P],
                                       ident[:])
                ins.then_inc(se_turned, 1)
            pe.wait_ge(se_ready, 4)
            pair_loop(pe, step, peel_first=True)
            for part in range(4):
                slots(BATCH // 2 - 1, 1, part)

        @block.vector
        def _(dve):
            dve.sem_inc(disp_exp, DISP_CREDIT)
            dve.sem_inc(disp_taken, DISP_CREDIT)
            dve.sem_inc(comb_taken, CREDIT)

            def statistics(pair, s, twice):
                n, o = 2 * pair + s + 1, 1 - s
                if twice:
                    dve.wait_ge(norm_step, 2 * n + 1)
                else:
                    dve.wait_ge(x_loaded[o], 16 * (pair + s + 1))
                row_stats(dve, stats_step, STATS_STEPS * (2 * n + twice), x_sb[o][:],
                          stats[:], mean_var[:], half_v[:], seed_bits[:], rstd[:]).then_inc(seed_ready, 1)

            def normalise(pair, s, twice):
                n, o = 2 * pair + s + 1, 1 - s
                if twice:
                    dve.wait_ge(slots_done, SLOTS_CREDIT + 4 * (n - 1))
                dve.wait_ge(newton_step, NEWTON_STEPS * (2 * n + twice + 1))
                dst = xh_sb[o] if twice else x_sb[o]
                for t in range(NT):
                    ins = dve.tensor_scalar(dst[:, t, :], x_sb[o][:, t, :], mean_var[:, t, 0:1],
                                            rstd[:, t:t + 1], ALU.subtract, ALU.mult)
                ins.then_inc(norm_step, 1)

            def step(pair, s, last):
                b = 2 * pair + s

                dve.wait_ge(xt_hi_done, b + 1)
                dve.tensor_tensor(xt_lo[s][:], turn_ps[0][:].rearrange("p (k t) n -> p k (t n)", k=KD),
                                  xt_hi[s][:].bitcast(F32), ALU.subtract).then_inc(xt_ready, 1)

                def comb_max_of(t):
                    n = NT * b + t
                    dve.wait_ge(comb_logits, n + 1)
                    dve.tensor_reduce(neg_max_c[t][:], comb_ps[:].rearrange("p a s -> p (a s)"), AX.X, ALU.max,
                                      negate=True).then_inc(comb_max, 1)

                def comb_take(t):
                    n = NT * b + t
                    dve.wait_ge(comb_exp, nth(n))
                    dve.reciprocal(inv_rows[:, bass.ds(n, 1)], sum_c[t][:])
                    dve.wait_ge(comb_stored[t], 16 * (b + 1))
                    for half in range(2):
                        dve.wait_ge(comb_turned, COMB_CREDIT + 2 * n + half + 1)
                        dve.tensor_copy(comb_t[t][:, 4 * half:4 * half + 4, :], turn_ps[0][:])\
                           .then_inc(comb_taken, 1)

                def disp_max_of(q):
                    n = QUARTERS * b + q
                    dve.wait_ge(disp_logits, n + 1)
                    dve.tensor_reduce(neg_max_d[q % 2][:], disp_ps[q % 2][:], AX.X, ALU.max, negate=True)\
                       .then_inc(disp_max, 1)

                def disp_divide(q):
                    n = QUARTERS * b + q
                    i = q % 2
                    dve.wait_ge(disp_exp, DISP_CREDIT + n + 1)
                    dve.reciprocal(inv_d[i][:], sum_d[i][:]).then_inc(inv_d_ready, 1)
                    dve.wait_ge(inv_d_ready, n + 1)
                    for j in range(2):
                        ins = dve.tensor_scalar(disp_t[i][:, j, :], disp_t[i][:, j, :], inv_d[i][:, j:j + 1],
                                                None, ALU.mult)
                    ins.then_inc(disp_ready, 1)

                comb_max_of(0)
                disp_max_of(0)
                disp_divide(0)
                if not last:
                    statistics(pair, s, 0)
                comb_max_of(1)
                disp_max_of(1)
                disp_divide(1)
                if not last:
                    normalise(pair, s, 0)
                    statistics(pair, s, 1)
                comb_take(0)
                disp_max_of(2)
                comb_take(1)
                if not last:
                    normalise(pair, s, 1)
                disp_divide(2)
                disp_max_of(3)
                disp_divide(3)

            for twice in range(2):
                statistics(-1, 1, twice)
                normalise(-1, 1, twice)
            for n in range(4):
                dve.wait_ge(se_hi_done, n + 1)
                k, cols = n // 2, slice((n % 2) * 4 * P, (n % 2 + 1) * 4 * P)
                dve.tensor_tensor(se_lo[:, k, cols], se_banks[n], se_hi[:, k, cols].bitcast(F32), ALU.subtract)
                for r in range(2):
                    ins = dve.tensor_tensor(pairs_of(sw_lo[:, k, cols])[:, :, r, :],
                                            pairs_of(se_banks[n])[:, :, 1 - r, :],
                                            pairs_of(sw_hi[:, k, cols])[:, :, r, :].bitcast(F32), ALU.subtract)
                ins.then_inc(se_ready, 1)
            pair_loop(dve, step)


def slot_experts(nc, tag, bg, bu, arena, stage, bd_sb, staged, bd_in, load_weights, load_bias,
                 load_first_rows):
    PART = 3 * W // SF
    GU_PARTS = -(-2 * W // PART)
    E = SLOT_EXPERTS
    assert W == SF * D and NS == 4 * P

    with ExitStack() as ctx:
        def sb(name, shape, dt=F32):
            return ctx.enter_context(nc.sbuf_tensor(f"{tag}_{name}", shape, dt))

        def pb(name, shape):
            return ctx.enter_context(nc.psum_tensor(f"{tag}_{name}", shape, F32))

        def sem(name):
            return ctx.enter_context(nc.semaphore(f"{tag}_{name}"))

        w_hi = [sb(f"w_hi{i}", [P, 3 * W], F32R) for i in range(2)]
        w_lo = [sb(f"w_lo{i}", [P, 3 * W], F32R) for i in range(2)]
        bg_sb = sb("bg", [P, E, SF])
        bu_sb = sb("bu", [P, E, SF])
        xs_hi = [sb(f"xs_hi{i}", [P, RANGE], F32R) for i in range(2)]
        xs_lo = [sb(f"xs_lo{i}", [P, RANGE], F32R) for i in range(2)]
        gelu = [sb(f"gelu{i}", [P, NS]) for i in range(2)]
        prod = [sb(f"prod{i}", [P, NS]) for i in range(2)]
        h_hi = [sb(f"h_hi{i}", [P, NS], F32R) for i in range(2)]
        h_lo = [sb(f"h_lo{i}", [P, NS], F32R) for i in range(2)]
        tick = sb("tick", [P, 1])
        g_ps = [pb(f"g{i}", [P, NS]) for i in range(2)]
        u_ps = [pb(f"u{i}", [P, NS]) for i in range(2)]
        y_ps = [pb(f"y{i}", [P, 4, D]) for i in range(2)]

        biases_in = sem("biases_in")
        w_hi_done = sem("w_hi_done")
        w_lo_done = sem("w_lo_done")
        x_hi_done = sem("x_hi_done")
        x_lo_done = sem("x_lo_done")
        gu_done = sem("gu_done")
        gelu_done = sem("gelu_done")
        prod_done = sem("prod_done")
        hi_done = sem("hi_done")
        lo_done = sem("lo_done")
        down_done = sem("down_done")
        y_taken = sem("y_taken")

        def slots_of(pair, s):
            return arena[:, bass.ds(pair, 1), s * RANGE:(s + 1) * RANGE].rearrange("p i c -> p (i c)")

        def expert_loop(eng, step, peel_first=False):
            if peel_first:
                step(0, 0, False)
                step(0, 1, False)
            with eng.Fori(1 if peel_first else 0, E // 2 - 1) as pair:
                step(pair, 0, False)
                step(pair, 1, False)
            step(E // 2 - 1, 0, False)
            step(E // 2 - 1, 1, True)

        block = ctx.enter_context(nc.Block())

        @block.sync
        def _(sp):
            sp.sem_inc(w_lo_done, 2 * SF)
            with sp.Fori(1, E // 2) as pair:
                for s in range(2):
                    e = 2 * pair + s
                    sp.wait_ge(w_lo_done, SF * e + SF)
                    load_weights(sp, e, s)
                    sp.wait_ge(y_taken, two_before(e))
                    load_bias(sp, e, s)
            load_first_rows(sp)

        @block.gpsimd
        def _(pool):
            def split(pair, s):
                for f in range(SF):
                    part = slice(f * PART, (f + 1) * PART)
                    pool.wait_ge(w_hi_done, SF * (2 * pair + s) + f + 1)
                    pool.tensor_tensor(w_lo[s][:, part], stage[s][:, part], w_hi[s][:, part].bitcast(F32),
                                       ALU.subtract).then_inc(w_lo_done, 1)

            with pool.Fori(0, E // 2) as pair:
                split(pair, 0)
                split(pair, 1)

        @block.scalar
        def _(act):
            act.dma_start(bg_sb[:], bg).then_inc(biases_in, 16)
            act.dma_start(bu_sb[:], bu).then_inc(biases_in, 16)

            def split_weights(pair, s, f):
                o = 1 - s
                part = slice(f * PART, (f + 1) * PART)
                if f == 0:
                    act.wait_ge(staged[o], 48 * (pair + s + 1))
                    if not (isinstance(pair, int) and pair < 0):
                        act.wait_ge(down_done, CREDIT + SF * (2 * pair + s))
                act.activation(w_hi[o][:, part], stage[o][:, part], ACT.Copy).then_inc(w_hi_done, 1)

            def split_slots(pair, s):
                act.activation(xs_hi[1 - s][:], slots_of(pair + s, 1 - s), ACT.Copy).then_inc(x_hi_done, 1)

            def expert(pair, s, last):
                for f in range(SF):
                    n = (2 * pair + s) * SF + f
                    i = f % 2
                    act.wait_ge(prod_done, two_before(n))
                    act.wait_ge(gu_done, n + 1)
                    act.activation(gelu[i][:], g_ps[i][:], ACT.Gelu,
                                   bias=bg_sb[:, bass.ds(2 * pair + s, 1), f]).then_inc(gelu_done, 1)
                    if not last:
                        split_weights(pair, s, f)
                    act.wait_ge(down_done, two_before(n))
                    act.wait_ge(prod_done, nth(n))
                    act.activation(h_hi[i][:], prod[i][:], ACT.Copy).then_inc(hi_done, 1)
                    if f == 1 and not last:
                        split_slots(pair, s)

            for f in range(SF):
                split_weights(-1, 1, f)
            split_slots(-1, 1)
            act.wait_ge(biases_in, 32)
            expert_loop(act, expert)

        @block.tensor
        def _(pe):
            pe.sem_inc(down_done, CREDIT)

            def three_passes(out, a_hi, a_lo, b_hi, b_lo, start, stop):
                pe.matmul(out, a_hi, b_hi, start=start, stop=False, skip_group_check=True)
                pe.matmul(out, a_lo, b_hi, start=False, stop=False, skip_group_check=True)
                return pe.matmul(out, a_hi, b_lo, start=False, stop=stop, skip_group_check=True)

            def gate_up(pair, s, f):
                e = 2 * pair + s
                n = e * SF + f
                if f == 0:
                    pe.wait_ge(w_lo_done, 2 * SF + SF * e + GU_PARTS)
                    pe.wait_ge(x_lo_done, e + 1)
                pe.wait_ge(prod_done, two_before(n))
                for ps, first in ((g_ps[f % 2], 0), (u_ps[f % 2], W)):
                    for k in range(KD):
                        a = slice(first + k * SLOT_HID + f * P, first + k * SLOT_HID + (f + 1) * P)
                        x = slice(k * NS, (k + 1) * NS)
                        ins = three_passes(ps[:], w_hi[s][:, a], w_lo[s][:, a], xs_hi[s][:, x], xs_lo[s][:, x],
                                           k == 0, k == KD - 1)
                ins.then_inc(gu_done, 1)

            def down(pair, s, f):
                e = 2 * pair + s
                n = e * SF + f
                i = f % 2
                if f == 0:
                    pe.wait_ge(w_lo_done, 2 * SF + SF * e + SF)
                    pe.wait_ge(y_taken, two_before(e))
                pe.wait_ge(lo_done, n + 1)
                for t in range(4):
                    a, c = slice(t * P, (t + 1) * P), slice(2 * W + f * D, 2 * W + (f + 1) * D)
                    ins = three_passes(y_ps[s][:, t, :], h_hi[i][:, a], h_lo[i][:, a], w_hi[s][:, c],
                                       w_lo[s][:, c], f == 0 and t % 2 == 0, f == SF - 1)
                ins.then_inc(down_done, 1)

            def expert(pair, s, last):
                for f in range(1, SF):
                    gate_up(pair, s, f)
                    down(pair, s, f - 1)
                if not last:
                    gate_up(pair + s, 1 - s, 0)
                down(pair, s, SF - 1)

            gate_up(0, 0, 0)
            expert_loop(pe, expert)

        @block.vector
        def _(dve):
            dve.sem_inc(prod_done, CREDIT)
            dve.sem_inc(y_taken, CREDIT)

            def split_slots(pair, s):
                o = 1 - s
                dve.wait_ge(x_hi_done, 2 * pair + s + 2)
                dve.tensor_tensor(xs_lo[o][:], slots_of(pair + s, o), xs_hi[o][:].bitcast(F32), ALU.subtract)\
                   .then_inc(x_lo_done, 1)

            def take(pair, s):
                dve.wait_ge(bd_in[s], 16 * (pair + 1))
                dve.wait_ge(down_done, nth(SF * (2 * pair + s) + SF - 1))
                for half in range(2):
                    rows = slice(half * SLOTS, (half + 1) * SLOTS)
                    dst = arena[rows, bass.ds(pair, 1), :].rearrange("p i (j r d) -> p (i j) r d", r=2, d=D)
                    ins = dve.tensor_tensor(dst[:, :, half ^ s, :], y_ps[s][rows, :, :],
                                            bd_sb[s][rows, :].unsqueeze(1).to_broadcast([SLOTS, 4, D]), ALU.add)
                ins.then_inc(y_taken, 1)

            def expert(pair, s, last):
                e = 2 * pair + s
                for f in range(SF):
                    n = e * SF + f
                    i = f % 2
                    dve.wait_ge(gelu_done, n + 1)
                    dve.scalar_tensor_tensor(prod[i][:], u_ps[i][:], bu_sb[:, bass.ds(e, 1), f], gelu[i][:],
                                             ALU.add, ALU.mult).then_inc(prod_done, 1)
                    dve.wait_ge(hi_done, n + 1)
                    dve.tensor_tensor(h_lo[i][:], prod[i][:], h_hi[i][:].bitcast(F32), ALU.subtract)\
                       .then_inc(lo_done, 1)
                    if f == 0 and not (isinstance(e, int) and e == 0):
                        take(*((pair, 0) if s else (pair - 1, 1)))
                    if f == 2 and not last:
                        split_slots(pair, s)

            dve.wait_ge(biases_in, 32)
            split_slots(-1, 1)
            expert_loop(dve, expert, peel_first=True)
            take(E // 2 - 1, 1)


def combine_slots(nc, tag, x_dram, comb_dram, inv_rows, arena, x_out, first_x, first_ct, loaded):
    with ExitStack() as ctx:
        def sb(name, shape, dt=F32):
            return ctx.enter_context(nc.sbuf_tensor(f"{tag}_{name}", shape, dt))

        def sem(name):
            return ctx.enter_context(nc.semaphore(f"{tag}_{name}"))

        x_sb = [first_x, sb("x1", [P, NT, D])]
        xo_sb = [sb(f"xo{i}", [P, NT, D]) for i in range(2)]
        ct_sb = [first_ct, sb("ct1", [P, ST, SEQ])]
        out_ps = [ctx.enter_context(nc.psum_tensor(f"{tag}_out{i}", [P, NT, D], F32)) for i in range(2)]

        out_done = sem("out_done")
        xo_ready = sem("xo_ready")
        stored = [sem(f"stored{i}") for i in range(2)]

        xo_dram = x_out.rearrange("b (t p) d -> b p t d", p=P)
        block = ctx.enter_context(nc.Block())

        def pairs(eng, step):
            with eng.Fori(0, BATCH // 2) as pair:
                step(pair, 0)
                step(pair, 1)

        @block.sync
        def _(sp):
            sp.sem_inc(stored[0], 16)
            sp.sem_inc(stored[1], 16)

            def load(pair, s):
                b = 2 * pair + s
                sp.wait_ge(out_done, two_before(b))
                sp.dma_start(ct_sb[s][:], comb_dram[b].rearrange("i s n -> s i n")).then_inc(loaded[s], 16)
                sp.wait_ge(xo_ready, two_before(b))
                sp.dma_start(x_sb[s][:], x_dram[b]).then_inc(loaded[s], 16)

            def store(pair, s):
                sp.wait_ge(xo_ready, nth(2 * pair + s))
                sp.dma_start(xo_dram[2 * pair + s], xo_sb[s][:]).then_inc(stored[s], 16)

            load(0, 1)
            with sp.Fori(0, BATCH // 2 - 1) as pair:
                for s in range(2):
                    store(pair, s)
                    load(pair + 1, s)
            for s in range(2):
                store(BATCH // 2 - 1, s)
            for s in range(2):
                sp.wait_ge(stored[s], 16 * (BATCH // 2 + 1))

        @block.tensor
        def _(pe):
            pe.sem_inc(out_done, CREDIT)

            def step(pair, s):
                b = 2 * pair + s
                pe.wait_ge(loaded[s], 32 * (pair + 1))
                pe.wait_ge(xo_ready, two_before(b))
                for t in range(NT):
                    for i in range(ST):
                        ins = pe.matmul(out_ps[s][:, t, :], ct_sb[s][:, i, t * P:(t + 1) * P],
                                        arena[:, i, bass.ts(b, D)], start=(i == 0), stop=(i == ST - 1))
                ins.then_inc(out_done, 1)

            pairs(pe, step)

        @block.vector
        def _(dve):
            dve.sem_inc(xo_ready, CREDIT)

            def step(pair, s):
                b = 2 * pair + s
                dve.wait_ge(out_done, nth(b))
                dve.wait_ge(stored[s], 16 * (pair + 1))
                for t in range(NT):
                    ins = dve.scalar_tensor_tensor(xo_sb[s][:, t, :], out_ps[s][:, t, :],
                                                   inv_rows[:, bass.ds(NT * b + t, 1)], x_sb[s][:, t, :],
                                                   ALU.mult, ALU.add)
                ins.then_inc(xo_ready, 1)

            pairs(dve, step)


def slot_mixture(nc, tag, x_in, norm_g, norm_b, slot_rows, wg, bg, wu, bu, wd, bd, x_out, ident_in):
    comb_dram = nc.dram_tensor(f"{tag}_comb", (BATCH, ST, P, SEQ), F32, kind="Internal").ap()
    with ExitStack() as ctx:
        def sb(name, shape):
            return ctx.enter_context(nc.sbuf_tensor(f"{tag}_{name}", shape, F32))

        arena = sb("arena", [P, SLOT_EXPERTS // 2, PAIR_COLS])
        inv_rows = sb("inv_rows", [P, TILES])
        stage = [sb(f"stage{i}", [P, 3 * W]) for i in range(2)]
        bd_sb = [sb(f"bd{i}", [P, D]) for i in range(2)]
        staged = [ctx.enter_context(nc.semaphore(f"{tag}_staged{i}")) for i in range(2)]
        bd_in = [ctx.enter_context(nc.semaphore(f"{tag}_bd_in{i}")) for i in range(2)]

        def load_weights(sp, e, s):
            for n, (w, parts) in enumerate(((wg, KD), (wu, KD), (wd, SF))):
                dst = stage[s][:, n * W:(n + 1) * W].rearrange("p (k n) -> p k n", k=parts)
                sp.dma_start(dst, w[e].rearrange("(k p) n -> p k n", p=P)).then_inc(staged[s], 16)

        def load_bias(sp, e, s):
            sp.dma_start(bd_sb[s][:], bd[e].partition_broadcast(P)).then_inc(bd_in[s], 16)

        def load_first_weights(sp):
            for e in range(2):
                load_weights(sp, e, e)
                load_bias(sp, e, e)

        dispatch_tokens(nc, f"{tag}d", x_in, norm_g, norm_b, ident_in, slot_rows, arena, inv_rows, comb_dram,
                        load_first_weights)
        first_x = sb("first_x", [P, NT, D])
        first_ct = sb("first_ct", [P, ST, SEQ])
        rows_loaded = [ctx.enter_context(nc.semaphore(f"{tag}_rows_loaded{i}")) for i in range(2)]
        x_dram = x_in.rearrange("b (t p) d -> b p t d", p=P)

        def load_first_rows(sp):
            sp.dma_start(first_ct[:], comb_dram[0].rearrange("i s n -> s i n")).then_inc(rows_loaded[0], 16)
            sp.dma_start(first_x[:], x_dram[0]).then_inc(rows_loaded[0], 16)

        slot_experts(nc, f"{tag}e", bg, bu, arena, stage, bd_sb, staged, bd_in, load_weights, load_bias,
                     load_first_rows)
        combine_slots(nc, f"{tag}c", x_dram, comb_dram, inv_rows, arena, x_out, first_x, first_ct, rows_loaded)


def two_layer_program(nc, a, out):
    hidden = [nc.dram_tensor(f"hidden{i}", (BATCH, SEQ, D), F32, kind="Internal").ap() for i in range(2)]
    cross_attention(nc, "l0", a["x"], a["ctx_t"], a["L0_xattn_Wq"], a["L0_xattn_Wk"], a["L0_xattn_Wv"],
                    a["L0_xattn_Wo"], a["L0_xattn_bo"], hidden[0], a["identity"], heads=8, head_dim=64)
    with ExitStack() as ctx:
        def sb(name, shape, dt=F32):
            return ctx.enter_context(nc.sbuf_tensor(name, shape, dt))

        slot_rows = sb("slot_rows", [P, ST, D])
        with ExitStack() as inner:
            def sb_inner(name, shape, dt=F32):
                return inner.enter_context(nc.sbuf_tensor(name, shape, dt))

            routed = (sb_inner("routed_x", [P, TILES, D]),
                      nc.dram_tensor("routed_y", (ROW_TILES * P, D), F32, kind="Internal").ap(),
                      [sb_inner(f"routed_row{i}", [P, TILES], U32) for i in range(CHOICES)],
                      [sb_inner(f"routed_gate{i}", [P, TILES]) for i in range(CHOICES)])
            routed_experts(nc, "l0f", hidden[0], a["L0_ffn_w_gate"], a["L0_ffn_w_gate_up"], a["L0_ffn_w_down"],
                           a["identity"], a["expert_numbers"], a["row_tile_numbers"], a["rows_below"],
                           a["experts_before"], routed)
            cross_attention(nc, "l1", None, a["ctx_t"], a["l1_wq"], a["l1_wk"], a["l1_wv"],
                            a["l1_wo"], a["L1_xattn_proj_b"], hidden[1], a["identity"], heads=16, head_dim=16,
                            q_bias=a["l1_bq"], k_bias=a["l1_bk"], v_bias=a["l1_bv"],
                            slots=(slot_rows, a["L1_ffn_slot_embeds"], a["L1_ffn_slot_g"], a["L1_ffn_slot_b"],
                                   a["L1_ffn_scale"]), routed=routed)
        slot_mixture(nc, "l1f", hidden[1], a["L1_ffn_norm_g"], a["L1_ffn_norm_b"], slot_rows,
                     a["L1_ffn_Wg"], a["l1_bg"], a["L1_ffn_Wu"], a["l1_bu"], a["L1_ffn_Wd"], a["L1_ffn_bd"],
                     out, a["identity"])


def kernel(**inputs):
    import numpy as _np
    import concourse.bacc as _bacc
    from concourse import mybir as _mybir
    from concourse.bass_utils import run_bass_kernel_spmd as _run

    heads, head_dim, row_group = 16, 16, 32

    def spread_heads(w):
        out = _np.zeros((*w.shape[:-1], heads, row_group), w.dtype)
        out[..., :head_dim] = w.reshape(*w.shape[:-1], heads, head_dim)
        return out.reshape(*w.shape[:-1], heads * row_group)

    def column_tiles(b):
        return b.reshape(-1, P).T

    i = {k: _np.asarray(v) for k, v in inputs.items()}
    inner = heads * head_dim
    kv_w, kv_b = i["L1_xattn_kv_w"], i["L1_xattn_kv_b"]
    laid = {k: v for k, v in i.items() if k.startswith("L0_")}
    for name in ("L1_xattn_proj_b", "L1_ffn_norm_g", "L1_ffn_norm_b", "L1_ffn_slot_g",
                 "L1_ffn_slot_b", "L1_ffn_scale", "L1_ffn_slot_embeds", "L1_ffn_Wg", "L1_ffn_Wu", "L1_ffn_Wd",
                 "L1_ffn_bd"):
        laid[name] = i[name]
    laid |= {
        "x": i["x"],
        "ctx_t": i["ctx_768"].transpose(0, 2, 1),
        "l1_wq": spread_heads(i["L1_xattn_q_w"]),
        "l1_wk": spread_heads(kv_w[:, :inner]),
        "l1_wv": kv_w[:, inner:],
        "l1_wo": spread_heads(i["L1_xattn_proj_w"].T).T,
        "l1_bq": column_tiles(spread_heads(i["L1_xattn_q_b"])),
        "l1_bk": column_tiles(spread_heads(kv_b[:inner])),
        "l1_bv": kv_b[inner:],
        "l1_bg": i["L1_ffn_bg"].reshape(SLOT_EXPERTS, SLOT_HID // P, P).transpose(2, 0, 1),
        "l1_bu": i["L1_ffn_bu"].reshape(SLOT_EXPERTS, SLOT_HID // P, P).transpose(2, 0, 1),
        "identity": _np.eye(P, dtype=_np.float32),
        "expert_numbers": _np.arange(EXPERTS, dtype=_np.float32),
        "row_tile_numbers": _np.arange(ROW_TILES, dtype=_np.float32),
        "rows_below": _np.triu(_np.ones((P, P), _np.float32), 1),
        "experts_before": _np.tril(_np.ones((EXPERTS, EXPERTS), _np.float32), -1).reshape(-1),
    }

    nc = _bacc.Bacc("TRN2", target_bir_lowering=False, num_devices=1)
    arrays, args = {}, {}
    for name, value in laid.items():
        arrays[f"in_{name}"] = _np.ascontiguousarray(value)
        args[name] = nc.dram_tensor(f"in_{name}", value.shape, _mybir.dt.from_np(value.dtype),
                                    kind="ExternalInput").ap()
    out = nc.dram_tensor("out", (BATCH, SEQ, D), _mybir.dt.float32, kind="ExternalOutput").ap()
    two_layer_program(nc, args, out)
    return _run(nc, [arrays], core_ids=[0]).results[0]["out"]
```
